# Optimizing a Trainium2 kernel written in Bass

```python
import numpy as np
import jax
import jax.numpy as jnp

def _softmax(x, axis=-1):
    return jax.nn.softmax(x, axis=axis)

def _gelu(x):
    return jax.nn.gelu(x, approximate=True)

def _silu(x):
    return jax.nn.silu(x)

def _sigmoid(x):
    return jax.nn.sigmoid(x)

def _layernorm(x, axis=-1, eps=1e-05):
    m = jnp.mean(x, axis=axis, keepdims=True)
    v = jnp.var(x, axis=axis, keepdims=True)
    return (x - m) / jnp.sqrt(v + eps)

def _scatter_add(tgt, idx, src, axis=0):
    return tgt.at[idx].add(src)

def _segment_sum(src, seg, n):
    return jax.ops.segment_sum(src, seg, n)
kernel_name = 'mk_conv_seq_d2_conv_nhwc512_r4_9a4b52'

def setup_inputs(seed: int=0):
    np.random.seed(seed)
    _w = jnp.asarray

    def _rec_inputs():
        import jax
        import jax.numpy as jnp
        _gk = jax.random.key(seed)
        x = -0.0003957 + 1 * jax.random.normal(jax.random.fold_in(_gk, 1), (8, 56, 56, 128), jnp.float32)
        return x
    x = _rec_inputs()

    def _L0_conv_setup():
        import jax, jax.numpy as jnp
        import numpy as np
        B, H, W, C = (8, 56, 56, 128)
        GROUP = 8
        S = C // GROUP
        DIM = H * S
        COF = int(0.25 * DIM + 1)

        def _spectral_branch(z, param, mlp_w):
            freq = jnp.fft.rfft(z, axis=-1)
            low, high = (freq[..., :COF], freq[..., COF:])
            mask = jnp.where(jnp.abs(high) >= param[..., None], 1.0, 0.0)
            rec = jnp.fft.irfft(jnp.concatenate([low, high * mask], axis=-1), axis=-1)
            rec = rec[..., ::2]
            return z + jnp.einsum('bli,oi->blo', rec, mlp_w)
        key = jax.random.key(seed)
        ks = jax.random.split(key, 8)
        inv = lambda n: 1.0 / np.sqrt(n)
        return {'x': jax.random.normal(ks[0], (B, H, W, C), jnp.float32), 'mlp_h1_w': jax.random.normal(ks[1], (DIM, DIM // 2), jnp.float32) * inv(DIM // 2), 'mlp_w1_w': jax.random.normal(ks[2], (DIM, DIM // 2), jnp.float32) * inv(DIM // 2), 'mlp_c_w': jax.random.normal(ks[3], (C, C), jnp.float32) * inv(C), 'reweight_h_w': jax.random.normal(ks[4], (C, C), jnp.float32) * inv(C), 'reweight_w_w': jax.random.normal(ks[5], (C, C), jnp.float32) * inv(C), 'param_h': jax.random.normal(ks[6], (1, W * GROUP), jnp.float32), 'param_w': jax.random.normal(ks[7], (1, H * GROUP), jnp.float32)}
    _L0_conv_all = _L0_conv_setup()
    _L0_conv_in = {k: v for k, v in _L0_conv_all.items() if k in ('mlp_h1_w', 'mlp_w1_w', 'mlp_c_w', 'reweight_h_w', 'reweight_w_w', 'param_h', 'param_w')}
    del _L0_conv_all

    def _L1_conv_setup():
        import jax, jax.numpy as jnp
        import numpy as np
        D_MODEL = 128
        NUM_HEADS = 8
        BIAS_SIZE = 2 * 30 - 1
        LN_EPS = 1e-05

        def _spatial_bias_matrix(spatial_bias, H, W):
            idx = jnp.arange(H * W)
            hh, ww = (idx // W, idx % W)
            dist = jnp.abs(hh[:, None] - hh[None, :]) + jnp.abs(ww[:, None] - ww[None, :])
            return spatial_bias[:, 0][dist]
        key = jax.random.key(seed)
        ks = jax.random.split(key, 12)
        d = D_MODEL
        s = 1.0 / np.sqrt(d)
        inp = {'x': jax.random.normal(ks[0], (16, 30, 30, d), dtype=jnp.float32), 'wq': jax.random.normal(ks[1], (d, d), dtype=jnp.float32) * s, 'bq': jnp.zeros((d,), jnp.float32), 'wk': jax.random.normal(ks[2], (d, d), dtype=jnp.float32) * s, 'bk': jnp.zeros((d,), jnp.float32), 'wv': jax.random.normal(ks[3], (d, d), dtype=jnp.float32) * s, 'bv': jnp.zeros((d,), jnp.float32), 'wo': jax.random.normal(ks[4], (d, d), dtype=jnp.float32) * s, 'bo': jnp.zeros((d,), jnp.float32), 'ln_gamma': jnp.ones((d,), jnp.float32), 'ln_beta': jnp.zeros((d,), jnp.float32), 'spatial_bias': jax.random.normal(ks[5], (BIAS_SIZE, BIAS_SIZE), dtype=jnp.float32) * 0.02}
        return inp
    _L1_conv_all = _L1_conv_setup()
    _L1_conv_in = {k: v for k, v in _L1_conv_all.items() if k in ('wq', 'bq', 'wk', 'bk', 'wv', 'bv', 'wo', 'bo', 'ln_gamma', 'ln_beta', 'spatial_bias')}
    del _L1_conv_all
    return {'x': x, 'L0_conv_mlp_h1_w': _L0_conv_in['mlp_h1_w'], 'L0_conv_mlp_w1_w': _L0_conv_in['mlp_w1_w'], 'L0_conv_mlp_c_w': _L0_conv_in['mlp_c_w'], 'L0_conv_reweight_h_w': _L0_conv_in['reweight_h_w'], 'L0_conv_reweight_w_w': _L0_conv_in['reweight_w_w'], 'L0_conv_param_h': _L0_conv_in['param_h'], 'L0_conv_param_w': _L0_conv_in['param_w'], 'L1_conv_wq': _L1_conv_in['wq'], 'L1_conv_bq': _L1_conv_in['bq'], 'L1_conv_wk': _L1_conv_in['wk'], 'L1_conv_bk': _L1_conv_in['bk'], 'L1_conv_wv': _L1_conv_in['wv'], 'L1_conv_bv': _L1_conv_in['bv'], 'L1_conv_wo': _L1_conv_in['wo'], 'L1_conv_bo': _L1_conv_in['bo'], 'L1_conv_ln_gamma': _L1_conv_in['ln_gamma'], 'L1_conv_ln_beta': _L1_conv_in['ln_beta'], 'L1_conv_spatial_bias': _L1_conv_in['spatial_bias']}

def reference(x, L0_conv_mlp_h1_w, L0_conv_mlp_w1_w, L0_conv_mlp_c_w, L0_conv_reweight_h_w, L0_conv_reweight_w_w, L0_conv_param_h, L0_conv_param_w, L1_conv_wq, L1_conv_bq, L1_conv_wk, L1_conv_bk, L1_conv_wv, L1_conv_bv, L1_conv_wo, L1_conv_bo, L1_conv_ln_gamma, L1_conv_ln_beta, L1_conv_spatial_bias):
    import jax
    import jax.numpy as jnp

    def _L0_conv_ref(x, mlp_h1_w, mlp_w1_w, mlp_c_w, reweight_h_w, reweight_w_w, param_h, param_w):
        import jax, jax.numpy as jnp
        import numpy as np
        B, H, W, C = (8, 56, 56, 128)
        GROUP = 8
        S = C // GROUP
        DIM = H * S
        COF = int(0.25 * DIM + 1)

        def _spectral_branch(z, param, mlp_w):
            freq = jnp.fft.rfft(z, axis=-1)
            low, high = (freq[..., :COF], freq[..., COF:])
            mask = jnp.where(jnp.abs(high) >= param[..., None], 1.0, 0.0)
            rec = jnp.fft.irfft(jnp.concatenate([low, high * mask], axis=-1), axis=-1)
            rec = rec[..., ::2]
            return z + jnp.einsum('bli,oi->blo', rec, mlp_w)
        h1 = x.reshape(B, H, W, GROUP, S).transpose(0, 3, 2, 1, 4).reshape(B, GROUP * W, H * S)
        h1 = _spectral_branch(h1, param_h, mlp_h1_w)
        h1 = h1.reshape(B, GROUP, W, H, S).transpose(0, 3, 2, 1, 4).reshape(B, H, W, C)
        w1 = x.reshape(B, H, W, GROUP, S).transpose(0, 1, 3, 2, 4).reshape(B, H * GROUP, W * S)
        w1 = _spectral_branch(w1, param_w, mlp_w1_w)
        w1 = w1.reshape(B, H, GROUP, W, S).transpose(0, 1, 3, 2, 4).reshape(B, H, W, C)
        c = jnp.einsum('bhwc,oc->bhwo', x, mlp_c_w)
        a = jnp.einsum('bwc,oc->bwo', h1.mean(axis=1), reweight_h_w)[:, None, :, :]
        b = jnp.einsum('bhc,oc->bho', w1.mean(axis=2), reweight_w_w)[:, :, None, :]
        return h1 * b + w1 * a + c * (a + b)

    def _L1_conv_ref(x, wq, bq, wk, bk, wv, bv, wo, bo, ln_gamma, ln_beta, spatial_bias):
        import jax, jax.numpy as jnp
        import numpy as np
        D_MODEL = 128
        NUM_HEADS = 8
        BIAS_SIZE = 2 * 30 - 1
        LN_EPS = 1e-05

        def _spatial_bias_matrix(spatial_bias, H, W):
            idx = jnp.arange(H * W)
            hh, ww = (idx // W, idx % W)
            dist = jnp.abs(hh[:, None] - hh[None, :]) + jnp.abs(ww[:, None] - ww[None, :])
            return spatial_bias[:, 0][dist]
        B, H, W, d_model = x.shape
        S = H * W
        d_k = d_model // NUM_HEADS
        x_seq = x.reshape(B, S, d_model)

        def proj(w, b):
            return (x_seq @ w + b).reshape(B, S, NUM_HEADS, d_k).transpose(0, 2, 1, 3)
        q = proj(wq, bq)
        k = proj(wk, bk)
        v = proj(wv, bv)
        scores = jnp.einsum('bhqd,bhkd->bhqk', q, k) / jnp.sqrt(jnp.float32(d_k))
        scores = scores + _spatial_bias_matrix(spatial_bias, H, W)[None, None]
        attn = jax.nn.softmax(scores, axis=-1)
        ctx = jnp.einsum('bhqk,bhkd->bhqd', attn, v)
        ctx = ctx.transpose(0, 2, 1, 3).reshape(B, S, d_model)
        out = ctx @ wo + bo
        resid = out + x_seq
        mu = jnp.mean(resid, axis=-1, keepdims=True)
        var = jnp.mean((resid - mu) ** 2, axis=-1, keepdims=True)
        out = (resid - mu) * jax.lax.rsqrt(var + LN_EPS) * ln_gamma + ln_beta
        return out.reshape(B, H, W, d_model)

    def _gn(v, G=32, eps=1e-05):
        B_, H_, W_, C_ = v.shape
        g = v.reshape(B_, H_, W_, G, C_ // G)
        m = jnp.mean(g, axis=(1, 2, 4), keepdims=True)
        s = jnp.var(g, axis=(1, 2, 4), keepdims=True)
        return ((g - m) / jnp.sqrt(s + eps)).reshape(v.shape)

    def _ln_c(v, eps=1e-06):
        m = jnp.mean(v, axis=-1, keepdims=True)
        s = jnp.var(v, axis=-1, keepdims=True)
        return (v - m) / jnp.sqrt(s + eps)

    def _ln_t(v, eps=1e-05):
        m = jnp.mean(v, axis=-1, keepdims=True)
        s = jnp.var(v, axis=-1, keepdims=True)
        return (v - m) / jnp.sqrt(s + eps)

    def _to_tokens(v):
        B_, H_, W_, C_ = v.shape
        return v.reshape(B_, H_ * W_, C_)

    def _from_tokens(t, like):
        return t.reshape(like.shape)
    x = _L0_conv_ref(x, L0_conv_mlp_h1_w, L0_conv_mlp_w1_w, L0_conv_mlp_c_w, L0_conv_reweight_h_w, L0_conv_reweight_w_w, L0_conv_param_h, L0_conv_param_w)
    x = _L1_conv_ref(x, L1_conv_wq, L1_conv_bq, L1_conv_wk, L1_conv_bk, L1_conv_wv, L1_conv_bv, L1_conv_wo, L1_conv_bo, L1_conv_ln_gamma, L1_conv_ln_beta, L1_conv_spatial_bias)
    return x

_drawn_inputs = setup_inputs


def setup_inputs(seed=0):
    import zlib

    import numpy as np

    out = dict(_drawn_inputs(seed))
    spreads = {'L1_conv_bq': (0.0, 0.8),
     'L1_conv_bk': (0.0, 2.0),
     'L1_conv_bv': (0.0, 0.1),
     'L1_conv_bo': (0.0, 0.1),
     'L1_conv_ln_gamma': (1.0, 0.2),
     'L1_conv_ln_beta': (0.0, 0.1)}
    factors = {'L0_conv_param_h': 8.0,
     'L0_conv_param_w': 8.0,
     'L1_conv_wq': 2.947,
     'L1_conv_wk': 2.841,
     'L1_conv_spatial_bias': 22.248}
    for name, (base, spread) in spreads.items():
        noise = np.random.default_rng([zlib.crc32(name.encode()), seed]).standard_normal(out[name].shape)
        drawn = base * np.exp(spread * noise) if base else spread * noise
        out[name] = jnp.asarray(drawn.astype(out[name].dtype))
    for name, factor in factors.items():
        out[name] = (out[name] * factor).astype(out[name].dtype)
    return out
```

```python
from contextlib import ExitStack

import concourse.bass as bass
import numpy as np
from concourse import mybir

ALU = mybir.AluOpType
ACT = mybir.ActivationFunctionType
AX = mybir.AxisListType
F32 = mybir.dt.float32
F16 = mybir.dt.float16
I32 = mybir.dt.int32

B, H, W, C = 8, 56, 56, 128
GROUPS, S = 8, 16
DIM = H * S
HALF = DIM // 2
Q = HALF // 2
KT = 112
NK = HALF // KT
GP = 64
KR = GP + H
OT = DIM // 128
DIAG = 2 * W - 1
HEADS, DK = 8, 16
HG = 4
NG = HEADS // HG
TOK = H * W
NT = H // 2
QC = 8
CH = QC * W
NC = H // QC
UT = QC // 2
RP = 64
STK = 4 * DK
WIN = DIAG * W
STG_K = (H + QC - 1) * W
STG_Q = (H + QC - 2) * W
DIST = 59
LN_EPS = 1e-5
HEAD = 1
RSQRT_GUESS = 0x5F3759DF
NEWTON = 4
LINKS = 9 + 4 * NEWTON


def constants():
    j = np.arange(Q)
    m = np.arange(HALF)[:, None]
    even = 2 * np.pi * ((2 * m * j) % DIM) / DIM
    odd = 2 * np.pi * (((2 * m + 1) * j) % DIM) / DIM
    e = np.concatenate([np.cos(even), -np.sin(even)], axis=1)
    o = np.concatenate([np.cos(odd), -np.sin(odd)], axis=1)
    e[:, Q] = 1.0 - 2.0 * (np.arange(HALF) % 2)
    o[:, Q] = 0.0
    inv = np.concatenate([np.cos(even), -np.sin(even)], axis=1) * 2.0 / DIM
    inv[:, 0] = 1.0 / DIM
    inv[:, Q] = (1.0 - 2.0 * (np.arange(HALF) % 2)) * 2.0 / DIM
    p = np.arange(128)
    flags = np.zeros((128, 4))
    flags[:, 0] = -1.0 * (p % 32 >= DK)
    flags[:, 1] = -1.0 * (p % STK >= 2 * DK)
    flags[:, 2] = -1.0 * (p >= W)
    flags[:, 3] = 1.0 * (p != 0)
    ident = np.eye(128)
    fold = (p[:KT, None] % W == np.arange(W)[None, :]) * 1.0
    sums = (p[:, None] % 32 == DK) * (p[:, None] // 32 == p[None, :] // 32) * 1.0
    s = np.abs(np.arange(DIAG) - (W - 1))
    dist = np.minimum(s[:, None] + s[None, :], DIST - 1).reshape(-1)
    pick = (np.arange(DIST)[:, None] == dist[None, :]) * 1.0
    mirror = np.eye(W)[:, ::-1]
    none = np.zeros((W, W))
    flips = np.stack([np.hstack([mirror, mirror]), np.hstack([mirror, none]), np.hstack([none, mirror])], axis=1)
    f = lambda a: np.ascontiguousarray(a, dtype=np.float32)
    return {"dft_even": f(e), "dft_odd": f(o), "inv_t": f(inv), "flags": f(flags), "ident": f(ident),
            "fold": f(fold), "sum_pick": f(sums), "dist_pick": f(pick), "flips": f(flips)}


def prepare_layer0(nc, a, w):
    with ExitStack() as ctx:
        sb = lambda n, s, d=F32: ctx.enter_context(nc.sbuf_tensor(n, s, d))
        sem = lambda n: ctx.enter_context(nc.semaphore(n))
        mlp = [sb(f"mlp{r}", [128, OT, HALF]) for r in range(2)]
        mlp_t = sb("mlp_t", [KT, NK, DIM])
        inv = sb("inv", [KT, NK, HALF])
        small = sb("small", [128, 3, 128])
        ps = ctx.enter_context(nc.psum_tensor("prep_ps", [128, 8, 512], F32))
        loaded, cleared = sem("prep_loaded"), sem("prep_cleared")
        tr_ready, tr_copied = sem("prep_tr_ready"), sem("prep_tr_copied")
        g_ready, g_copied = sem("prep_g_ready"), sem("prep_g_copied")
        small_ready, small_copied = sem("prep_small_ready"), sem("prep_small_copied")
        block = ctx.enter_context(nc.Block())

        @block.sync
        def _(sp):
            sp.dma_start(w["ident"][:], a["ident"]).then_inc(loaded, 16)
            sp.dma_start(w["flags"][:], a["flags"]).then_inc(loaded, 16)
            sp.dma_start(mlp[0][:], a["L0_conv_mlp_h1_w"].rearrange("(t p) m -> p t m", p=128)).then_inc(loaded, 16)
            sp.dma_start(inv[:], a["inv_t"].rearrange("(t p) m -> p t m", p=KT)).then_inc(loaded, 16)
            sp.dma_start(mlp[1][:], a["L0_conv_mlp_w1_w"].rearrange("(t p) m -> p t m", p=128)).then_inc(loaded, 16)
            for i, n in enumerate(("L0_conv_mlp_c_w", "L0_conv_reweight_h_w", "L0_conv_reweight_w_w")):
                sp.dma_start(small[:, i, :], a[n]).then_inc(loaded, 16)
            sp.wait_ge(cleared, 2)
            for dst, src in (("dft_e", "dft_even"), ("dft_o", "dft_odd")):
                for e in range(2):
                    sp.dma_start(w[dst][GP * e:GP * e + H, :, :],
                                 a[src].rearrange("(h k e) j -> e h k j", k=NK, e=2)[e]).then_inc(loaded, 16)
            sp.dma_start(w["par"][:, 0, :], a["L0_conv_param_h"].partition_broadcast(KT)).then_inc(loaded, 16)
            sp.dma_start(w["par"][:, 1, :], a["L0_conv_param_w"].partition_broadcast(KT)).then_inc(loaded, 16)
            sp.wait_ge(loaded, 16 * 14)

        @block.tensor
        def _(pe):
            pe.wait_ge(loaded, 16 * 14)
            for i in range(3):
                last = nc.tensor.transpose(ps[:, 7, 128 * i:128 * i + 128], small[:, i, :], w["ident"][:])
            last.then_inc(small_ready, 1)
            n = 0
            for r in range(2):
                if r:
                    pe.wait_ge(g_copied, 2 * NK)
                for mt in range(NK):
                    for part in range(2):
                        tiles = range(0, 4) if part == 0 else range(4, OT)
                        if n >= 2:
                            pe.wait_ge(tr_copied, n - 1)
                        for t in tiles:
                            last = nc.tensor.transpose(ps[0:KT, n % 2, 128 * (t % 4):128 * (t % 4) + 128],
                                                       mlp[r][:, t, mt * KT:(mt + 1) * KT], w["ident"][:])
                        last.then_inc(tr_ready, 1)
                        n += 1
                pe.wait_ge(tr_copied, n)
                for ct in range(NK):
                    for hf in range(2):
                        k = r * 2 * NK + ct * 2 + hf
                        if k >= 2:
                            pe.wait_ge(g_copied, k - 1)
                        for mt in range(NK):
                            last = nc.tensor.matmul(ps[0:KT, 2 + k % 2, 0:HALF], inv[:, mt, ct * KT:(ct + 1) * KT],
                                                    mlp_t[:, mt, hf * HALF:(hf + 1) * HALF],
                                                    start=mt == 0, stop=mt == NK - 1)
                        last.then_inc(g_ready, 1)

        @block.scalar
        def _(act):
            act.wait_ge(small_ready, 1)
            nc.scalar.copy(w["chan_t"][:].rearrange("p i c -> p (i c)"), ps[:, 7, 0:384]).then_inc(small_copied, 1)
            for k in range(4 * NK):
                r, ct, hf = k // (2 * NK), k // 2 % NK, k % 2
                act.wait_ge(g_ready, k + 1)
                nc.scalar.copy(w["G"][r][:, ct, hf * HALF:(hf + 1) * HALF], ps[0:KT, 2 + k % 2, 0:HALF]).then_inc(g_copied, 1)

        @block.vector
        def _(dve):
            for t in ("dft_e", "dft_o"):
                nc.vector.memset(w[t][:], 0.0).then_inc(cleared, 1)
            dve.wait_ge(loaded, 16 * 14)
            nc.vector.scalar_tensor_tensor(w["thr"][:, 0, :], w["par"][:, 0, :], 0.0, w["par"][:, 0, :], ALU.max, ALU.mult)
            nc.vector.scalar_tensor_tensor(w["thr"][:, 1, :].rearrange("p (g h) -> p h g", g=GROUPS),
                                           w["par"][:, 1, :].rearrange("p (h g) -> p h g", g=GROUPS), 0.0,
                                           w["par"][:, 1, :].rearrange("p (h g) -> p h g", g=GROUPS), ALU.max, ALU.mult)
            nc.vector.memset(w["Y"][:], 0.0)
            for n in range(4 * NK):
                r, mt, part = n // (2 * NK), n // 2 % NK, n % 2
                if n == 2 * NK:
                    dve.wait_ge(g_copied, 2 * NK)
                dve.wait_ge(tr_ready, n + 1)
                width = 512 if part == 0 else DIM - 512
                nc.vector.tensor_copy(mlp_t[:, mt, 512 * part:512 * part + width], ps[0:KT, n % 2, 0:width]).then_inc(tr_copied, 1)


def layer0(nc, a, w, scr):
    PARTS = 4
    PT = NT // PARTS
    with ExitStack() as ctx:
        sb = lambda n, s, d=F32: ctx.enter_context(nc.sbuf_tensor(n, s, d))
        sem = lambda n: ctx.enter_context(nc.semaphore(n))
        x = [sb(f"x{r}", [H, H * C]) for r in range(2)]
        zt = [sb(f"zt{i}", [KR, NK, HALF]) for i in range(2)]
        odd_re, odd_im = sb("odd_re", [KT, HALF]), sb("odd_im", [KT, HALF])
        hi_re, hi_im = sb("hi_re", [KT, HALF]), sb("hi_im", [KT, HALF])
        lo_re, lo_im = sb("lo_re", [KT, HALF]), sb("lo_im", [KT, HALF])
        sq_re, sq_im = sb("sq_re", [KT, HALF]), sb("sq_im", [KT, HALF])
        mask = sb("mask", [KT, HALF])
        mean, mean_t, rew = sb("mean", [H, 2, C]), sb("mean_t", [C, 2, H]), sb("rew", [H, 2, C])
        mh = [sb(f"mh{i}", [KT, PT, C]) for i in range(2)]
        mw = [sb(f"mw{i}", [KT, PT, C]) for i in range(2)]
        mx = [sb(f"mx{i}", [KT, PT, C]) for i in range(2)]
        mb = [sb(f"mb{i}", [KT, PT, C]) for i in range(2)]
        ma = [sb(f"ma{i}", [KT, C]) for i in range(2)]
        xt = [sb(f"xt{i}", [C, PT, KT]) for i in range(2)]
        ps = ctx.enter_context(nc.psum_tensor("l0_ps", [128, 8, 512], F32))
        TB, FB, IB = 0, 2, 6
        x_in, x_out = sem("x_in"), sem("x_out")
        tr_ready = sem("tr_ready")
        zt_act, zt_dve = sem("zt_act"), sem("zt_dve")
        odd_ready, even_ready = sem("odd_ready"), sem("even_ready")
        odd_copied = sem("odd_copied")
        high_ready, squared, masked = sem("high_ready"), sem("squared"), sem("masked")
        y_ready = sem("y_ready")
        inv_ready = sem("inv_ready")
        added, mean_ready, mean_tr, mean_copied = sem("added"), sem("mean_ready"), sem("mean_tr"), sem("mean_copied")
        rew_ready, rew_copied, rew_out = sem("rew_ready"), sem("rew_copied"), sem("rew_out")
        mix_in, mix_out = sem("mix_in"), sem("mix_out")
        xt_ready, xt_copied, chan_ready = sem("xt_ready"), sem("xt_copied"), sem("chan_ready")
        gap_clear = sem("gap_clear")
        passed = sem("passed")
        pool_step, dve_step, mixed = sem("pool_step"), sem("dve_step"), sem("mixed")
        block = ctx.enter_context(nc.Block())
        NT2 = S // 2
        NI = GROUPS

        xh = a["x"].rearrange("b h w c -> b w h c")
        oh = scr["h1"].rearrange("b h w c -> b w h c")
        tiles = lambda t: t.rearrange("b (j r) w c -> b r w j c", r=2)

        @block.sync
        def _(sp):
            with sp.Fori(0, B) as b:
                for r, src in enumerate((xh, a["x"])):
                    sp.dma_start(x[r][:].rearrange("p (t c) -> p t c", c=C),
                                 src[bass.ds(b, 1)].rearrange("o p t c -> (o p) t c")).then_inc(x_in, 16)
                for r, dst in enumerate((oh, scr["w1"])):
                    sp.wait_ge(added, HEAD + (b * 2 + r + 1) * NI * 2)
                    sp.sem_inc(passed, 1)
                    sp.dma_start(dst[bass.ds(b, 1)].rearrange("o p t c -> (o p) t c"),
                                 x[r][:].rearrange("p (t c) -> p t c", c=C)).then_inc(x_out, 16)
                sp.wait_ge(mean_ready, b * 2 + 2)
                for r in range(2):
                    sp.wait_ge(rew_copied, b * 2 + r + 1)
                    sp.sem_inc(passed, 1)
                    sp.dma_start(scr["rew"][bass.ds(b * 2 + r, 1)].rearrange("o p c -> (o p) c"), rew[:, r, :]).then_inc(rew_out, 16)
                sp.wait_ge(x_out, (b * 2 + 2) * 16)
                sp.wait_ge(rew_out, (b * 2 + 2) * 16)
                sp.sem_inc(passed, 1)

        @block.gpsimd
        def _(pool):
            with pool.Fori(0, B) as b:
                for r in range(2):
                    for jt in range(2):
                        n = (b * 2 + r) * 2 + jt
                        pool.wait_ge(squared, n * 2 + 2)
                        nc.gpsimd.tensor_tensor(sq_re[:], sq_re[:], sq_im[:], ALU.add).then_inc(masked, 1)
                pool.wait_ge(x_out, (b * 2 + 2) * 16)
                pool.wait_ge(rew_out, (b * 2 + 2) * 16)
                for p in range(PARTS):
                    i = p % 2
                    n = b * PARTS + p
                    if p >= 2:
                        pool.wait_ge(mix_out, (n - 1) * 32)
                        pool.sem_inc(passed, 1)
                    for src, dst in ((scr["h1"], mh[i]), (scr["w1"], mw[i]), (a["x"], mx[i])):
                        for rr in range(2):
                            v = tiles(src)[bass.ds(b, 1), rr, :, p * PT:(p + 1) * PT, :]
                            pool.dma_start(dst[rr * W:(rr + 1) * W, :, :], v.rearrange("o w j c -> (o w) j c")).then_inc(mix_in, 16)
                    for rr in range(2):
                        pool.dma_start(ma[i][rr * W:(rr + 1) * W, :],
                                       scr["rew"][bass.ds(b * 2, 1)].rearrange("o p c -> (o p) c")).then_inc(mix_in, 16)
                        hv = scr["rew"][bass.ds(b * 2 + 1, 1)].rearrange("o (j r) c -> r o j c", r=2)[rr, :, p * PT:(p + 1) * PT, :]
                        pool.dma_start(mb[i][rr * W:(rr + 1) * W, :, :], hv.broadcast_to([W, PT, C])).then_inc(mix_in, 16)
                    pool.wait_ge(mix_in, (n + 1) * 160)
                    am = ma[i][:].unsqueeze(1).broadcast_to([KT, PT, C])
                    nc.gpsimd.tensor_tensor(mh[i][:], mh[i][:], mb[i][:], ALU.mult).then_inc(pool_step, 1)
                    nc.gpsimd.tensor_tensor(mw[i][:], mw[i][:], am, ALU.mult).then_inc(pool_step, 1)
                    pool.wait_ge(pool_step, n * 4 + 2)
                    nc.gpsimd.tensor_tensor(mh[i][:], mh[i][:], mw[i][:], ALU.add).then_inc(pool_step, 1)
                    nc.gpsimd.tensor_tensor(mb[i][:], mb[i][:], am, ALU.add).then_inc(pool_step, 1)
                    pool.wait_ge(mixed, n + 1)
                    pool.sem_inc(passed, 1)
                    for rr in range(2):
                        v = tiles(scr["y"])[bass.ds(b, 1), rr, :, p * PT:(p + 1) * PT, :]
                        pool.dma_start(v.rearrange("o w j c -> (o w) j c"), mh[i][rr * W:(rr + 1) * W, :, :]).then_inc(mix_out, 16)
                pool.wait_ge(mix_out, (b + 1) * PARTS * 32)
                pool.sem_inc(passed, 1)

        @block.tensor
        def _(pe):
            with pe.Fori(0, B) as b:
                for r in range(2):
                    pe.wait_ge(x_in, (b + 1) * 32)
                    xv = x[r][:].rearrange("p (t c) -> p c t", c=C)
                    for t in range(S):
                        pe.wait_ge(zt_dve if t % 2 else zt_act, HEAD + (b * 2 + r) * NT2 + t // 2)
                        pe.sem_inc(passed, 1)
                        for g in range(GROUPS):
                            last = nc.tensor.transpose(ps[0:H, TB + t % 2, g * W:(g + 1) * W], xv[:, g * S + t, :], w["ident"][0:H, 0:H])
                        last.then_inc(tr_ready, 1)
                    pe.wait_ge(zt_act, HEAD + (b * 2 + r + 1) * NT2)
                    pe.wait_ge(zt_dve, HEAD + (b * 2 + r + 1) * NT2)
                    for jt in range(2):
                        n = (b * 2 + r) * 2 + jt
                        for part, (table, z, done) in enumerate(((w["dft_o"], zt[1], odd_ready), (w["dft_e"], zt[0], even_ready))):
                            for im in range(2):
                                if part == 0:
                                    pe.wait_ge(odd_copied, HEAD + n * 2)
                                else:
                                    pe.wait_ge(y_ready, HEAD + n * 2)
                                for k in range(NK):
                                    c0 = im * Q + jt * KT
                                    last = nc.tensor.matmul(ps[0:KT, FB + part * 2 + im, 0:HALF], table[:, k, c0:c0 + KT],
                                                            z[:, k, :], start=k == 0, stop=k == NK - 1)
                                last.then_inc(done, 1)
                    pe.wait_ge(y_ready, HEAD + (b * 2 + r + 1) * 4)
                    for i in range(NI):
                        n = (b * 2 + r) * NI + i
                        pe.wait_ge(added, HEAD + ((n - 1) * 2 if i >= 2 else (b * 2 + r) * NI * 2))
                        for k in range(NK):
                            last = nc.tensor.matmul(ps[0:GP + W, IB + i % 2, 0:HALF],
                                                    w["Y"][:, k, (i // 2) * 2 * GP:(i // 2) * 2 * GP + GP + W],
                                                    w["G"][r][:, k, (i % 2) * HALF:(i % 2 + 1) * HALF],
                                                    start=k == 0, stop=k == NK - 1)
                        last.then_inc(inv_ready, 1)
                for r in range(2):
                    pe.wait_ge(mean_ready, b * 2 + r + 1)
                    pe.sem_inc(passed, 1)
                    nc.tensor.transpose(ps[:, FB + r, 0:H], mean[:, r, :], w["ident"][0:H, 0:H]).then_inc(mean_tr, 1)
                    pe.wait_ge(mean_copied, b * 2 + r + 1)
                    nc.tensor.matmul(ps[0:H, FB + r, 128:256], mean_t[:, r, :], w["chan_t"][:, 1 + r, :],
                                     start=True, stop=True).then_inc(rew_ready, 1)
                pe.wait_ge(rew_copied, b * 2 + 2)
                for p in range(PARTS):
                    n = b * PARTS + p
                    pe.wait_ge(mix_in, (n + 1) * 160)
                    if p:
                        pe.wait_ge(xt_copied, n)
                    for t in range(PT):
                        last = nc.tensor.transpose(ps[:, FB + t // 4, KT * (t % 4):KT * (t % 4) + KT], mx[p % 2][:, t, :], w["ident"][0:KT, 0:KT])
                    last.then_inc(xt_ready, 1)
                    pe.wait_ge(xt_copied, n + 1)
                    if p:
                        pe.wait_ge(mixed, n)
                    for t in range(PT):
                        last = nc.tensor.matmul(ps[0:KT, FB + 2 + t // 4, C * (t % 4):C * (t % 4) + C], xt[p % 2][:, t, :],
                                                w["chan_t"][:, 0, :], start=True, stop=True)
                    last.then_inc(chan_ready, 1)
                pe.wait_ge(mixed, (b + 1) * PARTS)

        @block.scalar
        def _(act):
            for head in (zt_act, odd_copied):
                act.sem_inc(head, HEAD)
            act.wait_ge(gap_clear, 2)
            with act.Fori(0, B) as b:
                for r in range(2):
                    for t in range(NT2):
                        act.wait_ge(tr_ready, (b * 2 + r) * S + 2 * t + 1)
                        e = GP * (t % 2)
                        nc.scalar.copy(zt[0][e:e + H, t // 2, :], ps[0:H, TB, 0:HALF]).then_inc(zt_act, 1)
                    for jt in range(2):
                        n = (b * 2 + r) * 2 + jt
                        act.wait_ge(odd_ready, n * 2 + 1)
                        act.wait_ge(y_ready, HEAD + n * 2)
                        nc.scalar.copy(odd_re[:], ps[0:KT, FB, 0:HALF]).then_inc(odd_copied, 1)
                        act.wait_ge(odd_ready, n * 2 + 2)
                        nc.scalar.copy(odd_im[:], ps[0:KT, FB + 1, 0:HALF]).then_inc(odd_copied, 1)
                        act.wait_ge(high_ready, n * 2 + 1)
                        nc.scalar.activation(sq_re[:], hi_re[:], ACT.Square).then_inc(squared, 1)
                        act.wait_ge(high_ready, n * 2 + 2)
                        nc.scalar.activation(sq_im[:], hi_im[:], ACT.Square).then_inc(squared, 1)
                for r in range(2):
                    act.wait_ge(mean_tr, b * 2 + r + 1)
                    nc.scalar.activation(mean_t[:, r, :], ps[:, FB + r, 0:H], ACT.Copy, scale=1.0 / H).then_inc(mean_copied, 1)
                    act.wait_ge(rew_ready, b * 2 + r + 1)
                    nc.scalar.copy(rew[:, r, :], ps[0:H, FB + r, 128:256]).then_inc(rew_copied, 1)
                for p in range(PARTS):
                    n = b * PARTS + p
                    act.wait_ge(xt_ready, n + 1)
                    nc.scalar.copy(xt[p % 2][:, 0:4, :].rearrange("p t k -> p (t k)"), ps[:, FB, 0:4 * KT])
                    nc.scalar.copy(xt[p % 2][:, 4:PT, :].rearrange("p t k -> p (t k)"), ps[:, FB + 1, 0:(PT - 4) * KT]).then_inc(xt_copied, 1)

        @block.vector
        def _(dve):
            for head in (zt_dve, y_ready, added):
                dve.sem_inc(head, HEAD)
            for z in zt:
                nc.vector.memset(z[:], 0.0).then_inc(gap_clear, 1)
            dve.wait_ge(gap_clear, 2)
            with dve.Fori(0, B) as b:
                steps = 0
                per_image = 16 + 2 * PARTS

                def link(ins):
                    nonlocal steps
                    steps += 1
                    ins.then_inc(dve_step, 1)

                for r in range(2):
                    for t in range(NT2):
                        dve.wait_ge(tr_ready, (b * 2 + r) * S + 2 * t + 2)
                        e = GP * (t % 2)
                        nc.vector.tensor_copy(zt[1][e:e + H, t // 2, :], ps[0:H, TB + 1, 0:HALF]).then_inc(zt_dve, 1)
                    for jt in range(2):
                        n = (b * 2 + r) * 2 + jt
                        dve.wait_ge(odd_copied, HEAD + n * 2 + 1)
                        dve.wait_ge(even_ready, n * 2 + 1)
                        nc.vector.tensor_tensor(hi_re[:], ps[0:KT, FB + 2, 0:HALF], odd_re[:], ALU.subtract).then_inc(high_ready, 1)
                        link(nc.vector.tensor_tensor(lo_re[:], ps[0:KT, FB + 2, 0:HALF], odd_re[:], ALU.add))
                        dve.wait_ge(odd_copied, HEAD + n * 2 + 2)
                        dve.wait_ge(even_ready, n * 2 + 2)
                        if jt == 0:
                            nc.vector.scalar_tensor_tensor(hi_im[:], ps[0:KT, FB + 3, 0:HALF], w["flags"][0:KT, 3:4], odd_im[:],
                                                           ALU.mult, ALU.subtract).then_inc(high_ready, 1)
                        else:
                            nc.vector.tensor_tensor(hi_im[:], ps[0:KT, FB + 3, 0:HALF], odd_im[:], ALU.subtract).then_inc(high_ready, 1)
                        link(nc.vector.tensor_tensor(lo_im[:], ps[0:KT, FB + 3, 0:HALF], odd_im[:], ALU.add))
                        dve.wait_ge(masked, n + 1)
                        link(nc.vector.tensor_tensor(mask[:], sq_re[:], w["thr"][:, r, :], ALU.is_ge))
                        dve.wait_ge(dve_step, b * per_image + steps)
                        dve.wait_ge(high_ready, n * 2 + 2)
                        nc.vector.tensor_tensor(hi_re[:], hi_re[:], mask[:], ALU.mult)
                        link(nc.vector.tensor_tensor(hi_im[:], hi_im[:], mask[:], ALU.mult))
                        dve.wait_ge(dve_step, b * per_image + steps)
                        for im, (lo, hi) in enumerate(((lo_re, hi_re), (lo_im, hi_im))):
                            yv = w["Y"][:, im * 2 + jt, :].rearrange("p (g e) -> p g e", e=GP)[:, :, 0:W]
                            nc.vector.tensor_tensor(yv, lo[:].rearrange("p (g e) -> p g e", e=W),
                                                    hi[:].rearrange("p (g e) -> p g e", e=W), ALU.add).then_inc(y_ready, 1)
                    xg = x[r][:].rearrange("p (t g s) -> p g t s", g=GROUPS, s=S)
                    for i in range(NI):
                        n = (b * 2 + r) * NI + i
                        dve.wait_ge(inv_ready, n + 1)
                        for odd in range(2):
                            g, t0 = (i // 2) * 2 + odd, (i % 2) * (H // 2)
                            dst = xg[:, g, t0:t0 + H // 2, :]
                            nc.vector.tensor_tensor(dst, ps[GP * odd:GP * odd + W, IB + i % 2, 0:HALF].rearrange("p (t s) -> p t s", s=S),
                                                    dst, ALU.add).then_inc(added, 1)
                    dve.wait_ge(added, HEAD + (b * 2 + r + 1) * NI * 2)
                    nc.vector.tensor_reduce(mean[:, r, :], x[r][:].rearrange("p (t c) -> p c t", c=C), AX.X, ALU.add).then_inc(mean_ready, 1)
                for p in range(PARTS):
                    n = b * PARTS + p
                    i = p % 2
                    dve.wait_ge(pool_step, (n + 1) * 4)
                    dve.wait_ge(chan_ready, n + 1)
                    for hf, (t0, t1) in enumerate(((0, 4), (4, PT))):
                        nc.vector.tensor_tensor(mw[i][:, t0:t1, :], ps[0:KT, FB + 2 + hf, 0:C * (t1 - t0)].rearrange("p (t c) -> p t c", c=C),
                                                mb[i][:, t0:t1, :], ALU.mult).then_inc(dve_step, 1)
                        steps += 1
                    dve.wait_ge(dve_step, b * per_image + steps)
                    nc.vector.tensor_tensor(mh[i][:], mh[i][:], mw[i][:], ALU.add).then_inc(mixed, 1)
                assert steps == per_image, steps


def prepare_windows(nc, a, w, scr):
    with ExitStack() as ctx:
        sb = lambda n, s, d=F32: ctx.enter_context(nc.sbuf_tensor(n, s, d))
        sem = lambda n: ctx.enter_context(nc.semaphore(n))
        N = DIAG * DIAG
        pick, dist = sb("pick", [DIST, N]), sb("dist", [DIST, 1])
        line = sb("line", [1, N])
        mirrored = sb("mirrored", [W, WIN])
        flips = sb("flips", [W, 3, KT])
        high = sb("high", [KT, 2, 512], F16)
        ps = ctx.enter_context(nc.psum_tensor("win_ps", [128, 8, 512], F32))
        loaded, picked, copied, kept = sem("win_loaded"), sem("win_picked"), sem("win_copied"), sem("win_kept")
        spread, flipped, rounded, done = sem("win_spread"), sem("win_flipped"), sem("win_rounded"), sem("win_done")
        block = ctx.enter_context(nc.Block())
        pieces = [(i, min(512, N - i)) for i in range(0, N, 512)]
        cuts = [(i, min(512, WIN - i)) for i in range(0, WIN, 512)]
        query = WIN - W

        @block.sync
        def _(sp):
            sp.dma_start(pick[:], a["dist_pick"]).then_inc(loaded, 16)
            sp.dma_start(dist[:], a["L1_conv_spatial_bias"][:, 0:1], allow_slow_non_contiguous=True).then_inc(loaded, 16)
            sp.dma_start(flips[:], a["flips"]).then_inc(loaded, 16)
            sp.wait_ge(copied, len(pieces))
            sp.dma_start(scr["dist"].rearrange("s j -> (s j)").unsqueeze(0), line[:]).then_inc(kept, 16)
            sp.wait_ge(kept, 16)
            t = scr["dist"]
            sp.dma_start(mirrored[:].rearrange("p (s v) -> p s v", v=W),
                         bass.AP(t.tensor, t.offset, [[1, W], [DIAG, DIAG], [1, W]])).then_inc(spread, 16)
            sp.wait_ge(spread, 16)

        @block.tensor
        def _(pe):
            pe.wait_ge(loaded, 48)
            for n, (i, m) in enumerate(pieces):
                if n >= 8:
                    pe.wait_ge(copied, n - 7)
                nc.tensor.matmul(ps[0:1, n % 8, 0:m], dist[:], pick[:, i:i + m], start=True, stop=True).then_inc(picked, 1)
            pe.wait_ge(copied, len(pieces))
            pe.wait_ge(spread, 16)
            for n, (i, m) in enumerate(cuts):
                if n >= 2:
                    pe.wait_ge(done, 2 * n - 2)
                nc.tensor.matmul(ps[0:KT, n % 2, 0:m], flips[:, 0, :], mirrored[:, i:i + m], start=True, stop=True).then_inc(flipped, 1)
                m = min(m, query - i)
                nc.tensor.matmul(ps[0:KT, 2 + n % 2, 0:m], flips[:, 1, :], mirrored[:, i + W:i + W + m], start=True, stop=False)
                nc.tensor.matmul(ps[0:KT, 2 + n % 2, 0:m], flips[:, 2, :], mirrored[:, i:i + m], start=False, stop=True).then_inc(flipped, 1)

        @block.scalar
        def _(act):
            for n, (i, m) in enumerate(pieces):
                act.wait_ge(picked, n + 1)
                nc.scalar.copy(line[:, i:i + m], ps[0:1, n % 8, 0:m]).then_inc(copied, 1)
            for n, (i, m) in enumerate(cuts):
                act.wait_ge(flipped, 2 * n + 1)
                if n >= 2:
                    act.wait_ge(done, 2 * n - 2)
                nc.scalar.copy(high[:, n % 2, 0:m], ps[0:KT, n % 2, 0:m]).then_inc(rounded, 1)

        @block.vector
        def _(dve):
            for n, (i, m) in enumerate(cuts):
                dve.wait_ge(rounded, n + 1)
                nc.vector.scalar_tensor_tensor(w["by_key"][:, i:i + m], high[:, n % 2, 0:m], w["flags"][0:KT, 2:3],
                                               ps[0:KT, n % 2, 0:m], ALU.mult, ALU.add).then_inc(done, 1)
                dve.wait_ge(flipped, 2 * n + 2)
                m = min(m, query - i)
                nc.vector.tensor_copy(w["by_query"][:, i:i + m], ps[0:KT, 2 + n % 2, 0:m]).then_inc(done, 1)
            dve.wait_ge(done, 2 * len(cuts))


def layer1(nc, a, w, scr, out):
    with ExitStack() as ctx:
        sb = lambda n, s, d=F32: ctx.enter_context(nc.sbuf_tensor(n, s, d))
        sem = lambda n: ctx.enter_context(nc.semaphore(n))
        xn = sb("xn", [KT, NT, C])
        xT = sb("xT", [C, H * RP])
        qs = sb("qs", [STK, HG, TOK], F16)
        ks = sb("ks", [STK + 1, HG, H * RP], F16)
        v = sb("v", [GP + W, NT, HEADS, 32])
        p = [sb(f"p{i}", [GP + W, 2, CH]) for i in range(4)]
        q_max = sb("q_max", [STK + 1, HG, CH], F16)
        q_exp = sb("q_exp", [STK + 1, HG, CH], F16)
        win_max = sb("win_max", [KT, STG_Q], F16)
        win_exp = sb("win_exp", [KT, STG_K], F16)
        full = [sb(f"full{i}", [128, CH]) for i in range(2)]
        half = [sb(f"half{i}", [128, CH], F16) for i in range(2)]
        wq4, wk4 = sb("wq4", [C, HEADS, STK]), sb("wk4", [C, HEADS, STK])
        wv, wo = sb("wv", [C, C]), sb("wo", [128, NG, C])
        bq4, bk4 = sb("bq4", [128, HG]), sb("bk4", [128, HG])
        bv = sb("bv", [GP + W, C])
        bo, gamma, beta = sb("bo", [KT, C]), sb("gamma", [KT, C]), sb("beta", [KT, C])
        fold = sb("fold", [KT, W])
        fold16, id16 = sb("fold16", [KT, W], F16), sb("id16", [KT, KT], F16)
        sum_pick = sb("sum_pick", [128, 128])
        partial = sb("partial", [KT, UT * HG, NC])
        neg_max = sb("neg_max", [KT, UT * HG], F16)
        ctx_raw, recip, ctx1, ctx0c = sb("ctx_raw", [128, CH]), sb("recip", [128, CH]), sb("ctx1", [128, CH]), sb("ctx0c", [128, CH])
        ctx0 = sb("ctx0", [128, TOK])
        res, sq = sb("res", [KT, UT, C]), sb("sq", [KT, UT, C])
        stat = sb("stat", [KT, 3, UT])
        ps = ctx.enter_context(nc.psum_tensor("l1_ps", [128, 8, 512], F32))
        SB, CB, AB, MB = 0, 4, 5, 7

        loaded, set_up = sem("l1_loaded"), sem("l1_set_up")
        xn_in, xt_ready, xt_copied = sem("xn_in"), sem("l1_xt_ready"), sem("l1_xt_copied")
        v_ready, v_copied = sem("v_ready"), sem("v_copied")
        proj_ready, proj_full, proj_half, proj_done = sem("proj_ready"), sem("proj_full"), sem("proj_half"), sem("proj_done")
        staged_max, staged_exp = sem("staged_max"), sem("staged_exp")
        score_ready, max_done = sem("score_ready"), sem("max_done")
        neg_ready, row_ready, row_copied = sem("neg_ready"), sem("row_ready"), sem("row_copied")
        exp_ready, exp_done, pv_done = sem("exp_ready"), sem("exp_done"), sem("pv_done")
        ctx_copied, sum_ready, ctx_ready = sem("ctx_copied"), sem("sum_ready"), sem("ctx_ready")
        mix_ready, mixed_in, out_ready, stored = sem("mix_ready"), sem("mixed_in"), sem("out_ready"), sem("stored")
        res_free = sem("res_free")
        passed = sem("l1_passed")
        clear, recip_done, norm_step = sem("clear"), sem("recip_done"), sem("norm_step")
        sq_done, scaled = sem("sq_done"), sem("scaled")
        block = ctx.enter_context(nc.Block())
        EX = NT * 2
        MX = NT * HG
        LOADS = 8 + 16 + 1 + HEADS + 2 + 3 + 2
        PJ = 2 * NC * 2
        rows = lambda t, n=RP: t.rearrange("p (h e) -> p h e", e=n)

        def chunk_loop(eng, step):
            step(None, 0)
            with eng.Fori(0, NC - 1) as c:
                step(c, c + 1)
            step(NC - 1, None)

        @block.sync
        def _(sp):
            def load(dst, src):
                sp.dma_start(dst, src).then_inc(loaded, 16)
            sp.sem_inc(res_free, HEAD)
            sp.wait_ge(set_up, 1)
            for k in range(4):
                load(wq4[:, :, k * DK:(k + 1) * DK], a["L1_conv_wq"].rearrange("c (h d) -> c h d", d=DK))
                load(wk4[:, :, k * DK:(k + 1) * DK], a["L1_conv_wk"].rearrange("c (h d) -> c h d", d=DK))
            for n, (dst, src) in enumerate(((bq4, "L1_conv_bq"), (bk4, "L1_conv_bk"))):
                for k in range(8):
                    sp.dma_start(dst[k * DK:(k + 1) * DK, :], a[src].rearrange("(m e d) -> e d m", e=2, d=DK)[k // 4],
                                 allow_slow_non_contiguous=True).then_inc(loaded, 16)
            load(wv[:], a["L1_conv_wv"])
            for g in range(NG):
                for j in range(HG):
                    h = g * HG + j
                    load(wo[32 * j:32 * j + DK, g, :], a["L1_conv_wo"][h * DK:(h + 1) * DK, :])
            for r in range(2):
                load(bv[r * GP:r * GP + W, :], a["L1_conv_bv"].partition_broadcast(W))
            for dst, src in ((bo, "L1_conv_bo"), (gamma, "L1_conv_ln_gamma"), (beta, "L1_conv_ln_beta")):
                load(dst[:], a[src].partition_broadcast(KT))
            load(fold[:], a["fold"])
            load(sum_pick[:], a["sum_pick"])
            with sp.Fori(0, B) as b:
                for r in range(2):
                    sp.dma_start(xn[r * W:(r + 1) * W, :, :],
                                 scr["y"][bass.ds(b, 1)].rearrange("o (j r) w c -> r (o w) j c", r=2)[r]).then_inc(xn_in, 16)
                with sp.Fori(0, NC) as c:
                    n = b * NC + c
                    sp.wait_ge(out_ready, n + 1)
                    sp.sem_inc(passed, 1)
                    for r in range(2):
                        dst = out[bass.ds(b, 1), bass.ds(c * QC, QC)].rearrange("o (j r) w c -> r (o w) j c", r=2)[r]
                        sp.dma_start(dst, res[r * W:(r + 1) * W, :, :]).then_inc(stored, 16)
                    sp.wait_ge(stored, (n + 1) * 32)
                    sp.sem_inc(res_free, 1)
            sp.wait_ge(stored, B * NC * 32)

        @block.gpsimd
        def _(pool):
            with pool.Fori(0, B) as b:
                for g in range(NG):
                    base = (b * NG + g) * PJ
                    for n in range(PJ):
                        pool.wait_ge(proj_full, base + n + 1)
                        pool.sem_inc(passed, 1)
                        nc.gpsimd.tensor_copy(half[n % 2][:], full[n % 2][:]).then_inc(proj_half, 1)

        @block.tensor
        def _(pe):
            def scores(k):
                t, pair = k // 2, k % 2
                for e in range(2):
                    j, bank = 2 * pair + e, SB + 2 * pair + e
                    nc.tensor.matmul(ps[0:GP + W, bank, 0:CH], ks[:, j, t * 2 * RP:t * 2 * RP + GP + W], q_exp[:, j, :],
                                     start=True, stop=True)
                    for r in range(2):
                        s0 = (H - 1 - 2 * t - r) * W
                        last = nc.tensor.matmul(ps[r * GP:r * GP + W, bank, 0:CH], fold16[:], win_exp[:, s0:s0 + CH],
                                                start=False, stop=True, skip_group_check=True)
                last.then_inc(exp_ready, 1)

            def weigh(g, k):
                t, pair = k // 2, k % 2
                for e in range(2):
                    j = 2 * pair + e
                    last = nc.tensor.matmul(ps[32 * j:32 * j + 32, CB, 0:CH], v[:, t, g * HG + j, :], p[k % 4][:, e, :],
                                            start=t == 0, stop=t == NT - 1, skip_group_check=True)
                last.then_inc(pv_done, 1)

            def max_scores(i, base):
                t, j = i // HG, i % HG
                u, kc = t // NC, t % NC
                if i >= 2:
                    pe.wait_ge(max_done, base + i - 1)
                nc.tensor.matmul(ps[0:KT, AB + i % 2, 0:CH], q_max[:, j, u * KT:(u + 1) * KT],
                                 rows(ks[:, j, :])[:, kc * QC:(kc + 1) * QC, 0:W], start=True, stop=False)
                s0 = (QC * kc - 2 * u + QC - 2) * W
                nc.tensor.matmul(ps[0:KT, AB + i % 2, 0:CH], id16[:], win_max[:, s0:s0 + CH],
                                 start=False, stop=True).then_inc(score_ready, 1)

            pe.wait_ge(set_up, 2)
            with pe.Fori(0, B) as b:
                for g in range(NG):
                    G = b * NG + g
                    pe.wait_ge(ctx_ready, HEAD + G * NC)
                    pe.wait_ge(mixed_in, HEAD + b * NC)
                    if g == 0:
                        pe.wait_ge(xn_in, (b + 1) * 32)
                        for i in range(NC):
                            if i >= 2:
                                pe.wait_ge(xt_copied, b * NC + i - 1)
                            for t in range(UT):
                                last = nc.tensor.transpose(ps[:, AB + i % 2, t * KT:(t + 1) * KT], xn[:, i * UT + t, :], w["ident"][0:KT, 0:KT])
                            last.then_inc(xt_ready, 1)
                        pe.wait_ge(xt_copied, (b + 1) * NC)
                        for i in range(NC):
                            if i >= 2:
                                pe.wait_ge(v_copied, b * NC + i - 1)
                            for t in range(UT):
                                c0 = (i * UT + t) * 2 * RP
                                last = nc.tensor.matmul(ps[0:GP + W, AB + i % 2, t * C:(t + 1) * C], xT[:, c0:c0 + GP + W], wv[:],
                                                        start=True, stop=True)
                            last.then_inc(v_ready, 1)
                    for n in range(PJ):
                        m, ch, is_k = n // (2 * NC), n // 2 % NC, n % 2
                        h = g * HG + 2 * m
                        if n >= 4:
                            pe.wait_ge(proj_full, G * PJ + n - 3)
                        nc.tensor.matmul(ps[:, SB + n % 4, 0:CH], (wk4 if is_k else wq4)[:, h:h + 2, :].rearrange("c h k -> c (h k)"),
                                         rows(xT[:])[:, ch * QC:(ch + 1) * QC, 0:W], start=True, stop=True).then_inc(proj_ready, 1)
                    pe.wait_ge(proj_done, (G + 1) * PJ)
                    if g == 0:
                        pe.wait_ge(v_copied, (b + 1) * NC)

                    def step(c, q):
                        if c is not None:
                            n = G * NC + c
                            pe.wait_ge(staged_exp, HEAD + (n + 1) * 2)
                            pe.wait_ge(row_copied, (n + 1) * HG)
                        if q is not None:
                            pe.wait_ge(staged_max, (G * NC + q + 1) * 2)
                            pe.wait_ge(ctx_ready, HEAD + (G * NC + (0 if c is None else c)))
                            if g == 1:
                                pe.wait_ge(mixed_in, HEAD + (b * NC + (0 if c is None else c)))
                        for k in range(EX):
                            if c is not None:
                                if k >= 2:
                                    pe.wait_ge(exp_done, n * EX + k - 1)
                                scores(k)
                                if k >= 2:
                                    weigh(g, k - 2)
                            if q is not None:
                                for e in range(2):
                                    max_scores(2 * k + e, (G * NC + q) * MX)
                        if c is not None:
                            for k in (EX - 2, EX - 1):
                                pe.wait_ge(exp_done, n * EX + k + 1)
                                weigh(g, k)
                        if q is not None:
                            pe.wait_ge(neg_ready, G * NC + q + 1)
                            for j in range(HG):
                                for u in range(UT):
                                    last = nc.tensor.matmul(ps[32 * j:32 * j + 1, MB, u * KT:(u + 1) * KT],
                                                            neg_max[:, u * HG + j:u * HG + j + 1], id16[:], start=True, stop=True)
                            last.then_inc(row_ready, 1)
                        if c is not None:
                            pe.wait_ge(ctx_copied, n + 1)
                            nc.tensor.matmul(ps[:, AB, 0:CH], sum_pick[:], ctx_raw[:], start=True, stop=True).then_inc(sum_ready, 1)
                            if g == 1:
                                pe.wait_ge(ctx_ready, HEAD + n + 1)
                                for u in range(UT):
                                    for gg, cx in enumerate((ctx0c, ctx1)):
                                        last = nc.tensor.matmul(ps[0:KT, AB + 1, u * C:(u + 1) * C], cx[:, u * KT:(u + 1) * KT],
                                                                wo[:, gg, :], start=gg == 0, stop=gg == 1)
                                last.then_inc(mix_ready, 1)

                    chunk_loop(pe, step)

        @block.scalar
        def _(act):
            act.wait_ge(set_up, 2)
            with act.Fori(0, B) as b:
                for g in range(NG):
                    G = b * NG + g
                    for n in range(PJ):
                        is_k, m = n % 2, g * 2 + n // (2 * NC)
                        act.wait_ge(proj_ready, G * PJ + n + 1)
                        if n >= 2:
                            act.wait_ge(proj_done, G * PJ + n - 1)
                        nc.scalar.activation(full[n % 2][:], ps[:, SB + n % 4, 0:CH], ACT.Identity,
                                             bias=(bk4 if is_k else bq4)[:, m:m + 1],
                                             scale=1.0 if is_k else DK ** -0.5).then_inc(proj_full, 1)

                    def step(c, q):
                        if c is not None:
                            n = G * NC + c
                            for k in range(EX):
                                act.wait_ge(exp_ready, n * EX + k + 1)
                                if k >= 4:
                                    act.wait_ge(pv_done, n * EX + k - 3)
                                bank = SB + 2 * (k % 2)
                                nc.scalar.activation(p[k % 4][:], ps[0:GP + W, bank:bank + 2, 0:CH], ACT.Exp).then_inc(exp_done, 1)
                            act.wait_ge(pv_done, (n + 1) * EX)
                            act.wait_ge(ctx_ready, HEAD + n)
                            nc.scalar.copy(ctx_raw[:], ps[:, CB, 0:CH]).then_inc(ctx_copied, 1)
                        if q is not None:
                            act.wait_ge(row_ready, G * NC + q + 1)
                            for j in (2, 3):
                                nc.scalar.copy(q_exp[STK:STK + 1, j, :], ps[32 * j:32 * j + 1, MB, 0:CH]).then_inc(row_copied, 1)

                    chunk_loop(act, step)

        @block.vector
        def _(dve):
            for head in (ctx_ready, mixed_in, staged_exp):
                dve.sem_inc(head, HEAD)
            nc.vector.memset(xT[:], 0.0)
            nc.vector.memset(q_max[STK:STK + 1, :, :], 0.0)
            nc.vector.memset(ks[:], 0.0).then_inc(clear, 1)
            nc.vector.memset(v[:], 0.0).then_inc(clear, 1)
            nc.vector.memset(wo[:], 0.0)
            nc.vector.memset(bv[:], 0.0).then_inc(set_up, 1)
            dve.wait_ge(clear, 2)
            for j in range(HG):
                nc.vector.memset(rows(ks[STK:STK + 1, j, :])[:, :, 0:W], 1.0)
            for r in range(2):
                nc.vector.memset(v[r * GP:r * GP + W, :, :, DK:DK + 1], 1.0)
            dve.wait_ge(loaded, 16 * LOADS)
            nc.vector.tensor_copy(fold16[:], fold[:])
            nc.vector.tensor_copy(id16[:], w["ident"][0:KT, 0:KT])
            nc.vector.tensor_scalar(bq4[:], bq4[:], DK ** -0.5, None, ALU.mult).then_inc(set_up, 1)
            with dve.Fori(0, B) as b:
                for g in range(NG):
                    G = b * NG + g
                    if g == 0:
                        for i in range(NC):
                            dve.wait_ge(xt_ready, b * NC + i + 1)
                            nc.vector.tensor_copy(rows(xT[:])[:, i * QC:(i + 1) * QC, 0:W],
                                                  rows(ps[:, AB + i % 2, 0:CH], W)).then_inc(xt_copied, 1)
                        for i in range(NC):
                            dve.wait_ge(v_ready, b * NC + i + 1)
                            nc.vector.tensor_tensor(v[:, i * UT:(i + 1) * UT, :, 0:DK],
                                                    ps[0:GP + W, AB + i % 2, 0:UT * C].rearrange("p (t h d) -> p t h d", h=HEADS, d=DK),
                                                    bv[:].rearrange("p (h d) -> p h d", d=DK).unsqueeze(1).broadcast_to([GP + W, UT, HEADS, DK]),
                                                    ALU.add).then_inc(v_copied, 1)
                    for n in range(PJ):
                        m, ch, is_k = n // (2 * NC), n // 2 % NC, n % 2
                        dve.wait_ge(proj_half, G * PJ + n + 1)
                        for e in range(2):
                            part = slice(STK * e, STK * e + STK)
                            dst = (rows(ks[0:STK, 2 * m + e, :])[:, ch * QC:(ch + 1) * QC, 0:W] if is_k
                                   else rows(qs[:, 2 * m + e, :], W)[:, ch * QC:(ch + 1) * QC, :])
                            last = nc.vector.scalar_tensor_tensor(dst, rows(half[n % 2][part, :], W),
                                                                  w["flags"][part, 0:1] if is_k else w["flags"][part, 1:2],
                                                                  rows(full[n % 2][part, :], W), ALU.mult, ALU.add)
                        last.then_inc(proj_done, 1)

                    def step(c, q):
                        if q is not None:
                            n_max = G * NC + q
                            dve.wait_ge(proj_done, (G + 1) * PJ)
                            dve.wait_ge(staged_exp, HEAD + n_max * 2)
                            nc.vector.tensor_copy(q_max[0:STK, :, :], qs[:, :, bass.ds(q * CH, CH)]).then_inc(staged_max, 1)
                            nc.vector.tensor_copy(win_max[:], w["by_query"][:, bass.ds((H - QC - q * QC) * W, STG_Q)]).then_inc(staged_max, 1)
                            for i in range(MX):
                                t, j = i // HG, i % HG
                                u, kc = t // NC, t % NC
                                dve.wait_ge(score_ready, n_max * MX + i + 1)
                                nc.vector.tensor_reduce(partial[:, u * HG + j, kc:kc + 1], ps[0:KT, AB + i % 2, 0:CH], AX.X,
                                                        ALU.max).then_inc(max_done, 1)
                            dve.wait_ge(max_done, (n_max + 1) * MX)
                            nc.vector.tensor_reduce(neg_max[:], partial[:], AX.X, ALU.max, negate=True).then_inc(neg_ready, 1)
                            if c is not None:
                                dve.wait_ge(exp_ready, (G * NC + c + 1) * EX)
                            nc.vector.tensor_copy(q_exp[0:STK, :, :], q_max[0:STK, :, :]).then_inc(staged_exp, 1)
                            nc.vector.tensor_copy(win_exp[:], w["by_key"][:, bass.ds(q * QC * W, STG_K)]).then_inc(staged_exp, 1)
                            dve.wait_ge(row_ready, n_max + 1)
                            for j in (0, 1):
                                nc.vector.tensor_copy(q_exp[STK:STK + 1, j, :], ps[32 * j:32 * j + 1, MB, 0:CH]).then_inc(row_copied, 1)
                        if c is not None:
                            n = G * NC + c
                            dve.wait_ge(sum_ready, n + 1)
                            dve.wait_ge(ctx_ready, HEAD + n)
                            nc.vector.reciprocal(recip[:], ps[:, AB, 0:CH]).then_inc(recip_done, 1)
                            dve.wait_ge(recip_done, n + 1)
                            if g == 0:
                                nc.vector.tensor_tensor(ctx0[:, bass.ds(c * CH, CH)], ctx_raw[:], recip[:], ALU.mult).then_inc(ctx_ready, 1)
                            else:
                                nc.vector.tensor_copy(ctx0c[:], ctx0[:, bass.ds(c * CH, CH)])
                                nc.vector.tensor_tensor(ctx1[:], ctx_raw[:], recip[:], ALU.mult).then_inc(ctx_ready, 1)
                                normalise(b * NC + c, c)

                    def normalise(n, c):
                        done = 0

                        def link(ins):
                            nonlocal done
                            done += 1
                            ins.then_inc(norm_step, 1)
                            dve.wait_ge(norm_step, n * LINKS + done)

                        spread = lambda t: t.unsqueeze(2).broadcast_to([KT, UT, C])
                        each = lambda t: t[:].unsqueeze(1).broadcast_to([KT, UT, C])
                        dve.wait_ge(mix_ready, n + 1)
                        dve.wait_ge(res_free, HEAD + n)
                        nc.vector.tensor_tensor(res[:], ps[0:KT, AB + 1, :].rearrange("p (u c) -> p u c", c=C),
                                                xn[:, bass.ds(c * UT, UT), :], ALU.add).then_inc(mixed_in, 1)
                        dve.wait_ge(mixed_in, HEAD + n + 1)
                        link(nc.vector.tensor_tensor(res[:], res[:], each(bo), ALU.add))
                        link(nc.vector.tensor_reduce(stat[:, 0, :], res[:], AX.X, ALU.add))
                        link(nc.vector.tensor_scalar(stat[:, 0, :], stat[:, 0, :], 1.0 / C, None, ALU.mult))
                        link(nc.vector.tensor_tensor(res[:], res[:], spread(stat[:, 0, :]), ALU.subtract))
                        nc.vector.tensor_tensor(sq[:], res[:], res[:], ALU.mult).then_inc(sq_done, 1)
                        dve.wait_ge(sq_done, n + 1)
                        link(nc.vector.tensor_reduce(stat[:, 1, :], sq[:], AX.X, ALU.add))
                        var, y, t = stat[:, 2, :], stat[:, 0, :], stat[:, 1, :]
                        link(nc.vector.tensor_scalar(var, stat[:, 1, :], 1.0 / C, LN_EPS, ALU.mult, ALU.add))
                        link(nc.vector.tensor_scalar(y.bitcast(I32), var.bitcast(I32), 1, None, ALU.logical_shift_right))
                        link(nc.vector.tensor_scalar(y.bitcast(I32), y.bitcast(I32), -1, RSQRT_GUESS, ALU.mult, ALU.add))
                        for _ in range(NEWTON):
                            link(nc.vector.tensor_tensor(t, y, y, ALU.mult))
                            link(nc.vector.tensor_tensor(t, t, var, ALU.mult))
                            link(nc.vector.tensor_scalar(t, t, -0.5, 1.5, ALU.mult, ALU.add))
                            link(nc.vector.tensor_tensor(y, y, t, ALU.mult))
                        link(nc.vector.tensor_tensor(res[:], res[:], spread(y), ALU.mult))
                        assert done == LINKS
                        nc.vector.tensor_tensor(sq[:], res[:], each(gamma), ALU.mult).then_inc(scaled, 1)
                        dve.wait_ge(scaled, n + 1)
                        nc.vector.tensor_tensor(res[:], sq[:], each(beta), ALU.add).then_inc(out_ready, 1)

                    chunk_loop(dve, step)


def two_layers(nc, a, out):
    h1 = nc.dram_tensor("h1_scratch", [B, H, W, C], F32, kind="Internal").ap()
    w1 = nc.dram_tensor("w1_scratch", [B, H, W, C], F32, kind="Internal").ap()
    y = nc.dram_tensor("y_scratch", [B, H, W, C], F32, kind="Internal").ap()
    rew = nc.dram_tensor("rew_scratch", [2 * B, H, C], F32, kind="Internal").ap()
    dist = nc.dram_tensor("dist_scratch", [DIAG, DIAG], F32, kind="Internal").ap()
    scr = {"h1": h1, "w1": w1, "y": y, "rew": rew, "dist": dist}
    with ExitStack() as whole:
        keep = lambda c, n, s, d=F32: c.enter_context(nc.sbuf_tensor(n, s, d))
        w = {"ident": keep(whole, "ident_sb", [128, 128]), "flags": keep(whole, "flags_sb", [128, 4])}
        with ExitStack() as first:
            w["G"] = [keep(first, f"G{r}", [KT, NK, DIM]) for r in range(2)]
            w["dft_e"], w["dft_o"] = keep(first, "dft_e", [KR, NK, HALF]), keep(first, "dft_o", [KR, NK, HALF])
            w["chan_t"] = keep(first, "chan_t", [C, 3, C])
            w["par"], w["thr"] = keep(first, "par", [KT, 2, HALF]), keep(first, "thr", [KT, 2, HALF])
            w["Y"] = keep(first, "Y", [KT, NK, GROUPS * GP])
            prepare_layer0(nc, a, w)
            layer0(nc, a, w, scr)
        w["by_query"], w["by_key"] = keep(whole, "by_query", [KT, WIN], F16), keep(whole, "by_key", [KT, WIN], F16)
        prepare_windows(nc, a, w, scr)
        layer1(nc, a, w, scr, out)


_INS = ["x", "L0_conv_mlp_h1_w", "L0_conv_mlp_w1_w", "L0_conv_mlp_c_w", "L0_conv_reweight_h_w", "L0_conv_reweight_w_w",
        "L0_conv_param_h", "L0_conv_param_w", "L1_conv_wq", "L1_conv_bq", "L1_conv_wk", "L1_conv_bk", "L1_conv_wv",
        "L1_conv_bv", "L1_conv_wo", "L1_conv_bo", "L1_conv_ln_gamma", "L1_conv_ln_beta", "L1_conv_spatial_bias"]


def kernel(**inputs):
    import numpy as _np
    import concourse.bacc as _bacc
    from concourse import mybir as _mybir
    from concourse.bass_utils import run_bass_kernel_spmd as _run

    nc = _bacc.Bacc("TRN2", target_bir_lowering=False, num_devices=1)
    arrays, args = {}, {}
    given = {n: _np.ascontiguousarray(inputs[n]) for n in _INS}
    given.update(constants())
    for name, a in given.items():
        arrays[f"in_{name}"] = a
        args[name] = nc.dram_tensor(f"in_{name}", a.shape, _mybir.dt.from_np(a.dtype), kind="ExternalInput").ap()
    out = nc.dram_tensor("out_0", (B, H, W, C), _mybir.dt.from_np(_np.dtype("float32")), kind="ExternalOutput").ap()
    two_layers(nc, args, out)
    r = _run(nc, [arrays], core_ids=[0])
    return r.results[0]["out_0"]
```

```python
from contextlib import ExitStack

import concourse.bass as bass
import numpy as np
from concourse import mybir

ALU = mybir.AluOpType
ACT = mybir.ActivationFunctionType
AX = mybir.AxisListType
F32 = mybir.dt.float32
F16 = mybir.dt.float16
I32 = mybir.dt.int32

B, H, W, C = 8, 56, 56, 128
GROUPS, S = 8, 16
DIM = H * S
HALF = DIM // 2
Q = HALF // 2
KT = 112
NK = HALF // KT
GP = 64
KR = GP + H
OT = DIM // 128
DIAG = 2 * W - 1
HEADS, DK = 8, 16
HG = 4
NG = HEADS // HG
TOK = H * W
NT = H // 2
QC = 8
CH = QC * W
NC = H // QC
UT = QC // 2
RP = 64
STK = 4 * DK
WIN = DIAG * W
STG_K = (H + QC - 1) * W
STG_Q = (H + QC - 2) * RP
DIST = 59
LN_EPS = 1e-5
HEAD = 1
RSQRT_GUESS = 0x5F3759DF
NEWTON = 4
LINKS = 11 + 4 * NEWTON


def constants():
    j = np.arange(Q)
    m = np.arange(HALF)[:, None]
    even = 2 * np.pi * ((2 * m * j) % DIM) / DIM
    odd = 2 * np.pi * (((2 * m + 1) * j) % DIM) / DIM
    e = np.concatenate([np.cos(even), -np.sin(even)], axis=1)
    o = np.concatenate([np.cos(odd), -np.sin(odd)], axis=1)
    e[:, Q] = 1.0 - 2.0 * (np.arange(HALF) % 2)
    o[:, Q] = 0.0
    inv = np.concatenate([np.cos(even), -np.sin(even)], axis=1) * 2.0 / DIM
    inv[:, 0] = 1.0 / DIM
    inv[:, Q] = (1.0 - 2.0 * (np.arange(HALF) % 2)) * 2.0 / DIM
    p = np.arange(128)
    flags = np.zeros((128, 4))
    flags[:, 0] = -1.0 * (p % 32 >= DK)
    flags[:, 1] = -1.0 * (p % STK >= 2 * DK)
    flags[:, 2] = -1.0 * (p >= W)
    flags[:, 3] = 1.0 * (p != 0)
    ident = np.eye(128)
    fold = (p[:KT, None] % W == np.arange(W)[None, :]) * 1.0
    sums = (p[:, None] % 32 == DK) * (p[:, None] // 32 == p[None, :] // 32) * 1.0
    s = np.abs(np.arange(DIAG) - (W - 1))
    dist = np.minimum(s[:, None] + s[None, :], DIST - 1).reshape(-1)
    pick = (np.arange(DIST)[:, None] == dist[None, :]) * 1.0
    mirror = np.eye(W)[:, ::-1]
    none = np.zeros((W, W))
    flips = np.stack([np.hstack([mirror, mirror]), np.hstack([mirror, none]), np.hstack([none, mirror])], axis=1)
    f = lambda a: np.ascontiguousarray(a, dtype=np.float32)
    return {"dft_even": f(e), "dft_odd": f(o), "inv_t": f(inv), "flags": f(flags), "ident": f(ident),
            "fold": f(fold), "sum_pick": f(sums), "dist_pick": f(pick), "flips": f(flips)}


def prepare_layer0(nc, a, w):
    with ExitStack() as ctx:
        sb = lambda n, s, d=F32: ctx.enter_context(nc.sbuf_tensor(n, s, d))
        sem = lambda n: ctx.enter_context(nc.semaphore(n))
        mlp = [sb(f"mlp{r}", [128, OT, HALF]) for r in range(2)]
        mlp_t = sb("mlp_t", [KT, NK, DIM])
        inv = sb("inv", [KT, NK, HALF])
        small = sb("small", [128, 3, 128])
        ps = ctx.enter_context(nc.psum_tensor("prep_ps", [128, 8, 512], F32))
        loaded, cleared = sem("prep_loaded"), sem("prep_cleared")
        tr_ready, tr_copied = sem("prep_tr_ready"), sem("prep_tr_copied")
        g_ready, g_copied = sem("prep_g_ready"), sem("prep_g_copied")
        small_ready, small_copied = sem("prep_small_ready"), sem("prep_small_copied")
        block = ctx.enter_context(nc.Block())

        @block.sync
        def _(sp):
            sp.dma_start(w["ident"][:], a["ident"]).then_inc(loaded, 16)
            sp.dma_start(w["flags"][:], a["flags"]).then_inc(loaded, 16)
            sp.dma_start(mlp[0][:], a["L0_conv_mlp_h1_w"].rearrange("(t p) m -> p t m", p=128)).then_inc(loaded, 16)
            sp.dma_start(inv[:], a["inv_t"].rearrange("(t p) m -> p t m", p=KT)).then_inc(loaded, 16)
            sp.dma_start(mlp[1][:], a["L0_conv_mlp_w1_w"].rearrange("(t p) m -> p t m", p=128)).then_inc(loaded, 16)
            for i, n in enumerate(("L0_conv_mlp_c_w", "L0_conv_reweight_h_w", "L0_conv_reweight_w_w")):
                sp.dma_start(small[:, i, :], a[n]).then_inc(loaded, 16)
            sp.wait_ge(cleared, 2)
            for dst, src in (("dft_e", "dft_even"), ("dft_o", "dft_odd")):
                for e in range(2):
                    sp.dma_start(w[dst][GP * e:GP * e + H, :, :],
                                 a[src].rearrange("(h k e) j -> e h k j", k=NK, e=2)[e]).then_inc(loaded, 16)
            sp.dma_start(w["par"][:, 0, :], a["L0_conv_param_h"].partition_broadcast(KT)).then_inc(loaded, 16)
            sp.dma_start(w["par"][:, 1, :], a["L0_conv_param_w"].partition_broadcast(KT)).then_inc(loaded, 16)
            sp.wait_ge(loaded, 16 * 14)

        @block.tensor
        def _(pe):
            pe.wait_ge(loaded, 16 * 14)
            for i in range(3):
                last = nc.tensor.transpose(ps[:, 7, 128 * i:128 * i + 128], small[:, i, :], w["ident"][:])
            last.then_inc(small_ready, 1)
            n = 0
            for r in range(2):
                if r:
                    pe.wait_ge(g_copied, 2 * NK)
                for mt in range(NK):
                    for part in range(2):
                        tiles = range(0, 4) if part == 0 else range(4, OT)
                        if n >= 2:
                            pe.wait_ge(tr_copied, n - 1)
                        for t in tiles:
                            last = nc.tensor.transpose(ps[0:KT, n % 2, 128 * (t % 4):128 * (t % 4) + 128],
                                                       mlp[r][:, t, mt * KT:(mt + 1) * KT], w["ident"][:])
                        last.then_inc(tr_ready, 1)
                        n += 1
                pe.wait_ge(tr_copied, n)
                for ct in range(NK):
                    for hf in range(2):
                        k = r * 2 * NK + ct * 2 + hf
                        if k >= 2:
                            pe.wait_ge(g_copied, k - 1)
                        for mt in range(NK):
                            last = nc.tensor.matmul(ps[0:KT, 2 + k % 2, 0:HALF], inv[:, mt, ct * KT:(ct + 1) * KT],
                                                    mlp_t[:, mt, hf * HALF:(hf + 1) * HALF],
                                                    start=mt == 0, stop=mt == NK - 1)
                        last.then_inc(g_ready, 1)

        @block.scalar
        def _(act):
            act.wait_ge(small_ready, 1)
            nc.scalar.copy(w["chan_t"][:].rearrange("p i c -> p (i c)"), ps[:, 7, 0:384]).then_inc(small_copied, 1)
            for k in range(4 * NK):
                r, ct, hf = k // (2 * NK), k // 2 % NK, k % 2
                act.wait_ge(g_ready, k + 1)
                nc.scalar.copy(w["G"][r][:, ct, hf * HALF:(hf + 1) * HALF], ps[0:KT, 2 + k % 2, 0:HALF]).then_inc(g_copied, 1)

        @block.vector
        def _(dve):
            for t in ("dft_e", "dft_o"):
                nc.vector.memset(w[t][:], 0.0).then_inc(cleared, 1)
            dve.wait_ge(loaded, 16 * 14)
            nc.vector.scalar_tensor_tensor(w["thr"][:, 0, :], w["par"][:, 0, :], 0.0, w["par"][:, 0, :], ALU.max, ALU.mult)
            nc.vector.scalar_tensor_tensor(w["thr"][:, 1, :].rearrange("p (g h) -> p h g", g=GROUPS),
                                           w["par"][:, 1, :].rearrange("p (h g) -> p h g", g=GROUPS), 0.0,
                                           w["par"][:, 1, :].rearrange("p (h g) -> p h g", g=GROUPS), ALU.max, ALU.mult)
            nc.vector.memset(w["Y"][:], 0.0)
            for n in range(4 * NK):
                r, mt, part = n // (2 * NK), n // 2 % NK, n % 2
                if n == 2 * NK:
                    dve.wait_ge(g_copied, 2 * NK)
                dve.wait_ge(tr_ready, n + 1)
                width = 512 if part == 0 else DIM - 512
                nc.vector.tensor_copy(mlp_t[:, mt, 512 * part:512 * part + width], ps[0:KT, n % 2, 0:width]).then_inc(tr_copied, 1)


def layer0(nc, a, w, scr):
    PARTS = 4
    PT = NT // PARTS
    with ExitStack() as ctx:
        sb = lambda n, s, d=F32: ctx.enter_context(nc.sbuf_tensor(n, s, d))
        sem = lambda n: ctx.enter_context(nc.semaphore(n))
        x = [sb(f"x{r}", [H, H * C]) for r in range(2)]
        zt = [sb(f"zt{i}", [KR, NK, HALF]) for i in range(2)]
        odd_re, odd_im = sb("odd_re", [KT, HALF]), sb("odd_im", [KT, HALF])
        hi_re, hi_im = sb("hi_re", [KT, HALF]), sb("hi_im", [KT, HALF])
        lo_re, lo_im = sb("lo_re", [KT, HALF]), sb("lo_im", [KT, HALF])
        sq_re, sq_im = sb("sq_re", [KT, HALF]), sb("sq_im", [KT, HALF])
        mask = sb("mask", [KT, HALF])
        mean, mean_t, rew = sb("mean", [H, 2, C]), sb("mean_t", [C, 2, H]), sb("rew", [H, 2, C])
        mh = [sb(f"mh{i}", [KT, PT, C]) for i in range(2)]
        mw = [sb(f"mw{i}", [KT, PT, C]) for i in range(2)]
        mx = [sb(f"mx{i}", [KT, PT, C]) for i in range(2)]
        mb = [sb(f"mb{i}", [KT, PT, C]) for i in range(2)]
        ma = [sb(f"ma{i}", [KT, C]) for i in range(2)]
        xt = [sb(f"xt{i}", [C, PT, KT]) for i in range(2)]
        ps = ctx.enter_context(nc.psum_tensor("l0_ps", [128, 8, 512], F32))
        TB, FB, IB = 0, 2, 6
        x_in, x_out = sem("x_in"), sem("x_out")
        tr_ready = sem("tr_ready")
        zt_act, zt_dve = sem("zt_act"), sem("zt_dve")
        odd_ready, even_ready = sem("odd_ready"), sem("even_ready")
        odd_copied = sem("odd_copied")
        high_ready, squared, masked = sem("high_ready"), sem("squared"), sem("masked")
        y_ready = sem("y_ready")
        inv_ready = sem("inv_ready")
        added, mean_ready, mean_tr, mean_copied = sem("added"), sem("mean_ready"), sem("mean_tr"), sem("mean_copied")
        rew_ready, rew_copied, rew_out = sem("rew_ready"), sem("rew_copied"), sem("rew_out")
        mix_in, mix_out = sem("mix_in"), sem("mix_out")
        xt_ready, xt_copied, chan_ready = sem("xt_ready"), sem("xt_copied"), sem("chan_ready")
        gap_clear = sem("gap_clear")
        passed = sem("passed")
        pool_step, dve_step, mixed = sem("pool_step"), sem("dve_step"), sem("mixed")
        block = ctx.enter_context(nc.Block())
        NT2 = S // 2
        NI = GROUPS

        xh = a["x"].rearrange("b h w c -> b w h c")
        oh = scr["h1"].rearrange("b h w c -> b w h c")
        tiles = lambda t: t.rearrange("b (j r) w c -> b r w j c", r=2)

        @block.sync
        def _(sp):
            with sp.Fori(0, B) as b:
                for r, src in enumerate((xh, a["x"])):
                    sp.dma_start(x[r][:].rearrange("p (t c) -> p t c", c=C),
                                 src[bass.ds(b, 1)].rearrange("o p t c -> (o p) t c")).then_inc(x_in, 16)
                for r, dst in enumerate((oh, scr["w1"])):
                    sp.wait_ge(added, HEAD + (b * 2 + r + 1) * NI * 2)
                    sp.sem_inc(passed, 1)
                    sp.dma_start(dst[bass.ds(b, 1)].rearrange("o p t c -> (o p) t c"),
                                 x[r][:].rearrange("p (t c) -> p t c", c=C)).then_inc(x_out, 16)
                sp.wait_ge(mean_ready, b * 2 + 2)
                for r in range(2):
                    sp.wait_ge(rew_copied, b * 2 + r + 1)
                    sp.sem_inc(passed, 1)
                    sp.dma_start(scr["rew"][bass.ds(b * 2 + r, 1)].rearrange("o p c -> (o p) c"), rew[:, r, :]).then_inc(rew_out, 16)
                sp.wait_ge(x_out, (b * 2 + 2) * 16)
                sp.wait_ge(rew_out, (b * 2 + 2) * 16)
                sp.sem_inc(passed, 1)

        @block.gpsimd
        def _(pool):
            with pool.Fori(0, B) as b:
                for r in range(2):
                    for jt in range(2):
                        n = (b * 2 + r) * 2 + jt
                        pool.wait_ge(squared, n * 2 + 2)
                        nc.gpsimd.tensor_tensor(sq_re[:], sq_re[:], sq_im[:], ALU.add).then_inc(masked, 1)
                pool.wait_ge(x_out, (b * 2 + 2) * 16)
                pool.wait_ge(rew_out, (b * 2 + 2) * 16)
                for p in range(PARTS):
                    i = p % 2
                    n = b * PARTS + p
                    if p >= 2:
                        pool.wait_ge(mix_out, (n - 1) * 32)
                        pool.sem_inc(passed, 1)
                    for src, dst in ((scr["h1"], mh[i]), (scr["w1"], mw[i]), (a["x"], mx[i])):
                        for rr in range(2):
                            v = tiles(src)[bass.ds(b, 1), rr, :, p * PT:(p + 1) * PT, :]
                            pool.dma_start(dst[rr * W:(rr + 1) * W, :, :], v.rearrange("o w j c -> (o w) j c")).then_inc(mix_in, 16)
                    for rr in range(2):
                        pool.dma_start(ma[i][rr * W:(rr + 1) * W, :],
                                       scr["rew"][bass.ds(b * 2, 1)].rearrange("o p c -> (o p) c")).then_inc(mix_in, 16)
                        hv = scr["rew"][bass.ds(b * 2 + 1, 1)].rearrange("o (j r) c -> r o j c", r=2)[rr, :, p * PT:(p + 1) * PT, :]
                        pool.dma_start(mb[i][rr * W:(rr + 1) * W, :, :], hv.broadcast_to([W, PT, C])).then_inc(mix_in, 16)
                    pool.wait_ge(mix_in, (n + 1) * 160)
                    am = ma[i][:].unsqueeze(1).broadcast_to([KT, PT, C])
                    nc.gpsimd.tensor_tensor(mh[i][:], mh[i][:], mb[i][:], ALU.mult).then_inc(pool_step, 1)
                    nc.gpsimd.tensor_tensor(mw[i][:], mw[i][:], am, ALU.mult).then_inc(pool_step, 1)
                    pool.wait_ge(pool_step, n * 4 + 2)
                    nc.gpsimd.tensor_tensor(mh[i][:], mh[i][:], mw[i][:], ALU.add).then_inc(pool_step, 1)
                    nc.gpsimd.tensor_tensor(mb[i][:], mb[i][:], am, ALU.add).then_inc(pool_step, 1)
                    pool.wait_ge(mixed, n + 1)
                    pool.sem_inc(passed, 1)
                    for rr in range(2):
                        v = tiles(scr["y"])[bass.ds(b, 1), rr, :, p * PT:(p + 1) * PT, :]
                        pool.dma_start(v.rearrange("o w j c -> (o w) j c"), mh[i][rr * W:(rr + 1) * W, :, :]).then_inc(mix_out, 16)
                pool.wait_ge(mix_out, (b + 1) * PARTS * 32)
                pool.sem_inc(passed, 1)

        @block.tensor
        def _(pe):
            with pe.Fori(0, B) as b:
                for r in range(2):
                    pe.wait_ge(x_in, (b + 1) * 32)
                    xv = x[r][:].rearrange("p (t c) -> p c t", c=C)
                    for t in range(S):
                        pe.wait_ge(zt_dve if t % 2 else zt_act, HEAD + (b * 2 + r) * NT2 + t // 2)
                        pe.sem_inc(passed, 1)
                        for g in range(GROUPS):
                            last = nc.tensor.transpose(ps[0:H, TB + t % 2, g * W:(g + 1) * W], xv[:, g * S + t, :], w["ident"][0:H, 0:H])
                        last.then_inc(tr_ready, 1)
                    pe.wait_ge(zt_act, HEAD + (b * 2 + r + 1) * NT2)
                    pe.wait_ge(zt_dve, HEAD + (b * 2 + r + 1) * NT2)
                    for jt in range(2):
                        n = (b * 2 + r) * 2 + jt
                        for part, (table, z, done) in enumerate(((w["dft_o"], zt[1], odd_ready), (w["dft_e"], zt[0], even_ready))):
                            for im in range(2):
                                if part == 0:
                                    pe.wait_ge(odd_copied, HEAD + n * 2)
                                else:
                                    pe.wait_ge(y_ready, HEAD + n * 2)
                                for k in range(NK):
                                    c0 = im * Q + jt * KT
                                    last = nc.tensor.matmul(ps[0:KT, FB + part * 2 + im, 0:HALF], table[:, k, c0:c0 + KT],
                                                            z[:, k, :], start=k == 0, stop=k == NK - 1)
                                last.then_inc(done, 1)
                    pe.wait_ge(y_ready, HEAD + (b * 2 + r + 1) * 4)
                    for i in range(NI):
                        n = (b * 2 + r) * NI + i
                        pe.wait_ge(added, HEAD + ((n - 1) * 2 if i >= 2 else (b * 2 + r) * NI * 2))
                        for k in range(NK):
                            last = nc.tensor.matmul(ps[0:GP + W, IB + i % 2, 0:HALF],
                                                    w["Y"][:, k, (i // 2) * 2 * GP:(i // 2) * 2 * GP + GP + W],
                                                    w["G"][r][:, k, (i % 2) * HALF:(i % 2 + 1) * HALF],
                                                    start=k == 0, stop=k == NK - 1)
                        last.then_inc(inv_ready, 1)
                for r in range(2):
                    pe.wait_ge(mean_ready, b * 2 + r + 1)
                    pe.sem_inc(passed, 1)
                    nc.tensor.transpose(ps[:, FB + r, 0:H], mean[:, r, :], w["ident"][0:H, 0:H]).then_inc(mean_tr, 1)
                    pe.wait_ge(mean_copied, b * 2 + r + 1)
                    nc.tensor.matmul(ps[0:H, FB + r, 128:256], mean_t[:, r, :], w["chan_t"][:, 1 + r, :],
                                     start=True, stop=True).then_inc(rew_ready, 1)
                pe.wait_ge(rew_copied, b * 2 + 2)
                for p in range(PARTS):
                    n = b * PARTS + p
                    pe.wait_ge(mix_in, (n + 1) * 160)
                    if p:
                        pe.wait_ge(xt_copied, n)
                    for t in range(PT):
                        last = nc.tensor.transpose(ps[:, FB + t // 4, KT * (t % 4):KT * (t % 4) + KT], mx[p % 2][:, t, :], w["ident"][0:KT, 0:KT])
                    last.then_inc(xt_ready, 1)
                    pe.wait_ge(xt_copied, n + 1)
                    if p:
                        pe.wait_ge(mixed, n)
                    for t in range(PT):
                        last = nc.tensor.matmul(ps[0:KT, FB + 2 + t // 4, C * (t % 4):C * (t % 4) + C], xt[p % 2][:, t, :],
                                                w["chan_t"][:, 0, :], start=True, stop=True)
                    last.then_inc(chan_ready, 1)
                pe.wait_ge(mixed, (b + 1) * PARTS)

        @block.scalar
        def _(act):
            for head in (zt_act, odd_copied):
                act.sem_inc(head, HEAD)
            act.wait_ge(gap_clear, 2)
            with act.Fori(0, B) as b:
                for r in range(2):
                    for t in range(NT2):
                        act.wait_ge(tr_ready, (b * 2 + r) * S + 2 * t + 1)
                        e = GP * (t % 2)
                        nc.scalar.copy(zt[0][e:e + H, t // 2, :], ps[0:H, TB, 0:HALF]).then_inc(zt_act, 1)
                    for jt in range(2):
                        n = (b * 2 + r) * 2 + jt
                        act.wait_ge(odd_ready, n * 2 + 1)
                        act.wait_ge(y_ready, HEAD + n * 2)
                        nc.scalar.copy(odd_re[:], ps[0:KT, FB, 0:HALF]).then_inc(odd_copied, 1)
                        act.wait_ge(odd_ready, n * 2 + 2)
                        nc.scalar.copy(odd_im[:], ps[0:KT, FB + 1, 0:HALF]).then_inc(odd_copied, 1)
                        act.wait_ge(high_ready, n * 2 + 1)
                        nc.scalar.activation(sq_re[:], hi_re[:], ACT.Square).then_inc(squared, 1)
                        act.wait_ge(high_ready, n * 2 + 2)
                        nc.scalar.activation(sq_im[:], hi_im[:], ACT.Square).then_inc(squared, 1)
                for r in range(2):
                    act.wait_ge(mean_tr, b * 2 + r + 1)
                    nc.scalar.activation(mean_t[:, r, :], ps[:, FB + r, 0:H], ACT.Copy, scale=1.0 / H).then_inc(mean_copied, 1)
                    act.wait_ge(rew_ready, b * 2 + r + 1)
                    nc.scalar.copy(rew[:, r, :], ps[0:H, FB + r, 128:256]).then_inc(rew_copied, 1)
                for p in range(PARTS):
                    n = b * PARTS + p
                    act.wait_ge(xt_ready, n + 1)
                    nc.scalar.copy(xt[p % 2][:, 0:4, :].rearrange("p t k -> p (t k)"), ps[:, FB, 0:4 * KT])
                    nc.scalar.copy(xt[p % 2][:, 4:PT, :].rearrange("p t k -> p (t k)"), ps[:, FB + 1, 0:(PT - 4) * KT]).then_inc(xt_copied, 1)

        @block.vector
        def _(dve):
            for head in (zt_dve, y_ready, added):
                dve.sem_inc(head, HEAD)
            for z in zt:
                nc.vector.memset(z[:], 0.0).then_inc(gap_clear, 1)
            dve.wait_ge(gap_clear, 2)
            with dve.Fori(0, B) as b:
                steps = 0
                per_image = 16 + 2 * PARTS

                def link(ins):
                    nonlocal steps
                    steps += 1
                    ins.then_inc(dve_step, 1)

                for r in range(2):
                    for t in range(NT2):
                        dve.wait_ge(tr_ready, (b * 2 + r) * S + 2 * t + 2)
                        e = GP * (t % 2)
                        nc.vector.tensor_copy(zt[1][e:e + H, t // 2, :], ps[0:H, TB + 1, 0:HALF]).then_inc(zt_dve, 1)
                    for jt in range(2):
                        n = (b * 2 + r) * 2 + jt
                        dve.wait_ge(odd_copied, HEAD + n * 2 + 1)
                        dve.wait_ge(even_ready, n * 2 + 1)
                        nc.vector.tensor_tensor(hi_re[:], ps[0:KT, FB + 2, 0:HALF], odd_re[:], ALU.subtract).then_inc(high_ready, 1)
                        link(nc.vector.tensor_tensor(lo_re[:], ps[0:KT, FB + 2, 0:HALF], odd_re[:], ALU.add))
                        dve.wait_ge(odd_copied, HEAD + n * 2 + 2)
                        dve.wait_ge(even_ready, n * 2 + 2)
                        if jt == 0:
                            nc.vector.scalar_tensor_tensor(hi_im[:], ps[0:KT, FB + 3, 0:HALF], w["flags"][0:KT, 3:4], odd_im[:],
                                                           ALU.mult, ALU.subtract).then_inc(high_ready, 1)
                        else:
                            nc.vector.tensor_tensor(hi_im[:], ps[0:KT, FB + 3, 0:HALF], odd_im[:], ALU.subtract).then_inc(high_ready, 1)
                        link(nc.vector.tensor_tensor(lo_im[:], ps[0:KT, FB + 3, 0:HALF], odd_im[:], ALU.add))
                        dve.wait_ge(masked, n + 1)
                        link(nc.vector.tensor_tensor(mask[:], sq_re[:], w["thr"][:, r, :], ALU.is_ge))
                        dve.wait_ge(dve_step, b * per_image + steps)
                        dve.wait_ge(high_ready, n * 2 + 2)
                        nc.vector.tensor_tensor(hi_re[:], hi_re[:], mask[:], ALU.mult)
                        link(nc.vector.tensor_tensor(hi_im[:], hi_im[:], mask[:], ALU.mult))
                        dve.wait_ge(dve_step, b * per_image + steps)
                        for im, (lo, hi) in enumerate(((lo_re, hi_re), (lo_im, hi_im))):
                            yv = w["Y"][:, im * 2 + jt, :].rearrange("p (g e) -> p g e", e=GP)[:, :, 0:W]
                            nc.vector.tensor_tensor(yv, lo[:].rearrange("p (g e) -> p g e", e=W),
                                                    hi[:].rearrange("p (g e) -> p g e", e=W), ALU.add).then_inc(y_ready, 1)
                    xg = x[r][:].rearrange("p (t g s) -> p g t s", g=GROUPS, s=S)
                    for i in range(NI):
                        n = (b * 2 + r) * NI + i
                        dve.wait_ge(inv_ready, n + 1)
                        for odd in range(2):
                            g, t0 = (i // 2) * 2 + odd, (i % 2) * (H // 2)
                            dst = xg[:, g, t0:t0 + H // 2, :]
                            nc.vector.tensor_tensor(dst, ps[GP * odd:GP * odd + W, IB + i % 2, 0:HALF].rearrange("p (t s) -> p t s", s=S),
                                                    dst, ALU.add).then_inc(added, 1)
                    dve.wait_ge(added, HEAD + (b * 2 + r + 1) * NI * 2)
                    nc.vector.tensor_reduce(mean[:, r, :], x[r][:].rearrange("p (t c) -> p c t", c=C), AX.X, ALU.add).then_inc(mean_ready, 1)
                for p in range(PARTS):
                    n = b * PARTS + p
                    i = p % 2
                    dve.wait_ge(pool_step, (n + 1) * 4)
                    dve.wait_ge(chan_ready, n + 1)
                    for hf, (t0, t1) in enumerate(((0, 4), (4, PT))):
                        nc.vector.tensor_tensor(mw[i][:, t0:t1, :], ps[0:KT, FB + 2 + hf, 0:C * (t1 - t0)].rearrange("p (t c) -> p t c", c=C),
                                                mb[i][:, t0:t1, :], ALU.mult).then_inc(dve_step, 1)
                        steps += 1
                    dve.wait_ge(dve_step, b * per_image + steps)
                    nc.vector.tensor_tensor(mh[i][:], mh[i][:], mw[i][:], ALU.add).then_inc(mixed, 1)
                assert steps == per_image, steps


def prepare_windows(nc, a, w, scr):
    with ExitStack() as ctx:
        sb = lambda n, s, d=F32: ctx.enter_context(nc.sbuf_tensor(n, s, d))
        sem = lambda n: ctx.enter_context(nc.semaphore(n))
        N = DIAG * DIAG
        pick, dist = sb("pick", [DIST, N]), sb("dist", [DIST, 1])
        line = sb("line", [1, N])
        mirrored = sb("mirrored", [W, WIN])
        flips = sb("flips", [W, 3, KT])
        high = sb("high", [KT, 2, 512], F16)
        by_query = sb("by_query", [KT, DIAG - 1, RP], F16)
        ps = ctx.enter_context(nc.psum_tensor("win_ps", [128, 8, 512], F32))
        loaded, picked, copied, kept = sem("win_loaded"), sem("win_picked"), sem("win_copied"), sem("win_kept")
        spread, flipped, rounded, done = sem("win_spread"), sem("win_flipped"), sem("win_rounded"), sem("win_done")
        padded = sem("win_padded")
        block = ctx.enter_context(nc.Block())
        pieces = [(i, min(512, N - i)) for i in range(0, N, 512)]
        cut = 512 // W * W
        cuts = [(i, min(cut, WIN - i)) for i in range(0, WIN, cut)]
        query = WIN - W

        @block.sync
        def _(sp):
            sp.dma_start(pick[:], a["dist_pick"]).then_inc(loaded, 16)
            sp.dma_start(dist[:], a["L1_conv_spatial_bias"][:, 0:1], allow_slow_non_contiguous=True).then_inc(loaded, 16)
            sp.dma_start(flips[:], a["flips"]).then_inc(loaded, 16)
            sp.wait_ge(copied, len(pieces))
            sp.dma_start(scr["dist"].rearrange("s j -> (s j)").unsqueeze(0), line[:]).then_inc(kept, 16)
            sp.wait_ge(kept, 16)
            t = scr["dist"]
            sp.dma_start(mirrored[:].rearrange("p (s v) -> p s v", v=W),
                         bass.AP(t.tensor, t.offset, [[1, W], [DIAG, DIAG], [1, W]])).then_inc(spread, 16)
            sp.wait_ge(spread, 16)
            sp.wait_ge(done, 2 * len(cuts))
            sp.dma_start(scr["by_query"], by_query[:].rearrange("p s v -> p (s v)")).then_inc(kept, 16)
            sp.wait_ge(kept, 32)

        @block.gpsimd
        def _(pool):
            nc.gpsimd.memset(by_query[:], 0.0).then_inc(padded, 1)

        @block.tensor
        def _(pe):
            pe.wait_ge(loaded, 48)
            for n, (i, m) in enumerate(pieces):
                if n >= 8:
                    pe.wait_ge(copied, n - 7)
                nc.tensor.matmul(ps[0:1, n % 8, 0:m], dist[:], pick[:, i:i + m], start=True, stop=True).then_inc(picked, 1)
            pe.wait_ge(copied, len(pieces))
            pe.wait_ge(spread, 16)
            for n, (i, m) in enumerate(cuts):
                if n >= 2:
                    pe.wait_ge(done, 2 * n - 2)
                nc.tensor.matmul(ps[0:KT, n % 2, 0:m], flips[:, 0, :], mirrored[:, i:i + m], start=True, stop=True).then_inc(flipped, 1)
                m = min(m, query - i)
                nc.tensor.matmul(ps[0:KT, 2 + n % 2, 0:m], flips[:, 1, :], mirrored[:, i + W:i + W + m], start=True, stop=False)
                nc.tensor.matmul(ps[0:KT, 2 + n % 2, 0:m], flips[:, 2, :], mirrored[:, i:i + m], start=False, stop=True).then_inc(flipped, 1)

        @block.scalar
        def _(act):
            for n, (i, m) in enumerate(pieces):
                act.wait_ge(picked, n + 1)
                nc.scalar.copy(line[:, i:i + m], ps[0:1, n % 8, 0:m]).then_inc(copied, 1)
            for n, (i, m) in enumerate(cuts):
                act.wait_ge(flipped, 2 * n + 1)
                if n >= 2:
                    act.wait_ge(done, 2 * n - 2)
                nc.scalar.copy(high[:, n % 2, 0:m], ps[0:KT, n % 2, 0:m]).then_inc(rounded, 1)

        @block.vector
        def _(dve):
            dve.wait_ge(padded, 1)
            for n, (i, m) in enumerate(cuts):
                dve.wait_ge(rounded, n + 1)
                nc.vector.scalar_tensor_tensor(w["by_key"][:, i:i + m], high[:, n % 2, 0:m], w["flags"][0:KT, 2:3],
                                               ps[0:KT, n % 2, 0:m], ALU.mult, ALU.add).then_inc(done, 1)
                dve.wait_ge(flipped, 2 * n + 2)
                m = min(m, query - i)
                nc.vector.tensor_copy(by_query[:, i // W:(i + m) // W, 0:W],
                                      ps[0:KT, 2 + n % 2, 0:m].rearrange("p (s v) -> p s v", v=W)).then_inc(done, 1)
            dve.wait_ge(done, 2 * len(cuts))


def layer1(nc, a, w, scr, out):
    with ExitStack() as ctx:
        sb = lambda n, s, d=F32: ctx.enter_context(nc.sbuf_tensor(n, s, d))
        sem = lambda n: ctx.enter_context(nc.semaphore(n))
        VW = DK + 1
        xc = [sb(f"xc{i}", [KT, UT, C]) for i in range(2)]
        xT = sb("xT", [C, QC * RP])
        qs = sb("qs", [STK + 1, HG, TOK], F16)
        ks = [sb(f"ks{g}", [STK + 1, HG, H * RP], F16) for g in range(NG)]
        v = [sb(f"v{g}", [GP + W, NT * HG * VW + 32 - VW]) for g in range(NG)]
        p = [sb(f"p{i}", [GP + W, 2, CH]) for i in range(4)]
        q_max = sb("q_max", [STK + 1, HG, CH], F16)
        q_exp = sb("q_exp", [STK + 1, HG, CH], F16)
        q_pick = sb("q_pick", [128, HG, CH], F16)
        key_win = [sb(f"key_win{i}", [DK + KT, STG_Q], F16) for i in range(2)]
        win_exp = sb("win_exp", [KT, STG_K], F16)
        full = [sb(f"full{i}", [128, CH]) for i in range(3)]
        half = [sb(f"half{i}", [128, CH], F16) for i in range(3)]
        wq4, wk4 = sb("wq4", [C, HEADS, STK]), sb("wk4", [C, HEADS, STK])
        wv, wo = sb("wv", [C, C]), sb("wo", [128, NG, C])
        bq4, bk4 = sb("bq4", [128, HG]), sb("bk4", [128, HG])
        bv = sb("bv", [GP + W, C])
        bo, gamma, beta = sb("bo", [KT, C]), sb("gamma", [KT, C]), sb("beta", [KT, C])
        fold16, id16 = sb("fold16", [KT, W], F16), sb("id16", [KT, KT], F16)
        sum_pick = sb("sum_pick", [128, 128])
        partial = sb("partial", [KT, UT * HG, NC])
        neg_max = sb("neg_max", [KT, UT * HG], F16)
        ctx_raw, recip, ctx1, ctx0c = sb("ctx_raw", [128, CH]), sb("recip", [128, CH]), sb("ctx1", [128, CH]), sb("ctx0c", [128, CH])
        ctx0 = sb("ctx0", [128, TOK])
        res_in, res = sb("res_in", [KT, UT, C]), sb("res", [KT, UT, C])
        stat = sb("stat", [KT, 3, UT])
        ps = ctx.enter_context(nc.psum_tensor("l1_ps", [128, 8, 512], F32))
        SB, CB, AB, MB = 0, 4, 5, 7

        loaded, set_up, clear = sem("l1_loaded"), sem("l1_set_up"), sem("clear")
        xc_in, xt_ready = [sem(f"xc{i}_in") for i in range(2)], sem("l1_xt_ready")
        side_ready, side_free = sem("side_ready"), sem("side_free")
        proj_full, proj_half, proj_done, v_done = sem("proj_full"), sem("proj_half"), sem("proj_done"), sem("v_done")
        staged_max, staged_exp = sem("staged_max"), sem("staged_exp")
        win_in, keys_in = [sem(f"win_in{i}") for i in range(2)], [sem(f"keys_in{i}") for i in range(2)]
        score_ready, max_done, neg_ready, row_copied = sem("score_ready"), sem("max_done"), sem("neg_ready"), sem("row_copied")
        exp_ready, exp_done, pv_done = sem("exp_ready"), sem("exp_done"), sem("pv_done")
        ctx_copied, recip_done, ctx_ready = sem("ctx_copied"), sem("recip_done"), sem("ctx_ready")
        res_loaded, mixed_in, out_ready, stored, res_free = (sem("res_loaded"), sem("mixed_in"), sem("out_ready"),
                                                             sem("stored"), sem("res_free"))
        norm_step = sem("norm_step")
        passed = sem("l1_passed")
        block = ctx.enter_context(nc.Block())
        EX = NT * 2
        MX = NT * HG
        PJ = NC * 4
        LOADS = 8 + 16 + 1 + HEADS + 2 + 3 + 2
        K_CTX, K_SUM, K_RECIP, K_MIX, K_NORM = 2, 3, 5, 11, 12
        K_PREP = 14
        PREP = NC * 6
        K_ROWS = 52
        LAG = 2
        AHEAD = NC + 1
        C_PREP = NC - 2
        ahead = lambda k: min(MX, -(-MX * (k + 1) // (K_ROWS - 3)))
        rows = lambda t, n=RP: t.rearrange("p (h e) -> p h e", e=n)

        def number_sides(last):
            place = {}
            for g in range(NG):
                for c in range(NC):
                    final = last and g == NG - 1
                    if c or g:
                        place[g, c, "sum"] = len(place)
                        if g and c:
                            place[g, c, "mix"] = len(place)
                    for k in range(EX):
                        if k == K_ROWS and not (final and c == NC - 1):
                            place[g, c, "rows"] = len(place)
                        if c == C_PREP and k >= K_PREP and not final:
                            place[g, c, k - K_PREP] = len(place)
            place["end", "sum"] = len(place)
            place["end", "mix"] = len(place)
            return place

        FIRST = PREP + 1
        PLACES = {last: number_sides(last) for last in (False, True)}
        SIDES = len(PLACES[False])

        def side(b, last, g, c, what):
            place = PLACES[last]
            if g == "end":
                return FIRST + b * SIDES + place["end", what]
            if isinstance(c, int):
                return FIRST + b * SIDES + place[g, c, what]
            return FIRST + b * SIDES + place[g, 1, what] + (c - 1) * (place[g, 2, what] - place[g, 1, what])

        def images(eng, image):
            with eng.Fori(0, B - 1) as b:
                image(b, False)
            image(B - 1, True)

        def chunks(eng, g, last, step):
            final = last and g == NG - 1
            step(0, None if g == 0 else NC - 1, True, False)
            with eng.Fori(1, C_PREP) as c:
                step(c, c - 1, True, False)
            step(C_PREP, C_PREP - 1, True, not final)
            step(NC - 1, NC - 2, not final, False)

        @block.sync
        def _(sp):
            def load(dst, src):
                sp.dma_start(dst, src).then_inc(loaded, 16)
            sp.wait_ge(set_up, 1)
            load(ctx0c[0:KT, 0:W], a["fold"])
            for k in range(4):
                load(wq4[:, :, k * DK:(k + 1) * DK], a["L1_conv_wq"].rearrange("c (h d) -> c h d", d=DK))
                load(wk4[:, :, k * DK:(k + 1) * DK], a["L1_conv_wk"].rearrange("c (h d) -> c h d", d=DK))
            for dst, src in ((bq4, "L1_conv_bq"), (bk4, "L1_conv_bk")):
                for k in range(8):
                    sp.dma_start(dst[k * DK:(k + 1) * DK, :], a[src].rearrange("(m e d) -> e d m", e=2, d=DK)[k // 4],
                                 allow_slow_non_contiguous=True).then_inc(loaded, 16)
            load(wv[:], a["L1_conv_wv"])
            for g in range(NG):
                for j in range(HG):
                    h = g * HG + j
                    load(wo[32 * j:32 * j + DK, g, :], a["L1_conv_wo"][h * DK:(h + 1) * DK, :])
            for r in range(2):
                load(bv[r * GP:r * GP + W, :], a["L1_conv_bv"].partition_broadcast(W))
            for dst, src in ((bo, "L1_conv_bo"), (gamma, "L1_conv_ln_gamma"), (beta, "L1_conv_ln_beta")):
                load(dst[:], a[src].partition_broadcast(KT))
            load(sum_pick[:], a["sum_pick"])
            sp.wait_ge(clear, 2 * NG)
            with sp.Fori(0, B) as b:
                for g in range(NG):
                    G = b * NG + g
                    with sp.Fori(0, NC) as c:
                        for i in range(UT * HG):
                            u, j = i // HG, i % HG
                            sp.wait_ge(score_ready, ((G * NC + c) * UT * HG + i - 1) * NC + AHEAD)
                            sp.sem_inc(passed, 1)
                            if i < 2:
                                sp.dma_start(key_win[i][DK:DK + KT, :],
                                             scr["by_query"][:, bass.ds((H - QC - c * QC) * RP, STG_Q)]).then_inc(win_in[i], 16)
                                sp.wait_ge(proj_done, (G + 1) * PJ)
                                sp.sem_inc(passed, 1)
                            s0 = (QC - 2 - 2 * u) * RP
                            sp.dma_start(key_win[i % 2][0:DK, s0:s0 + H * RP], ks[g][0:DK, j, :]).then_inc(keys_in[i % 2], 16)

        @block.gpsimd
        def _(pool):
            def piece(t, b, c, r):
                return t[bass.ds(b, 1), bass.ds(c * QC, QC)].rearrange("o (j r) w c -> r (o w) j c", r=2)[r]

            def load_chunk(b, ch):
                for r in range(2):
                    pool.dma_start(xc[ch % 2][r * W:(r + 1) * W, :, :], piece(scr["y"], b, ch, r)).then_inc(xc_in[ch % 2], 16)

            def project(b, G):
                load_chunk(b, 0)
                for ch in range(NC):
                    if ch + 1 < NC:
                        if ch:
                            pool.wait_ge(xt_ready, G * NC + ch)
                            pool.sem_inc(passed, 1)
                        load_chunk(b, ch + 1)
                    for i in range(4):
                        n = G * PJ + ch * 4 + i
                        m = (ch * 4 + i) % 3
                        pool.wait_ge(proj_full, n + 1)
                        pool.sem_inc(passed, 1)
                        nc.gpsimd.tensor_copy(half[m][:], full[m][:]).then_inc(proj_half, 1)
                pool.wait_ge(xt_ready, (G + 1) * NC)
                pool.sem_inc(passed, 1)

            def load_residual(b, c):
                pool.wait_ge(out_ready, HEAD + b * NC + c)
                pool.sem_inc(passed, 1)
                for r in range(2):
                    pool.dma_start(res_in[r * W:(r + 1) * W, :, :], piece(scr["y"], b, c, r)).then_inc(res_loaded, 16)

            def store(b, c):
                n = b * NC + c
                pool.wait_ge(out_ready, HEAD + n + 1)
                pool.sem_inc(passed, 1)
                for r in range(2):
                    pool.dma_start(piece(out, b, c, r), res[r * W:(r + 1) * W, :, :]).then_inc(stored, 16)
                pool.wait_ge(stored, (n + 1) * 32)
                pool.sem_inc(res_free, 1)

            def outputs(b, first, end):
                with pool.Fori(first, end) as c:
                    load_residual(b, c)
                    store(b, c)

            pool.sem_inc(res_free, HEAD)
            with pool.Fori(0, 1) as b:
                project(b, b)

            def image(b, last):
                project(b, b * NG + 1)
                outputs(b, 0, C_PREP - 1)
                load_residual(b, C_PREP - 1)
                if not last:
                    project(b + 1, b * NG + 2)
                store(b, C_PREP - 1)
                outputs(b, C_PREP, NC)
            images(pool, image)

        @block.tensor
        def _(pe):
            def scores(g, k):
                t, pair = k // 2, k % 2
                for e in range(2):
                    j, bank = 2 * pair + e, SB + 2 * pair + e
                    nc.tensor.matmul(ps[0:GP + W, bank, 0:CH], ks[g][:, j, t * 2 * RP:t * 2 * RP + GP + W], q_exp[:, j, :],
                                     start=True, stop=True)
                    for r in range(2):
                        s0 = (H - 1 - 2 * t - r) * W
                        last = nc.tensor.matmul(ps[r * GP:r * GP + W, bank, 0:CH], fold16[:], win_exp[:, s0:s0 + CH],
                                                start=False, stop=True, skip_group_check=True)
                last.then_inc(exp_ready, 1)

            def weigh(g, k):
                t, pair = k // 2, k % 2
                for e in range(2):
                    j = 2 * pair + e
                    v0 = (t * HG + j) * VW
                    last = nc.tensor.matmul(ps[32 * j:32 * j + 32, CB, 0:CH], v[g][:, v0:v0 + 32], p[k % 4][:, e, :],
                                            start=t == 0, stop=t == NT - 1, skip_group_check=True)
                last.then_inc(pv_done, 1)

            def max_scores(m, i):
                tile, kc = i // NC, i % NC
                u, j, place = tile // HG, tile % HG, tile % 2
                if i in (0, NC):
                    pe.wait_ge(win_in[place], (m + 1) * 16)
                if kc == 0:
                    pe.wait_ge(keys_in[place], (m * UT * HG // 2 + tile // 2 + 1) * 16)
                if i >= 2:
                    pe.wait_ge(max_done, m * MX + i - 1)
                s0 = QC * kc - 2 * u + QC - 2
                nc.tensor.matmul(ps[0:KT, AB + i % 2, 0:CH], q_pick[:, j, u * KT:(u + 1) * KT],
                                 rows(key_win[place][:])[:, s0:s0 + QC, 0:W], start=True, stop=True).then_inc(score_ready, 1)

            def turn_rows(m, n):
                pe.wait_ge(neg_ready, m + 1)
                pe.wait_ge(side_free, HEAD + n)
                for j in range(HG):
                    for u in range(UT):
                        last = nc.tensor.matmul(ps[32 * j:32 * j + 1, MB, u * KT:(u + 1) * KT],
                                                neg_max[:, u * HG + j:u * HG + j + 1], id16[:], start=True, stop=True)
                last.then_inc(side_ready, 1)

            def project(G, g, t, n):
                ch, i = t // 6, t % 6
                pe.wait_ge(side_free, HEAD + n)
                if i == 0:
                    in_buffer = (NC + 1 - ch % 2) // 2
                    pe.wait_ge(xc_in[ch % 2], (G * in_buffer + ch // 2 + 1) * 32)
                    for u in range(UT):
                        last = nc.tensor.transpose(ps[:, MB, u * KT:(u + 1) * KT], xc[ch % 2][:, u, :], w["ident"][0:KT, 0:KT])
                    last.then_inc(side_ready, 1)
                elif i < 5:
                    h = g * HG + 2 * ((i - 1) // 2)
                    nc.tensor.matmul(ps[:, MB, 0:CH], (wk4 if i % 2 == 0 else wq4)[:, h:h + 2, :].rearrange("c h k -> c (h k)"),
                                     rows(xT[:])[:, :, 0:W], start=True, stop=True).then_inc(side_ready, 1)
                else:
                    for u in range(UT):
                        last = nc.tensor.matmul(ps[0:GP + W, MB, u * HG * DK:(u + 1) * HG * DK], xT[:, u * 2 * RP:u * 2 * RP + GP + W],
                                                wv[:, g * HG * DK:(g + 1) * HG * DK], start=True, stop=True)
                    last.then_inc(side_ready, 1)

            def spread_sums(n_chunk, n):
                pe.wait_ge(ctx_copied, n_chunk + 1)
                pe.wait_ge(side_free, HEAD + n)
                nc.tensor.matmul(ps[:, MB, 0:CH], sum_pick[:], ctx_raw[:], start=True, stop=True).then_inc(side_ready, 1)

            def mix(n_chunk, n):
                pe.wait_ge(ctx_ready, HEAD + n_chunk + 1)
                pe.wait_ge(side_free, HEAD + n)
                for u in range(UT):
                    for gg, cx in enumerate((ctx0c, ctx1)):
                        last = nc.tensor.matmul(ps[0:KT, MB, u * C:(u + 1) * C], cx[:, u * KT:(u + 1) * KT],
                                                wo[:, gg, :], start=gg == 0, stop=gg == 1)
                last.then_inc(side_ready, 1)

            pe.sem_inc(exp_ready, HEAD)
            pe.sem_inc(score_ready, AHEAD)
            pe.sem_inc(pv_done, 4)
            pe.wait_ge(set_up, 2)
            with pe.Fori(0, 1) as z:
                for t in range(PREP):
                    project(z, 0, t, z + t)
                pe.wait_ge(proj_done, PJ)
                pe.wait_ge(staged_max, 2)
                for i in range(MX):
                    max_scores(z, i)
                turn_rows(z, z + PREP)

            def image(b, last):
                for g in range(NG):
                    G = b * NG + g

                    def step(c, before, maxima, projections):
                        n = G * NC + c
                        m = n + 1
                        gm = g if not (isinstance(c, int) and c == NC - 1) else 1 - g
                        for k in range(EX):
                            pe.wait_ge(exp_done, 2 + n * EX + k - 1)
                            if k < 2 and before is not None:
                                weigh(g if not (isinstance(c, int) and c == 0) else 1 - g, EX - 2 + k)
                            if k == 0:
                                pe.wait_ge(staged_exp, HEAD + (n + 1) * 2)
                            scores(g, k)
                            if k >= 2:
                                if k == 2 and before is not None:
                                    pe.wait_ge(ctx_copied, n)
                                weigh(g, k - 2)
                            if k == K_SUM and before is not None:
                                spread_sums(n - 1, side(b, last, g, c, "sum"))
                            if k == K_MIX and before is not None and g and not (isinstance(c, int) and c == 0):
                                mix(n - 1, side(b, last, g, c, "mix"))
                            if maxima:
                                if k == 0:
                                    pe.wait_ge(staged_max, (m + 1) * 2)
                                    pe.wait_ge(proj_done, (G + 1 + (gm != g)) * PJ)
                                for i in range(ahead(k - 1) if k else 0, ahead(k)):
                                    max_scores(m, i)
                                if k == K_ROWS:
                                    turn_rows(m, side(b, last, g, c, "rows"))
                            if projections and k >= K_PREP:
                                project(G + 1, 1 - g, k - K_PREP, side(b, last, g, c, k - K_PREP))

                    if g:
                        pe.wait_ge(v_done, (G + 1) * NC)
                    else:
                        pe.wait_ge(v_done, (G + 1) * NC)
                    chunks(pe, g, last, step)
                n = b * NG * NC + NG * NC - 1
                for k in range(2):
                    pe.wait_ge(exp_done, 2 + n * EX + EX - 1 + k)
                    weigh(1, EX - 2 + k)
                spread_sums(n, side(b, last, "end", 0, "sum"))
                mix(n, side(b, last, "end", 0, "mix"))
            images(pe, image)

        @block.scalar
        def _(act):
            def project(G, g, t, n):
                ch, i = t // 6, t % 6
                if i == 0:
                    act.wait_ge(side_ready, n + 1)
                    nc.scalar.copy(rows(xT[:])[:, :, 0:W], rows(ps[:, MB, 0:CH], W)).then_inc(side_free, 1)
                    act.wait_ge(side_free, HEAD + n + 1)
                    act.sem_inc(xt_ready, 1)
                elif i < 5:
                    pn = ch * 4 + i - 1
                    is_k, m = i % 2 == 0, g * 2 + (i - 1) // 2
                    act.wait_ge(side_ready, n + 1)
                    if pn >= 3:
                        act.wait_ge(proj_done, G * PJ + pn - 2)
                    nc.scalar.activation(full[pn % 3][:], ps[:, MB, 0:CH], ACT.Identity,
                                         bias=(bk4 if is_k else bq4)[:, m:m + 1],
                                         scale=1.0 if is_k else DK ** -0.5).then_inc(proj_full, 1)
                    act.wait_ge(proj_full, G * PJ + pn + 1)
                    act.sem_inc(side_free, 1)

            def copy_rows(n):
                act.wait_ge(side_ready, n + 1)
                for j in (2, 3):
                    nc.scalar.copy(q_max[STK:STK + 1, j, :], ps[32 * j:32 * j + 1, MB, 0:CH]).then_inc(row_copied, 1)

            def copy_context(n):
                act.wait_ge(pv_done, 4 + (n + 1) * EX)
                act.wait_ge(ctx_ready, HEAD + n)
                nc.scalar.copy(ctx_raw[:], ps[:, CB, 0:CH]).then_inc(ctx_copied, 1)

            act.sem_inc(exp_done, 2)
            act.sem_inc(side_free, HEAD)
            act.wait_ge(set_up, 2)
            with act.Fori(0, 1) as z:
                for t in range(PREP):
                    project(z, 0, t, z + t)
                copy_rows(z + PREP)

            def image(b, last):
                for g in range(NG):
                    G = b * NG + g

                    def step(c, before, maxima, projections):
                        n = G * NC + c
                        for k in range(EX):
                            if k == K_CTX and before is not None:
                                copy_context(n - 1)
                            act.wait_ge(pv_done, 4 + n * EX + k - 3)
                            act.wait_ge(exp_ready, HEAD + n * EX + k + 1)
                            bank = SB + 2 * (k % 2)
                            nc.scalar.activation(p[k % 4][:], ps[0:GP + W, bank:bank + 2, 0:CH], ACT.Exp).then_inc(exp_done, 1)
                            if maxima and k == K_ROWS:
                                copy_rows(side(b, last, g, c, "rows"))
                            if projections and k >= K_PREP:
                                project(G + 1, 1 - g, k - K_PREP, side(b, last, g, c, k - K_PREP))
                    chunks(act, g, last, step)
                copy_context(b * NG * NC + NG * NC - 1)
            images(act, image)

        @block.vector
        def _(dve):
            for head in (ctx_ready, mixed_in, staged_exp, out_ready):
                dve.sem_inc(head, HEAD)
            nc.vector.memset(wo[:], 0.0)
            nc.vector.memset(bv[:], 0.0).then_inc(set_up, 1)
            for t in (*ks, *v):
                nc.vector.memset(t[:], 0.0).then_inc(clear, 1)
            nc.vector.memset(xT[:], 0.0)
            nc.vector.memset(qs[STK:STK + 1, :, :], 0.0)
            dve.wait_ge(clear, 2 * NG)
            for g in range(NG):
                for j in range(HG):
                    nc.vector.memset(rows(ks[g][STK:STK + 1, j, :])[:, :, 0:W], 1.0)
                for r in range(2):
                    nc.vector.memset(v[g][r * GP:r * GP + W, 0:NT * HG * VW].rearrange("p (t d) -> p t d", d=VW)[:, :, DK:VW], 1.0)
            dve.wait_ge(loaded, 16 * LOADS)
            nc.vector.tensor_copy(fold16[:], ctx0c[0:KT, 0:W])
            nc.vector.tensor_copy(id16[:], w["ident"][0:KT, 0:KT])
            nc.vector.tensor_copy(q_pick[:].rearrange("p h (u q) -> p (h u) q", q=KT),
                                  w["ident"][:, DK:DK + KT].unsqueeze(1).broadcast_to([128, HG * UT, KT]))
            nc.vector.tensor_scalar(bq4[:], bq4[:], DK ** -0.5, None, ALU.mult).then_inc(set_up, 1)
            dve.wait_ge(set_up, 2)

            def split(G, g, t):
                ch, i = t // 6, t % 6
                if 1 <= i < 5:
                    pn = ch * 4 + i - 1
                    is_k, m = i % 2 == 0, (i - 1) // 2
                    dve.wait_ge(proj_half, G * PJ + pn + 1)
                    for e in range(2):
                        part = slice(STK * e, STK * e + STK)
                        dst = (rows(ks[g][0:STK, 2 * m + e, :])[:, ch * QC:(ch + 1) * QC, 0:W] if is_k
                               else rows(qs[0:STK, 2 * m + e, :], W)[:, ch * QC:(ch + 1) * QC, :])
                        last = nc.vector.scalar_tensor_tensor(dst, rows(half[pn % 3][part, :], W),
                                                              w["flags"][part, 0:1] if is_k else w["flags"][part, 1:2],
                                                              rows(full[pn % 3][part, :], W), ALU.mult, ALU.add)
                    last.then_inc(proj_done, 1)

            def add_values(g, t, n):
                ch, i = t // 6, t % 6
                if i == 5:
                    dve.wait_ge(side_ready, n + 1)
                    nc.vector.tensor_tensor(
                        v[g][:, 0:NT * HG * VW].rearrange("p (t h d) -> p t h d", h=HG, d=VW)[:, ch * UT:(ch + 1) * UT, :, 0:DK],
                        ps[0:GP + W, MB, 0:UT * HG * DK].rearrange("p (t h d) -> p t h d", h=HG, d=DK),
                        bv[:, g * HG * DK:(g + 1) * HG * DK].rearrange("p (h d) -> p h d", d=DK).unsqueeze(1).broadcast_to([GP + W, UT, HG, DK]),
                        ALU.add).then_inc(v_done, 1)

            def stage_max(m, c):
                dve.wait_ge(staged_exp, HEAD + m * 2)
                nc.vector.tensor_copy(q_max[:], qs[:, :, bass.ds(c * CH, CH)]).then_inc(staged_max, 1)
                nc.vector.tensor_copy(q_pick[0:DK], qs[0:DK, :, bass.ds(c * CH, CH)]).then_inc(staged_max, 1)

            def find_max(i, base):
                tile, kc = i // NC, i % NC
                dve.wait_ge(score_ready, AHEAD + base + i + 1)
                nc.vector.tensor_reduce(partial[:, tile, kc:kc + 1], ps[0:KT, AB + i % 2, 0:CH], AX.X,
                                        ALU.max).then_inc(max_done, 1)

            def join_max(m):
                dve.wait_ge(max_done, (m + 1) * MX)
                nc.vector.tensor_reduce(neg_max[:], partial[:], AX.X, ALU.max, negate=True).then_inc(neg_ready, 1)

            def copy_rows(m, n):
                dve.wait_ge(side_ready, n + 1)
                dve.wait_ge(staged_max, (m + 1) * 2)
                for j in (0, 1):
                    nc.vector.tensor_copy(q_max[STK:STK + 1, j, :], ps[32 * j:32 * j + 1, MB, 0:CH]).then_inc(row_copied, 1)
                dve.wait_ge(row_copied, (m + 1) * HG)
                dve.sem_inc(side_free, 1)

            def invert(piece, n_chunk, n):
                cut = slice(piece * KT, (piece + 1) * KT)
                if piece == 0:
                    dve.wait_ge(ctx_ready, HEAD + n_chunk)
                dve.wait_ge(side_ready, n + 1)
                nc.vector.reciprocal(recip[:, cut], ps[:, MB, cut]).then_inc(recip_done, 1)

            def normalise_context(g, c, n_chunk):
                dve.wait_ge(recip_done, (n_chunk + 1) * UT)
                dve.sem_inc(side_free, 1)
                if g == 0:
                    nc.vector.tensor_tensor(ctx0[:, bass.ds(c * CH, CH)], ctx_raw[:], recip[:], ALU.mult).then_inc(ctx_ready, 1)
                else:
                    nc.vector.tensor_copy(ctx0c[:], ctx0[:, bass.ds(c * CH, CH)])
                    nc.vector.tensor_tensor(ctx1[:], ctx_raw[:], recip[:], ALU.mult).then_inc(ctx_ready, 1)

            def norm(n, n_side):
                done = 0

                def link(ins):
                    nonlocal done
                    done += 1
                    ins.then_inc(norm_step, 1)
                    return done

                spread = lambda t: t.unsqueeze(2).broadcast_to([KT, UT, C])
                each = lambda t: t[:].unsqueeze(1).broadcast_to([KT, UT, C])
                after = lambda: dve.wait_ge(norm_step, n * LINKS + done)
                dve.wait_ge(side_ready, n_side + 1)
                dve.wait_ge(res_loaded, (n + 1) * 32)
                dve.wait_ge(res_free, HEAD + n)
                nc.vector.tensor_tensor(res[:], ps[0:KT, MB, :].rearrange("p (u c) -> p u c", c=C),
                                        res_in[:], ALU.add).then_inc(mixed_in, 1)
                yield
                dve.wait_ge(mixed_in, HEAD + n + 1)
                dve.sem_inc(side_free, 1)
                link(nc.vector.tensor_tensor(res[:], res[:], each(bo), ALU.add))
                yield
                after()
                link(nc.vector.tensor_reduce(stat[:, 0, :], res[:], AX.X, ALU.add))
                yield
                after()
                link(nc.vector.tensor_scalar(stat[:, 0, :], stat[:, 0, :], 1.0 / C, None, ALU.mult))
                yield
                after()
                link(nc.vector.tensor_tensor(res[:], res[:], spread(stat[:, 0, :]), ALU.subtract))
                yield
                after()
                link(nc.vector.tensor_tensor(res_in[:], res[:], res[:], ALU.mult))
                yield
                after()
                link(nc.vector.tensor_reduce(stat[:, 1, :], res_in[:], AX.X, ALU.add))
                yield
                after()
                var, y, t = stat[:, 2, :], stat[:, 0, :], stat[:, 1, :]
                link(nc.vector.tensor_scalar(var, stat[:, 1, :], 1.0 / C, LN_EPS, ALU.mult, ALU.add))
                yield
                after()
                link(nc.vector.tensor_scalar(y.bitcast(I32), var.bitcast(I32), 1, None, ALU.logical_shift_right))
                yield
                after()
                link(nc.vector.tensor_scalar(y.bitcast(I32), y.bitcast(I32), -1, RSQRT_GUESS, ALU.mult, ALU.add))
                yield
                for _ in range(NEWTON):
                    after()
                    link(nc.vector.tensor_tensor(t, y, y, ALU.mult))
                    yield
                    after()
                    link(nc.vector.tensor_tensor(t, t, var, ALU.mult))
                    yield
                    after()
                    link(nc.vector.tensor_scalar(t, t, -0.5, 1.5, ALU.mult, ALU.add))
                    yield
                    after()
                    link(nc.vector.tensor_tensor(y, y, t, ALU.mult))
                    yield
                after()
                link(nc.vector.tensor_tensor(res[:], res[:], spread(y), ALU.mult))
                yield
                after()
                link(nc.vector.tensor_tensor(res_in[:], res[:], each(gamma), ALU.mult))
                yield
                after()
                assert done == LINKS
                nc.vector.tensor_tensor(res[:], res_in[:], each(beta), ALU.add).then_inc(out_ready, 1)
                yield

            with dve.Fori(0, 1) as z:
                for t in range(PREP):
                    add_values(0, t, z + t)
                    if t % 6 == 5:
                        dve.wait_ge(v_done, z + t // 6 + 1)
                        dve.sem_inc(side_free, 1)
                    if t >= LAG:
                        split(z, 0, t - LAG)
                for t in range(PREP - LAG, PREP):
                    split(z, 0, t)
                dve.wait_ge(proj_done, PJ)
                stage_max(z, z)
                for i in range(MX):
                    find_max(i, z)
                join_max(z)
                copy_rows(z, z + PREP)

            def image(b, last):
                for g in range(NG):
                    G = b * NG + g

                    def step(c, before, maxima, projections):
                        n = G * NC + c
                        m = n + 1
                        cross = isinstance(c, int) and c == 0
                        g_before = 1 - g if cross else g
                        dve.wait_ge(exp_ready, HEAD + n * EX)
                        dve.wait_ge(row_copied, (n + 1) * HG)
                        nc.vector.tensor_copy(q_exp[:], q_max[:]).then_inc(staged_exp, 1)
                        nc.vector.tensor_copy(win_exp[:], w["by_key"][:, bass.ds(c * QC * W, STG_K)]).then_inc(staged_exp, 1)
                        if maxima:
                            if isinstance(c, int) and c == NC - 1:
                                dve.wait_ge(proj_done, (G + 2) * PJ)
                                stage_max(m, b * 0)
                            else:
                                stage_max(m, c + 1)
                        finish = norm(b * NC + before, side(b, last, g, c, "mix")) if before is not None and g_before else None
                        for k in range(EX):
                            if maxima:
                                for i in range(ahead(k - 1) if k else 0, ahead(k)):
                                    find_max(i, m * MX)
                                if k == K_ROWS - 3:
                                    join_max(m)
                                if k == K_ROWS:
                                    copy_rows(m, side(b, last, g, c, "rows"))
                            if before is not None:
                                if K_RECIP <= k < K_RECIP + UT:
                                    invert(k - K_RECIP, n - 1, side(b, last, g, c, "sum"))
                                if k == K_RECIP + UT:
                                    normalise_context(g_before, before, n - 1)
                                if finish and k >= K_NORM:
                                    next(finish, None)
                            if projections and k >= K_PREP:
                                t = k - K_PREP
                                n_side = side(b, last, g, c, t)
                                add_values(1 - g, t, n_side)
                                if t % 6 == 5:
                                    dve.wait_ge(v_done, (G + 1) * NC + t // 6 + 1)
                                    dve.sem_inc(side_free, 1)
                                if t >= LAG:
                                    split(G + 1, 1 - g, t - LAG)
                        if projections:
                            for t in range(PREP - LAG, PREP):
                                split(G + 1, 1 - g, t)
                    chunks(dve, g, last, step)
                n = b * NG * NC + NG * NC - 1
                for piece in range(UT):
                    invert(piece, n, side(b, last, "end", 0, "sum"))
                normalise_context(1, b * 0 + NC - 1, n)
                for _ in norm(b * NC + NC - 1, side(b, last, "end", 0, "mix")):
                    pass
            images(dve, image)


def two_layers(nc, a, out):
    h1 = nc.dram_tensor("h1_scratch", [B, H, W, C], F32, kind="Internal").ap()
    w1 = nc.dram_tensor("w1_scratch", [B, H, W, C], F32, kind="Internal").ap()
    y = nc.dram_tensor("y_scratch", [B, H, W, C], F32, kind="Internal").ap()
    rew = nc.dram_tensor("rew_scratch", [2 * B, H, C], F32, kind="Internal").ap()
    dist = nc.dram_tensor("dist_scratch", [DIAG, DIAG], F32, kind="Internal").ap()
    by_query = nc.dram_tensor("by_query_scratch", [KT, (DIAG - 1) * RP], F16, kind="Internal").ap()
    scr = {"h1": h1, "w1": w1, "y": y, "rew": rew, "dist": dist, "by_query": by_query}
    with ExitStack() as whole:
        keep = lambda c, n, s, d=F32: c.enter_context(nc.sbuf_tensor(n, s, d))
        w = {"ident": keep(whole, "ident_sb", [128, 128]), "flags": keep(whole, "flags_sb", [128, 4])}
        with ExitStack() as first:
            w["G"] = [keep(first, f"G{r}", [KT, NK, DIM]) for r in range(2)]
            w["dft_e"], w["dft_o"] = keep(first, "dft_e", [KR, NK, HALF]), keep(first, "dft_o", [KR, NK, HALF])
            w["chan_t"] = keep(first, "chan_t", [C, 3, C])
            w["par"], w["thr"] = keep(first, "par", [KT, 2, HALF]), keep(first, "thr", [KT, 2, HALF])
            w["Y"] = keep(first, "Y", [KT, NK, GROUPS * GP])
            prepare_layer0(nc, a, w)
            layer0(nc, a, w, scr)
        w["by_key"] = keep(whole, "by_key", [KT, WIN], F16)
        prepare_windows(nc, a, w, scr)
        layer1(nc, a, w, scr, out)


_INS = ["x", "L0_conv_mlp_h1_w", "L0_conv_mlp_w1_w", "L0_conv_mlp_c_w", "L0_conv_reweight_h_w", "L0_conv_reweight_w_w",
        "L0_conv_param_h", "L0_conv_param_w", "L1_conv_wq", "L1_conv_bq", "L1_conv_wk", "L1_conv_bk", "L1_conv_wv",
        "L1_conv_bv", "L1_conv_wo", "L1_conv_bo", "L1_conv_ln_gamma", "L1_conv_ln_beta", "L1_conv_spatial_bias"]


def kernel(**inputs):
    import numpy as _np
    import concourse.bacc as _bacc
    from concourse import mybir as _mybir
    from concourse.bass_utils import run_bass_kernel_spmd as _run

    nc = _bacc.Bacc("TRN2", target_bir_lowering=False, num_devices=1)
    arrays, args = {}, {}
    given = {n: _np.ascontiguousarray(inputs[n]) for n in _INS}
    given.update(constants())
    for name, a in given.items():
        arrays[f"in_{name}"] = a
        args[name] = nc.dram_tensor(f"in_{name}", a.shape, _mybir.dt.from_np(a.dtype), kind="ExternalInput").ap()
    out = nc.dram_tensor("out_0", (B, H, W, C), _mybir.dt.from_np(_np.dtype("float32")), kind="ExternalOutput").ap()
    two_layers(nc, args, out)
    r = _run(nc, [arrays], core_ids=[0])
    return r.results[0]["out_0"]
```

```python
from contextlib import ExitStack

import concourse.bass as bass
import numpy as np
from concourse import mybir

ALU = mybir.AluOpType
ACT = mybir.ActivationFunctionType
AX = mybir.AxisListType
F32 = mybir.dt.float32
F16 = mybir.dt.float16
I32 = mybir.dt.int32

B, H, W, C = 8, 56, 56, 128
GROUPS, S = 8, 16
DIM = H * S
HALF = DIM // 2
Q = HALF // 2
KT = 112
NK = HALF // KT
GP = 64
KR = GP + H
OT = DIM // 128
DIAG = 2 * W - 1
HEADS, DK = 8, 16
HG = 4
NG = HEADS // HG
TOK = H * W
NT = H // 2
QC = 8
CH = QC * W
NC = H // QC
UT = QC // 2
RP = 64
STK = 4 * DK
WIN = DIAG * W
STG_K = (H + QC - 1) * W
STG_Q = (H + QC - 2) * RP
DIST = 59
LN_EPS = 1e-5
HEAD = 1
RSQRT_GUESS = 0x5F3759DF
NEWTON = 4
LINKS = 11 + 4 * NEWTON


def constants():
    j = np.arange(Q)
    m = np.arange(HALF)[:, None]
    even = 2 * np.pi * ((2 * m * j) % DIM) / DIM
    odd = 2 * np.pi * (((2 * m + 1) * j) % DIM) / DIM
    e = np.concatenate([np.cos(even), -np.sin(even)], axis=1)
    o = np.concatenate([np.cos(odd), -np.sin(odd)], axis=1)
    e[:, Q] = 1.0 - 2.0 * (np.arange(HALF) % 2)
    o[:, Q] = 0.0
    inv = np.concatenate([np.cos(even), -np.sin(even)], axis=1) * 2.0 / DIM
    inv[:, 0] = 1.0 / DIM
    inv[:, Q] = (1.0 - 2.0 * (np.arange(HALF) % 2)) * 2.0 / DIM
    p = np.arange(128)
    flags = np.zeros((128, 4))
    flags[:, 0] = -1.0 * (p % 32 >= DK)
    flags[:, 1] = -1.0 * (p % STK >= 2 * DK)
    flags[:, 2] = -1.0 * (p >= W)
    flags[:, 3] = 1.0 * (p != 0)
    ident = np.eye(128)
    fold = (p[:KT, None] % W == np.arange(W)[None, :]) * 1.0
    sums = (p[:, None] % 32 == DK) * (p[:, None] // 32 == p[None, :] // 32) * 1.0
    s = np.abs(np.arange(DIAG) - (W - 1))
    dist = np.minimum(s[:, None] + s[None, :], DIST - 1).reshape(-1)
    pick = (np.arange(DIST)[:, None] == dist[None, :]) * 1.0
    mirror = np.eye(W)[:, ::-1]
    none = np.zeros((W, W))
    flips = np.stack([np.hstack([mirror, mirror]), np.hstack([mirror, none]), np.hstack([none, mirror])], axis=1)
    f = lambda a: np.ascontiguousarray(a, dtype=np.float32)
    return {"dft_even": f(e), "dft_odd": f(o), "inv_t": f(inv), "flags": f(flags), "ident": f(ident),
            "fold": f(fold), "sum_pick": f(sums), "dist_pick": f(pick), "flips": f(flips)}


def prepare_layer0(nc, a, w):
    with ExitStack() as ctx:
        sb = lambda n, s, d=F32: ctx.enter_context(nc.sbuf_tensor(n, s, d))
        sem = lambda n: ctx.enter_context(nc.semaphore(n))
        mlp = [sb(f"mlp{r}", [128, OT, HALF]) for r in range(2)]
        mlp_t = sb("mlp_t", [KT, NK, DIM])
        inv = sb("inv", [KT, NK, HALF])
        small = sb("small", [128, 3, 128])
        ps = ctx.enter_context(nc.psum_tensor("prep_ps", [128, 8, 512], F32))
        loaded, cleared = sem("prep_loaded"), sem("prep_cleared")
        tr_ready, tr_copied = sem("prep_tr_ready"), sem("prep_tr_copied")
        g_ready, g_copied = sem("prep_g_ready"), sem("prep_g_copied")
        small_ready, small_copied = sem("prep_small_ready"), sem("prep_small_copied")
        block = ctx.enter_context(nc.Block())

        @block.sync
        def _(sp):
            sp.dma_start(w["ident"][:], a["ident"]).then_inc(loaded, 16)
            sp.dma_start(w["flags"][:], a["flags"]).then_inc(loaded, 16)
            sp.dma_start(mlp[0][:], a["L0_conv_mlp_h1_w"].rearrange("(t p) m -> p t m", p=128)).then_inc(loaded, 16)
            sp.dma_start(inv[:], a["inv_t"].rearrange("(t p) m -> p t m", p=KT)).then_inc(loaded, 16)
            sp.dma_start(mlp[1][:], a["L0_conv_mlp_w1_w"].rearrange("(t p) m -> p t m", p=128)).then_inc(loaded, 16)
            for i, n in enumerate(("L0_conv_mlp_c_w", "L0_conv_reweight_h_w", "L0_conv_reweight_w_w")):
                sp.dma_start(small[:, i, :], a[n]).then_inc(loaded, 16)
            sp.wait_ge(cleared, 2)
            for dst, src in (("dft_e", "dft_even"), ("dft_o", "dft_odd")):
                for e in range(2):
                    sp.dma_start(w[dst][GP * e:GP * e + H, :, :],
                                 a[src].rearrange("(h k e) j -> e h k j", k=NK, e=2)[e]).then_inc(loaded, 16)
            sp.dma_start(w["par"][:, 0, :], a["L0_conv_param_h"].partition_broadcast(KT)).then_inc(loaded, 16)
            sp.dma_start(w["par"][:, 1, :], a["L0_conv_param_w"].partition_broadcast(KT)).then_inc(loaded, 16)
            sp.wait_ge(loaded, 16 * 14)

        @block.tensor
        def _(pe):
            pe.wait_ge(loaded, 16 * 14)
            for i in range(3):
                last = nc.tensor.transpose(ps[:, 7, 128 * i:128 * i + 128], small[:, i, :], w["ident"][:])
            last.then_inc(small_ready, 1)
            n = 0
            for r in range(2):
                if r:
                    pe.wait_ge(g_copied, 2 * NK)
                for mt in range(NK):
                    for part in range(2):
                        tiles = range(0, 4) if part == 0 else range(4, OT)
                        if n >= 2:
                            pe.wait_ge(tr_copied, n - 1)
                        for t in tiles:
                            last = nc.tensor.transpose(ps[0:KT, n % 2, 128 * (t % 4):128 * (t % 4) + 128],
                                                       mlp[r][:, t, mt * KT:(mt + 1) * KT], w["ident"][:])
                        last.then_inc(tr_ready, 1)
                        n += 1
                pe.wait_ge(tr_copied, n)
                for ct in range(NK):
                    for hf in range(2):
                        k = r * 2 * NK + ct * 2 + hf
                        if k >= 2:
                            pe.wait_ge(g_copied, k - 1)
                        for mt in range(NK):
                            last = nc.tensor.matmul(ps[0:KT, 2 + k % 2, 0:HALF], inv[:, mt, ct * KT:(ct + 1) * KT],
                                                    mlp_t[:, mt, hf * HALF:(hf + 1) * HALF],
                                                    start=mt == 0, stop=mt == NK - 1)
                        last.then_inc(g_ready, 1)

        @block.scalar
        def _(act):
            act.wait_ge(small_ready, 1)
            nc.scalar.copy(w["chan_t"][:].rearrange("p i c -> p (i c)"), ps[:, 7, 0:384]).then_inc(small_copied, 1)
            for k in range(4 * NK):
                r, ct, hf = k // (2 * NK), k // 2 % NK, k % 2
                act.wait_ge(g_ready, k + 1)
                nc.scalar.copy(w["G"][r][:, ct, hf * HALF:(hf + 1) * HALF], ps[0:KT, 2 + k % 2, 0:HALF]).then_inc(g_copied, 1)

        @block.vector
        def _(dve):
            for t in ("dft_e", "dft_o"):
                nc.vector.memset(w[t][:], 0.0).then_inc(cleared, 1)
            dve.wait_ge(loaded, 16 * 14)
            nc.vector.scalar_tensor_tensor(w["thr"][:, 0, :], w["par"][:, 0, :], 0.0, w["par"][:, 0, :], ALU.max, ALU.mult)
            nc.vector.scalar_tensor_tensor(w["thr"][:, 1, :].rearrange("p (g h) -> p h g", g=GROUPS),
                                           w["par"][:, 1, :].rearrange("p (h g) -> p h g", g=GROUPS), 0.0,
                                           w["par"][:, 1, :].rearrange("p (h g) -> p h g", g=GROUPS), ALU.max, ALU.mult)
            nc.vector.memset(w["Y"][:], 0.0)
            for n in range(4 * NK):
                r, mt, part = n // (2 * NK), n // 2 % NK, n % 2
                if n == 2 * NK:
                    dve.wait_ge(g_copied, 2 * NK)
                dve.wait_ge(tr_ready, n + 1)
                width = 512 if part == 0 else DIM - 512
                nc.vector.tensor_copy(mlp_t[:, mt, 512 * part:512 * part + width], ps[0:KT, n % 2, 0:width]).then_inc(tr_copied, 1)


def layer0(nc, a, w, scr):
    PARTS = 4
    PT = NT // PARTS
    with ExitStack() as ctx:
        sb = lambda n, s, d=F32: ctx.enter_context(nc.sbuf_tensor(n, s, d))
        sem = lambda n: ctx.enter_context(nc.semaphore(n))
        x = [sb(f"x{r}", [H, H * C]) for r in range(2)]
        zt = [sb(f"zt{i}", [KR, NK, HALF]) for i in range(2)]
        odd_re, odd_im = sb("odd_re", [KT, HALF]), sb("odd_im", [KT, HALF])
        hi_re, hi_im = sb("hi_re", [KT, HALF]), sb("hi_im", [KT, HALF])
        lo_re, lo_im = sb("lo_re", [KT, HALF]), sb("lo_im", [KT, HALF])
        sq_re, sq_im = sb("sq_re", [KT, HALF]), sb("sq_im", [KT, HALF])
        mask = sb("mask", [KT, HALF])
        mean, mean_t, rew = sb("mean", [H, 2, C]), sb("mean_t", [C, 2, H]), sb("rew", [H, 2, C])
        mh = [sb(f"mh{i}", [KT, PT, C]) for i in range(2)]
        mw = [sb(f"mw{i}", [KT, PT, C]) for i in range(2)]
        mx = [sb(f"mx{i}", [KT, PT, C]) for i in range(2)]
        mb = [sb(f"mb{i}", [KT, PT, C]) for i in range(2)]
        ma = [sb(f"ma{i}", [KT, C]) for i in range(2)]
        xt = [sb(f"xt{i}", [C, PT, KT]) for i in range(2)]
        ps = ctx.enter_context(nc.psum_tensor("l0_ps", [128, 8, 512], F32))
        TB, FB, IB = 0, 2, 6
        x_in, x_out = [sem(f"x{r}_in") for r in range(2)], sem("x_out")
        tr_ready = sem("tr_ready")
        zt_act, zt_dve = sem("zt_act"), sem("zt_dve")
        odd_ready, even_ready = sem("odd_ready"), sem("even_ready")
        odd_copied = sem("odd_copied")
        high_ready, squared, masked = sem("high_ready"), sem("squared"), sem("masked")
        y_ready = sem("y_ready")
        inv_ready = sem("inv_ready")
        added, mean_ready, mean_tr, mean_copied = sem("added"), sem("mean_ready"), sem("mean_tr"), sem("mean_copied")
        rew_ready, rew_copied, rew_out = sem("rew_ready"), sem("rew_copied"), sem("rew_out")
        mix_in, mix_out = [sem(f"mix_in{i}") for i in range(2)], sem("mix_out")
        xt_ready, xt_copied, chan_ready = sem("xt_ready"), sem("xt_copied"), sem("chan_ready")
        gap_clear = sem("gap_clear")
        passed = sem("passed")
        pool_step, dve_step, mixed = sem("pool_step"), sem("dve_step"), sem("mixed")
        block = ctx.enter_context(nc.Block())
        NT2 = S // 2
        NI = GROUPS

        xh = a["x"].rearrange("b h w c -> b w h c")
        oh = scr["h1"].rearrange("b h w c -> b w h c")
        tiles = lambda t: t.rearrange("b (j r) w c -> b r w j c", r=2)

        def images(eng, image):
            with eng.Fori(0, 1) as b:
                image(b, None, True)
            with eng.Fori(1, B - 1) as b:
                image(b, b - 1, True)
            with eng.Fori(B - 1, B) as b:
                image(b, b - 1, False)

        @block.sync
        def _(sp):
            def load_image(b, r):
                sp.dma_start(x[r][:].rearrange("p (t c) -> p t c", c=C),
                             (a["x"] if r else xh)[bass.ds(b, 1)].rearrange("o p t c -> (o p) t c")).then_inc(x_in[r], 16)

            def load_tokens(b, p):
                for src, dst in ((scr["h1"], mh[p % 2]), (scr["w1"], mw[p % 2]), (a["x"], mx[p % 2])):
                    for rr in range(2):
                        v = tiles(src)[bass.ds(b, 1), rr, :, p * PT:(p + 1) * PT, :]
                        sp.dma_start(dst[rr * W:(rr + 1) * W, :, :], v.rearrange("o w j c -> (o w) j c")).then_inc(mix_in[p % 2], 16)

            def load_means(b, p):
                for rr in range(2):
                    sp.dma_start(ma[p % 2][rr * W:(rr + 1) * W, :],
                                 scr["rew"][bass.ds(b * 2, 1)].rearrange("o p c -> (o p) c")).then_inc(mix_in[p % 2], 16)
                    hv = scr["rew"][bass.ds(b * 2 + 1, 1)].rearrange("o (j r) c -> r o j c", r=2)[rr, :, p * PT:(p + 1) * PT, :]
                    sp.dma_start(mb[p % 2][rr * W:(rr + 1) * W, :, :], hv.broadcast_to([W, PT, C])).then_inc(mix_in[p % 2], 16)

            def store_branch(b, r):
                sp.wait_ge(added, HEAD + (b * 2 + r + 1) * NI * 2)
                sp.sem_inc(passed, 1)
                sp.dma_start((scr["w1"] if r else oh)[bass.ds(b, 1)].rearrange("o p t c -> (o p) t c"),
                             x[r][:].rearrange("p (t c) -> p t c", c=C)).then_inc(x_out, 16)
                sp.wait_ge(x_out, (b * 2 + r + 1) * 16)
                sp.sem_inc(passed, 1)

            def store_means(b):
                for r in range(2):
                    sp.wait_ge(rew_copied, b * 2 + r + 1)
                    sp.sem_inc(passed, 1)
                    sp.dma_start(scr["rew"][bass.ds(b * 2 + r, 1)].rearrange("o p c -> (o p) c"), rew[:, r, :]).then_inc(rew_out, 16)
                sp.wait_ge(rew_out, (b * 2 + 2) * 16)
                sp.sem_inc(passed, 1)
                for p in range(2):
                    load_means(b, p)

            def store_mix(b, p):
                n = b * PARTS + p
                sp.wait_ge(mixed, HEAD + n + 1)
                sp.sem_inc(passed, 1)
                for rr in range(2):
                    v = tiles(scr["y"])[bass.ds(b, 1), rr, :, p * PT:(p + 1) * PT, :]
                    sp.dma_start(v.rearrange("o w j c -> (o w) j c"), mh[p % 2][rr * W:(rr + 1) * W, :, :]).then_inc(mix_out, 16)
                sp.wait_ge(mix_out, (n + 1) * 32)
                sp.sem_inc(passed, 1)
                if p + 2 < PARTS:
                    load_tokens(b, p + 2)
                    load_means(b, p + 2)

            def image(b, before, more):
                if before is None:
                    for r in range(2):
                        load_image(b, r)
                else:
                    store_means(before)
                    sp.wait_ge(mean_ready, before * 2 + 2)
                    sp.sem_inc(passed, 1)
                    load_image(b, 1)
                store_branch(b, 0)
                if before is not None:
                    for p in range(2):
                        store_mix(before, p)
                if more:
                    sp.wait_ge(mean_ready, b * 2 + 1)
                    sp.sem_inc(passed, 1)
                    load_image(b + 1, 0)
                store_branch(b, 1)
                if before is not None:
                    for p in range(2, PARTS):
                        store_mix(before, p)
                for p in range(2):
                    load_tokens(b, p)

            images(sp, image)
            with sp.Fori(B - 1, B) as b:
                store_means(b)
                for p in range(PARTS):
                    store_mix(b, p)

        @block.gpsimd
        def _(pool):
            def add_squares(b, r):
                for jt in range(2):
                    n = (b * 2 + r) * 2 + jt
                    pool.wait_ge(squared, n * 2 + 2)
                    nc.gpsimd.tensor_tensor(sq_re[:], sq_re[:], sq_im[:], ALU.add).then_inc(masked, 1)

            def mix(b, parts):
                for p in parts:
                    i = p % 2
                    n = b * PARTS + p
                    pool.wait_ge(mix_in[i], (b * (PARTS // 2) + p // 2 + 1) * 160)
                    am = ma[i][:].unsqueeze(1).broadcast_to([KT, PT, C])
                    nc.gpsimd.tensor_tensor(mh[i][:], mh[i][:], mb[i][:], ALU.mult).then_inc(pool_step, 1)
                    nc.gpsimd.tensor_tensor(mw[i][:], mw[i][:], am, ALU.mult).then_inc(pool_step, 1)
                    pool.wait_ge(pool_step, n * 4 + 2)
                    nc.gpsimd.tensor_tensor(mh[i][:], mh[i][:], mw[i][:], ALU.add).then_inc(pool_step, 1)
                    nc.gpsimd.tensor_tensor(mb[i][:], mb[i][:], am, ALU.add).then_inc(pool_step, 1)

            def image(b, before, more):
                for r in range(2):
                    add_squares(b, r)
                    if before is not None:
                        mix(before, range(2 * r, 2 * r + 2))
            images(pool, image)
            with pool.Fori(B - 1, B) as b:
                mix(b, range(PARTS))

        @block.tensor
        def _(pe):
            def transposes(b, r):
                pe.wait_ge(x_in[r], (b + 1) * 16)
                xv = x[r][:].rearrange("p (t c) -> p c t", c=C)
                for t in range(S):
                    pe.wait_ge(zt_dve if t % 2 else zt_act, HEAD + (b * 2 + r) * NT2 + t // 2)
                    pe.sem_inc(passed, 1)
                    for g in range(GROUPS):
                        last = nc.tensor.transpose(ps[0:H, TB + t % 2, g * W:(g + 1) * W], xv[:, g * S + t, :], w["ident"][0:H, 0:H])
                    last.then_inc(tr_ready, 1)
                pe.wait_ge(zt_act, HEAD + (b * 2 + r + 1) * NT2)
                pe.wait_ge(zt_dve, HEAD + (b * 2 + r + 1) * NT2)

            def forward(b, r):
                for jt in range(2):
                    n = (b * 2 + r) * 2 + jt
                    for part, (table, z, done) in enumerate(((w["dft_o"], zt[1], odd_ready), (w["dft_e"], zt[0], even_ready))):
                        for im in range(2):
                            if part == 0:
                                pe.wait_ge(odd_copied, HEAD + n * 2)
                            else:
                                pe.wait_ge(y_ready, HEAD + n * 2)
                            for k in range(NK):
                                c0 = im * Q + jt * KT
                                last = nc.tensor.matmul(ps[0:KT, FB + part * 2 + im, 0:HALF], table[:, k, c0:c0 + KT],
                                                        z[:, k, :], start=k == 0, stop=k == NK - 1)
                            last.then_inc(done, 1)

            def inverse(b, r):
                pe.wait_ge(y_ready, HEAD + (b * 2 + r + 1) * 4)
                for i in range(NI):
                    n = (b * 2 + r) * NI + i
                    pe.wait_ge(added, HEAD + ((n - 1) * 2 if i >= 2 else (b * 2 + r) * NI * 2))
                    for k in range(NK):
                        last = nc.tensor.matmul(ps[0:GP + W, IB + i % 2, 0:HALF],
                                                w["Y"][:, k, (i // 2) * 2 * GP:(i // 2) * 2 * GP + GP + W],
                                                w["G"][r][:, k, (i % 2) * HALF:(i % 2 + 1) * HALF],
                                                start=k == 0, stop=k == NK - 1)
                    last.then_inc(inv_ready, 1)

            def reweight(b):
                for r in range(2):
                    pe.wait_ge(mean_ready, b * 2 + r + 1)
                    pe.sem_inc(passed, 1)
                    nc.tensor.transpose(ps[:, TB + r, 0:H], mean[:, r, :], w["ident"][0:H, 0:H]).then_inc(mean_tr, 1)
                for r in range(2):
                    pe.wait_ge(mean_copied, b * 2 + r + 1)
                    nc.tensor.matmul(ps[0:H, TB + r, 128:256], mean_t[:, r, :], w["chan_t"][:, 1 + r, :],
                                     start=True, stop=True).then_inc(rew_ready, 1)

            def mix(b, parts):
                pe.wait_ge(rew_copied, b * 2 + 2)
                for p in parts:
                    n = b * PARTS + p
                    pe.wait_ge(mix_in[p % 2], (b * (PARTS // 2) + p // 2 + 1) * 160)
                    if p:
                        pe.wait_ge(xt_copied, n)
                    for t in range(PT):
                        last = nc.tensor.transpose(ps[:, FB + t // 4, KT * (t % 4):KT * (t % 4) + KT], mx[p % 2][:, t, :], w["ident"][0:KT, 0:KT])
                    last.then_inc(xt_ready, 1)
                    pe.wait_ge(xt_copied, n + 1)
                    if p:
                        pe.wait_ge(mixed, HEAD + n)
                    for t in range(PT):
                        last = nc.tensor.matmul(ps[0:KT, FB + 2 + t // 4, C * (t % 4):C * (t % 4) + C], xt[p % 2][:, t, :],
                                                w["chan_t"][:, 0, :], start=True, stop=True)
                    last.then_inc(chan_ready, 1)

            def image(b, before, more):
                for r in range(2):
                    transposes(b, r)
                    if before is not None:
                        pe.wait_ge(mixed, HEAD + before * PARTS + 2 * r)
                    forward(b, r)
                    if before is not None and r == 0:
                        reweight(before)
                    inverse(b, r)
                    if before is not None:
                        mix(before, range(2 * r, 2 * r + 2))
            pe.sem_inc(mean_tr, 2)
            images(pe, image)
            with pe.Fori(B - 1, B) as b:
                pe.wait_ge(mixed, HEAD + b * PARTS)
                reweight(b)
                mix(b, range(PARTS))

        @block.scalar
        def _(act):
            for head in (zt_act, odd_copied):
                act.sem_inc(head, HEAD)
            act.wait_ge(gap_clear, 2)
            def branch(b, r):
                for t in range(NT2):
                    act.wait_ge(tr_ready, (b * 2 + r) * S + 2 * t + 1)
                    e = GP * (t % 2)
                    nc.scalar.copy(zt[0][e:e + H, t // 2, :], ps[0:H, TB, 0:HALF]).then_inc(zt_act, 1)
                for jt in range(2):
                    n = (b * 2 + r) * 2 + jt
                    act.wait_ge(odd_ready, n * 2 + 1)
                    act.wait_ge(y_ready, HEAD + n * 2)
                    nc.scalar.copy(odd_re[:], ps[0:KT, FB, 0:HALF]).then_inc(odd_copied, 1)
                    act.wait_ge(odd_ready, n * 2 + 2)
                    nc.scalar.copy(odd_im[:], ps[0:KT, FB + 1, 0:HALF]).then_inc(odd_copied, 1)
                    act.wait_ge(high_ready, n * 2 + 1)
                    nc.scalar.activation(sq_re[:], hi_re[:], ACT.Square).then_inc(squared, 1)
                    act.wait_ge(high_ready, n * 2 + 2)
                    nc.scalar.activation(sq_im[:], hi_im[:], ACT.Square).then_inc(squared, 1)

            def reweight(b):
                for r in range(2):
                    act.wait_ge(mean_tr, 2 + b * 2 + r + 1)
                    nc.scalar.activation(mean_t[:, r, :], ps[:, TB + r, 0:H], ACT.Copy, scale=1.0 / H).then_inc(mean_copied, 1)
                for r in range(2):
                    act.wait_ge(rew_ready, b * 2 + r + 1)
                    nc.scalar.copy(rew[:, r, :], ps[0:H, TB + r, 128:256]).then_inc(rew_copied, 1)

            def mix(b, parts):
                for p in parts:
                    n = b * PARTS + p
                    act.wait_ge(xt_ready, n + 1)
                    nc.scalar.copy(xt[p % 2][:, 0:4, :].rearrange("p t k -> p (t k)"), ps[:, FB, 0:4 * KT])
                    nc.scalar.copy(xt[p % 2][:, 4:PT, :].rearrange("p t k -> p (t k)"), ps[:, FB + 1, 0:(PT - 4) * KT]).then_inc(xt_copied, 1)

            def image(b, before, more):
                for r in range(2):
                    branch(b, r)
                    if before is not None:
                        if r == 0:
                            reweight(before)
                        mix(before, range(2 * r, 2 * r + 2))
            images(act, image)
            with act.Fori(B - 1, B) as b:
                reweight(b)
                mix(b, range(PARTS))

        @block.vector
        def _(dve):
            for head in (zt_dve, y_ready, added, mixed):
                dve.sem_inc(head, HEAD)
            for z in zt:
                nc.vector.memset(z[:], 0.0).then_inc(gap_clear, 1)
            dve.wait_ge(gap_clear, 2)
            per_image = 16 + 2 * PARTS

            def average(b, r):
                dve.wait_ge(mean_tr, b * 2 + r + 1)
                dve.wait_ge(added, HEAD + (b * 2 + r + 1) * NI * 2)
                nc.vector.tensor_reduce(mean[:, r, :], x[r][:].rearrange("p (t c) -> p c t", c=C), AX.X, ALU.add).then_inc(mean_ready, 1)

            def mix(b, parts, start, steps):
                for p in parts:
                    n = b * PARTS + p
                    i = p % 2
                    dve.wait_ge(pool_step, (n + 1) * 4)
                    dve.wait_ge(chan_ready, n + 1)
                    for hf, (t0, t1) in enumerate(((0, 4), (4, PT))):
                        nc.vector.tensor_tensor(mw[i][:, t0:t1, :], ps[0:KT, FB + 2 + hf, 0:C * (t1 - t0)].rearrange("p (t c) -> p t c", c=C),
                                                mb[i][:, t0:t1, :], ALU.mult).then_inc(dve_step, 1)
                        steps += 1
                    dve.wait_ge(dve_step, start + steps)
                    nc.vector.tensor_tensor(mh[i][:], mh[i][:], mw[i][:], ALU.add).then_inc(mixed, 1)
                return steps

            def image(b, before, more):
                start = 0 if before is None else b * per_image - 2 * PARTS
                steps = 0

                def link(ins):
                    nonlocal steps
                    steps += 1
                    ins.then_inc(dve_step, 1)

                for r in range(2):
                    for t in range(NT2):
                        dve.wait_ge(tr_ready, (b * 2 + r) * S + 2 * t + 2)
                        e = GP * (t % 2)
                        nc.vector.tensor_copy(zt[1][e:e + H, t // 2, :], ps[0:H, TB + 1, 0:HALF]).then_inc(zt_dve, 1)
                    if r:
                        average(b, 0)
                    elif before is not None:
                        average(before, 1)
                    for jt in range(2):
                        n = (b * 2 + r) * 2 + jt
                        dve.wait_ge(odd_copied, HEAD + n * 2 + 1)
                        dve.wait_ge(even_ready, n * 2 + 1)
                        nc.vector.tensor_tensor(hi_re[:], ps[0:KT, FB + 2, 0:HALF], odd_re[:], ALU.subtract).then_inc(high_ready, 1)
                        link(nc.vector.tensor_tensor(lo_re[:], ps[0:KT, FB + 2, 0:HALF], odd_re[:], ALU.add))
                        dve.wait_ge(odd_copied, HEAD + n * 2 + 2)
                        dve.wait_ge(even_ready, n * 2 + 2)
                        if jt == 0:
                            nc.vector.scalar_tensor_tensor(hi_im[:], ps[0:KT, FB + 3, 0:HALF], w["flags"][0:KT, 3:4], odd_im[:],
                                                           ALU.mult, ALU.subtract).then_inc(high_ready, 1)
                        else:
                            nc.vector.tensor_tensor(hi_im[:], ps[0:KT, FB + 3, 0:HALF], odd_im[:], ALU.subtract).then_inc(high_ready, 1)
                        link(nc.vector.tensor_tensor(lo_im[:], ps[0:KT, FB + 3, 0:HALF], odd_im[:], ALU.add))
                        dve.wait_ge(masked, n + 1)
                        link(nc.vector.tensor_tensor(mask[:], sq_re[:], w["thr"][:, r, :], ALU.is_ge))
                        dve.wait_ge(dve_step, start + steps)
                        dve.wait_ge(high_ready, n * 2 + 2)
                        nc.vector.tensor_tensor(hi_re[:], hi_re[:], mask[:], ALU.mult)
                        link(nc.vector.tensor_tensor(hi_im[:], hi_im[:], mask[:], ALU.mult))
                        dve.wait_ge(dve_step, start + steps)
                        for im, (lo, hi) in enumerate(((lo_re, hi_re), (lo_im, hi_im))):
                            yv = w["Y"][:, im * 2 + jt, :].rearrange("p (g e) -> p g e", e=GP)[:, :, 0:W]
                            nc.vector.tensor_tensor(yv, lo[:].rearrange("p (g e) -> p g e", e=W),
                                                    hi[:].rearrange("p (g e) -> p g e", e=W), ALU.add).then_inc(y_ready, 1)
                    xg = x[r][:].rearrange("p (t g s) -> p g t s", g=GROUPS, s=S)
                    for i in range(NI):
                        n = (b * 2 + r) * NI + i
                        dve.wait_ge(inv_ready, n + 1)
                        for odd in range(2):
                            g, t0 = (i // 2) * 2 + odd, (i % 2) * (H // 2)
                            dst = xg[:, g, t0:t0 + H // 2, :]
                            nc.vector.tensor_tensor(dst, ps[GP * odd:GP * odd + W, IB + i % 2, 0:HALF].rearrange("p (t s) -> p t s", s=S),
                                                    dst, ALU.add).then_inc(added, 1)
                    if before is not None:
                        steps = mix(before, range(2 * r, 2 * r + 2), start, steps)
            images(dve, image)
            with dve.Fori(B - 1, B) as b:
                average(b, 1)
                mix(b, range(PARTS), (b + 1) * per_image - 2 * PARTS, 0)


def prepare_windows(nc, a, w, scr):
    with ExitStack() as ctx:
        sb = lambda n, s, d=F32: ctx.enter_context(nc.sbuf_tensor(n, s, d))
        sem = lambda n: ctx.enter_context(nc.semaphore(n))
        N = DIAG * DIAG
        pick, dist = sb("pick", [DIST, N]), sb("dist", [DIST, 1])
        line = sb("line", [1, N])
        mirrored = sb("mirrored", [W, WIN])
        flips = sb("flips", [W, 3, KT])
        high = sb("high", [KT, 2, 512], F16)
        by_query = sb("by_query", [KT, DIAG - 1, RP], F16)
        ps = ctx.enter_context(nc.psum_tensor("win_ps", [128, 8, 512], F32))
        loaded, picked, copied, kept = sem("win_loaded"), sem("win_picked"), sem("win_copied"), sem("win_kept")
        spread, flipped, rounded, done = sem("win_spread"), sem("win_flipped"), sem("win_rounded"), sem("win_done")
        padded = sem("win_padded")
        block = ctx.enter_context(nc.Block())
        pieces = [(i, min(512, N - i)) for i in range(0, N, 512)]
        cut = 512 // W * W
        cuts = [(i, min(cut, WIN - i)) for i in range(0, WIN, cut)]
        query = WIN - W

        @block.sync
        def _(sp):
            sp.dma_start(pick[:], a["dist_pick"]).then_inc(loaded, 16)
            sp.dma_start(dist[:], a["L1_conv_spatial_bias"][:, 0:1], allow_slow_non_contiguous=True).then_inc(loaded, 16)
            sp.dma_start(flips[:], a["flips"]).then_inc(loaded, 16)
            sp.wait_ge(copied, len(pieces))
            sp.dma_start(scr["dist"].rearrange("s j -> (s j)").unsqueeze(0), line[:]).then_inc(kept, 16)
            sp.wait_ge(kept, 16)
            t = scr["dist"]
            sp.dma_start(mirrored[:].rearrange("p (s v) -> p s v", v=W),
                         bass.AP(t.tensor, t.offset, [[1, W], [DIAG, DIAG], [1, W]])).then_inc(spread, 16)
            sp.wait_ge(spread, 16)
            sp.wait_ge(done, 2 * len(cuts))
            sp.dma_start(scr["by_query"], by_query[:].rearrange("p s v -> p (s v)")).then_inc(kept, 16)
            sp.wait_ge(kept, 32)

        @block.gpsimd
        def _(pool):
            nc.gpsimd.memset(by_query[:], 0.0).then_inc(padded, 1)

        @block.tensor
        def _(pe):
            pe.wait_ge(loaded, 48)
            for n, (i, m) in enumerate(pieces):
                if n >= 8:
                    pe.wait_ge(copied, n - 7)
                nc.tensor.matmul(ps[0:1, n % 8, 0:m], dist[:], pick[:, i:i + m], start=True, stop=True).then_inc(picked, 1)
            pe.wait_ge(copied, len(pieces))
            pe.wait_ge(spread, 16)
            for n, (i, m) in enumerate(cuts):
                if n >= 2:
                    pe.wait_ge(done, 2 * n - 2)
                nc.tensor.matmul(ps[0:KT, n % 2, 0:m], flips[:, 0, :], mirrored[:, i:i + m], start=True, stop=True).then_inc(flipped, 1)
                m = min(m, query - i)
                nc.tensor.matmul(ps[0:KT, 2 + n % 2, 0:m], flips[:, 1, :], mirrored[:, i + W:i + W + m], start=True, stop=False)
                nc.tensor.matmul(ps[0:KT, 2 + n % 2, 0:m], flips[:, 2, :], mirrored[:, i:i + m], start=False, stop=True).then_inc(flipped, 1)

        @block.scalar
        def _(act):
            for n, (i, m) in enumerate(pieces):
                act.wait_ge(picked, n + 1)
                nc.scalar.copy(line[:, i:i + m], ps[0:1, n % 8, 0:m]).then_inc(copied, 1)
            for n, (i, m) in enumerate(cuts):
                act.wait_ge(flipped, 2 * n + 1)
                if n >= 2:
                    act.wait_ge(done, 2 * n - 2)
                nc.scalar.copy(high[:, n % 2, 0:m], ps[0:KT, n % 2, 0:m]).then_inc(rounded, 1)

        @block.vector
        def _(dve):
            dve.wait_ge(padded, 1)
            for n, (i, m) in enumerate(cuts):
                dve.wait_ge(rounded, n + 1)
                nc.vector.scalar_tensor_tensor(w["by_key"][:, i:i + m], high[:, n % 2, 0:m], w["flags"][0:KT, 2:3],
                                               ps[0:KT, n % 2, 0:m], ALU.mult, ALU.add).then_inc(done, 1)
                dve.wait_ge(flipped, 2 * n + 2)
                m = min(m, query - i)
                nc.vector.tensor_copy(by_query[:, i // W:(i + m) // W, 0:W],
                                      ps[0:KT, 2 + n % 2, 0:m].rearrange("p (s v) -> p s v", v=W)).then_inc(done, 1)
            dve.wait_ge(done, 2 * len(cuts))


def layer1(nc, a, w, scr, out):
    with ExitStack() as ctx:
        sb = lambda n, s, d=F32: ctx.enter_context(nc.sbuf_tensor(n, s, d))
        sem = lambda n: ctx.enter_context(nc.semaphore(n))
        VW = DK + 1
        xc = [sb(f"xc{i}", [KT, UT, C]) for i in range(2)]
        xT = sb("xT", [C, QC * RP])
        qs = sb("qs", [STK, HG, TOK], F16)
        ks = [sb(f"ks{g}", [STK + 1, HG, H * RP], F16) for g in range(NG)]
        v = [sb(f"v{g}", [GP + W, NT * HG * VW + 32 - VW]) for g in range(NG)]
        p = [sb(f"p{i}", [GP + W, 2, CH]) for i in range(4)]
        q_max = sb("q_max", [STK + 1, HG, CH], F16)
        q_exp = sb("q_exp", [STK + 1, HG, CH], F16)
        q_pick = sb("q_pick", [128, HG, CH], F16)
        key_win = [sb(f"key_win{i}", [DK + KT, STG_Q], F16) for i in range(2)]
        win_exp = sb("win_exp", [KT, STG_K], F16)
        full = [sb(f"full{i}", [128, CH]) for i in range(3)]
        half = [sb(f"half{i}", [128, CH], F16) for i in range(3)]
        wq4, wk4 = sb("wq4", [C, HEADS, STK]), sb("wk4", [C, HEADS, STK])
        wv, wo = sb("wv", [C, C]), sb("wo", [128, NG, C])
        bq4, bk4 = sb("bq4", [128, HG]), sb("bk4", [128, HG])
        bv = sb("bv", [GP + W, C])
        bo, gamma, beta = sb("bo", [KT, C]), sb("gamma", [KT, C]), sb("beta", [KT, C])
        fold16, id16 = sb("fold16", [KT, W], F16), sb("id16", [KT, KT], F16)
        sum_pick = sb("sum_pick", [128, 128])
        partial = sb("partial", [KT, UT * HG, NC])
        neg_max = sb("neg_max", [KT, UT * HG], F16)
        ctx_raw, recip, ctx1, ctx0c = sb("ctx_raw", [128, CH]), sb("recip", [128, CH]), sb("ctx1", [128, CH]), sb("ctx0c", [128, CH])
        ctx0 = sb("ctx0", [128, TOK])
        res_in, res = sb("res_in", [KT, UT, C]), sb("res", [KT, UT, C])
        stat = sb("stat", [KT, 3, UT])
        ps = ctx.enter_context(nc.psum_tensor("l1_ps", [128, 8, 512], F32))
        SB, CB, AB, MB = 0, 4, 5, 7

        loaded, set_up, clear = sem("l1_loaded"), sem("l1_set_up"), sem("clear")
        xc_in, xt_ready = [sem(f"xc{i}_in") for i in range(2)], sem("l1_xt_ready")
        side_ready, side_free = sem("side_ready"), sem("side_free")
        proj_full, proj_half, proj_done, v_done = sem("proj_full"), sem("proj_half"), sem("proj_done"), sem("v_done")
        staged_max, staged_pick, staged_exp = sem("staged_max"), sem("staged_pick"), sem("staged_exp")
        win_in, keys_in = [sem(f"win_in{i}") for i in range(2)], [sem(f"keys_in{i}") for i in range(2)]
        score_ready, max_done, neg_ready, row_copied = sem("score_ready"), sem("max_done"), sem("neg_ready"), sem("row_copied")
        exp_ready, exp_done, pv_done = sem("exp_ready"), sem("exp_done"), sem("pv_done")
        ctx_copied, recip_done, ctx_ready = sem("ctx_copied"), sem("recip_done"), sem("ctx_ready")
        res_loaded, mixed_in, out_ready, stored, res_free = (sem("res_loaded"), sem("mixed_in"), sem("out_ready"),
                                                             sem("stored"), sem("res_free"))
        norm_step = sem("norm_step")
        passed = sem("l1_passed")
        block = ctx.enter_context(nc.Block())
        EX = NT * 2
        MX = NT * HG
        PJ = NC * 4
        LOADS = 8 + 16 + 1 + HEADS + 2 + 3 + 2
        K_CTX, K_SUM, K_RECIP, K_MIX, K_NORM = 2, 3, 5, 10, 11
        K_PREP = 12
        PREP = NC * 6
        K_LATE, K_NEXT = 4, 6
        K_ROWS = 52
        LAG = 2
        CLEARED = 6
        AHEAD = NC + 1
        C_PREP = NC - 2

        def ahead(k, g, c):
            first = 0 if not isinstance(c, int) else K_LATE if c == NC - 1 else K_NEXT if c == g == 0 else 0
            return max(0, min(MX, -(-MX * (k + 1 - first) // (K_ROWS - 3 - first))))

        rows = lambda t, n=RP: t.rearrange("p (h e) -> p h e", e=n)
        key_rows = lambda g: ks[g][:].rearrange("p h (s e) -> p (h s) e", e=RP)

        def number_sides(last):
            place = {}
            for g in range(NG):
                for c in range(NC):
                    final = last and g == NG - 1
                    if c or g:
                        place[g, c, "sum"] = len(place)
                        if g and c:
                            place[g, c, "mix"] = len(place)
                    for k in range(EX):
                        if k == K_ROWS and not (final and c == NC - 1):
                            place[g, c, "rows"] = len(place)
                        if c == C_PREP and K_PREP <= k < K_PREP + PREP and not final:
                            place[g, c, k - K_PREP] = len(place)
            place["end", "sum"] = len(place)
            place["end", "mix"] = len(place)
            return place

        FIRST = PREP + 1
        PLACES = {last: number_sides(last) for last in (False, True)}
        SIDES = len(PLACES[False])

        def side(b, last, g, c, what):
            place = PLACES[last]
            if g == "end":
                return FIRST + b * SIDES + place["end", what]
            if isinstance(c, int):
                return FIRST + b * SIDES + place[g, c, what]
            return FIRST + b * SIDES + place[g, 1, what] + (c - 1) * (place[g, 2, what] - place[g, 1, what])

        def images(eng, image):
            with eng.Fori(0, B - 1) as b:
                image(b, False)
            image(B - 1, True)

        def chunks(eng, g, last, step):
            final = last and g == NG - 1
            step(0, None if g == 0 else NC - 1, True, False)
            with eng.Fori(1, C_PREP) as c:
                step(c, c - 1, True, False)
            step(C_PREP, C_PREP - 1, True, not final)
            step(NC - 1, NC - 2, not final, False)

        @block.sync
        def _(sp):
            def load(dst, src):
                sp.dma_start(dst, src).then_inc(loaded, 16)
            sp.wait_ge(set_up, 1)
            load(ctx0c[0:KT, 0:W], a["fold"])
            for k in range(4):
                load(wq4[:, :, k * DK:(k + 1) * DK], a["L1_conv_wq"].rearrange("c (h d) -> c h d", d=DK))
                load(wk4[:, :, k * DK:(k + 1) * DK], a["L1_conv_wk"].rearrange("c (h d) -> c h d", d=DK))
            for dst, src in ((bq4, "L1_conv_bq"), (bk4, "L1_conv_bk")):
                for k in range(8):
                    sp.dma_start(dst[k * DK:(k + 1) * DK, :], a[src].rearrange("(m e d) -> e d m", e=2, d=DK)[k // 4],
                                 allow_slow_non_contiguous=True).then_inc(loaded, 16)
            load(wv[:], a["L1_conv_wv"])
            for g in range(NG):
                for j in range(HG):
                    h = g * HG + j
                    load(wo[32 * j:32 * j + DK, g, :], a["L1_conv_wo"][h * DK:(h + 1) * DK, :])
            for r in range(2):
                load(bv[r * GP:r * GP + W, :], a["L1_conv_bv"].partition_broadcast(W))
            for dst, src in ((bo, "L1_conv_bo"), (gamma, "L1_conv_ln_gamma"), (beta, "L1_conv_ln_beta")):
                load(dst[:], a[src].partition_broadcast(KT))
            load(sum_pick[:], a["sum_pick"])
            sp.wait_ge(clear, CLEARED)
            with sp.Fori(0, B) as b:
                for g in range(NG):
                    G = b * NG + g
                    with sp.Fori(0, NC) as c:
                        for i in range(UT * HG):
                            u, j = i // HG, i % HG
                            sp.wait_ge(score_ready, ((G * NC + c) * UT * HG + i - 1) * NC + AHEAD)
                            sp.sem_inc(passed, 1)
                            if i < 2:
                                sp.dma_start(key_win[i][DK:DK + KT, :],
                                             scr["by_query"][:, bass.ds((H - QC - c * QC) * RP, STG_Q)]).then_inc(win_in[i], 16)
                                sp.wait_ge(proj_done, (G + 1) * PJ)
                                sp.sem_inc(passed, 1)
                            s0 = (QC - 2 - 2 * u) * RP
                            sp.dma_start(key_win[i % 2][0:DK, s0:s0 + H * RP], ks[g][0:DK, j, :]).then_inc(keys_in[i % 2], 16)

        @block.gpsimd
        def _(pool):
            def piece(t, b, c, r):
                return t[bass.ds(b, 1), bass.ds(c * QC, QC)].rearrange("o (j r) w c -> r (o w) j c", r=2)[r]

            def load_chunk(b, ch):
                for r in range(2):
                    pool.dma_start(xc[ch % 2][r * W:(r + 1) * W, :, :], piece(scr["y"], b, ch, r)).then_inc(xc_in[ch % 2], 16)

            def project(b, G):
                load_chunk(b, 0)
                for ch in range(NC):
                    if ch + 1 < NC:
                        if ch:
                            pool.wait_ge(xt_ready, G * NC + ch)
                            pool.sem_inc(passed, 1)
                        load_chunk(b, ch + 1)
                    for i in range(4):
                        n = G * PJ + ch * 4 + i
                        m = (ch * 4 + i) % 3
                        pool.wait_ge(proj_full, n + 1)
                        pool.sem_inc(passed, 1)
                        nc.gpsimd.tensor_copy(half[m][:], full[m][:]).then_inc(proj_half, 1)
                pool.wait_ge(xt_ready, (G + 1) * NC)
                pool.sem_inc(passed, 1)

            def load_residual(b, c):
                pool.wait_ge(out_ready, HEAD + b * NC + c)
                pool.sem_inc(passed, 1)
                for r in range(2):
                    pool.dma_start(res_in[r * W:(r + 1) * W, :, :], piece(scr["y"], b, c, r)).then_inc(res_loaded, 16)

            def store(b, c):
                n = b * NC + c
                pool.wait_ge(out_ready, HEAD + n + 1)
                pool.sem_inc(passed, 1)
                for r in range(2):
                    pool.dma_start(piece(out, b, c, r), res[r * W:(r + 1) * W, :, :]).then_inc(stored, 16)
                pool.wait_ge(stored, (n + 1) * 32)
                pool.sem_inc(res_free, 1)

            def outputs(b, first, end):
                with pool.Fori(first, end) as c:
                    load_residual(b, c)
                    store(b, c)

            nc.gpsimd.memset(key_rows(1)[STK:STK + 1, :, 0:W], 1.0).then_inc(clear, 1)
            pool.sem_inc(res_free, HEAD)
            with pool.Fori(0, 1) as b:
                project(b, b)

            def image(b, last):
                project(b, b * NG + 1)
                outputs(b, 0, C_PREP - 1)
                load_residual(b, C_PREP - 1)
                if not last:
                    project(b + 1, b * NG + 2)
                store(b, C_PREP - 1)
                outputs(b, C_PREP, NC)
            images(pool, image)

        @block.tensor
        def _(pe):
            def scores(g, k, between):
                t, pair = k // 2, k % 2
                for e in range(2):
                    j, bank = 2 * pair + e, SB + 2 * pair + e
                    nc.tensor.matmul(ps[0:GP + W, bank, 0:CH], ks[g][:, j, t * 2 * RP:t * 2 * RP + GP + W], q_exp[:, j, :],
                                     start=True, stop=True)
                    for r in range(2):
                        s0 = (H - 1 - 2 * t - r) * W
                        last = nc.tensor.matmul(ps[r * GP:r * GP + W, bank, 0:CH], fold16[:], win_exp[:, s0:s0 + CH],
                                                start=False, stop=True, skip_group_check=True)
                    if e == 0:
                        between()
                last.then_inc(exp_ready, 1)

            def weigh(g, k):
                t, pair = k // 2, k % 2
                for e in range(2):
                    j = 2 * pair + e
                    v0 = (t * HG + j) * VW
                    last = nc.tensor.matmul(ps[32 * j:32 * j + 32, CB, 0:CH], v[g][:, v0:v0 + 32], p[k % 4][:, e, :],
                                            start=t == 0, stop=t == NT - 1, skip_group_check=True)
                last.then_inc(pv_done, 1)

            def max_scores(m, i):
                tile, kc = i // NC, i % NC
                u, j, place = tile // HG, tile % HG, tile % 2
                if i in (0, NC):
                    pe.wait_ge(win_in[place], (m + 1) * 16)
                if kc == 0:
                    pe.wait_ge(keys_in[place], (m * UT * HG // 2 + tile // 2 + 1) * 16)
                if i >= 2:
                    pe.wait_ge(max_done, m * MX + i - 1)
                s0 = QC * kc - 2 * u + QC - 2
                nc.tensor.matmul(ps[0:KT, AB + i % 2, 0:CH], q_pick[:, j, u * KT:(u + 1) * KT],
                                 rows(key_win[place][:])[:, s0:s0 + QC, 0:W], start=True, stop=True).then_inc(score_ready, 1)

            def turn_rows(m, n):
                pe.wait_ge(neg_ready, m + 1)
                pe.wait_ge(side_free, HEAD + n)
                for j in range(HG):
                    for u in range(UT):
                        last = nc.tensor.matmul(ps[32 * j:32 * j + 1, MB, u * KT:(u + 1) * KT],
                                                neg_max[:, u * HG + j:u * HG + j + 1], id16[:], start=True, stop=True)
                last.then_inc(side_ready, 1)

            def project(G, g, t, n):
                ch, i = t // 6, t % 6
                pe.wait_ge(side_free, HEAD + n)
                if i == 0:
                    in_buffer = (NC + 1 - ch % 2) // 2
                    pe.wait_ge(xc_in[ch % 2], (G * in_buffer + ch // 2 + 1) * 32)
                    for u in range(UT):
                        last = nc.tensor.transpose(ps[:, MB, u * KT:(u + 1) * KT], xc[ch % 2][:, u, :], w["ident"][0:KT, 0:KT])
                    last.then_inc(side_ready, 1)
                elif i < 5:
                    h = g * HG + 2 * ((i - 1) // 2)
                    nc.tensor.matmul(ps[:, MB, 0:CH], (wk4 if i % 2 == 0 else wq4)[:, h:h + 2, :].rearrange("c h k -> c (h k)"),
                                     rows(xT[:])[:, :, 0:W], start=True, stop=True).then_inc(side_ready, 1)
                else:
                    for u in range(UT):
                        last = nc.tensor.matmul(ps[0:GP + W, MB, u * HG * DK:(u + 1) * HG * DK], xT[:, u * 2 * RP:u * 2 * RP + GP + W],
                                                wv[:, g * HG * DK:(g + 1) * HG * DK], start=True, stop=True)
                    last.then_inc(side_ready, 1)

            def spread_sums(n_chunk, n):
                pe.wait_ge(ctx_copied, n_chunk + 1)
                pe.wait_ge(side_free, HEAD + n)
                nc.tensor.matmul(ps[:, MB, 0:CH], sum_pick[:], ctx_raw[:], start=True, stop=True).then_inc(side_ready, 1)

            def mix(n_chunk, n):
                pe.wait_ge(ctx_ready, HEAD + n_chunk + 1)
                pe.wait_ge(side_free, HEAD + n)
                for u in range(UT):
                    for gg, cx in enumerate((ctx0c, ctx1)):
                        last = nc.tensor.matmul(ps[0:KT, MB, u * C:(u + 1) * C], cx[:, u * KT:(u + 1) * KT],
                                                wo[:, gg, :], start=gg == 0, stop=gg == 1)
                last.then_inc(side_ready, 1)

            pe.sem_inc(exp_ready, HEAD)
            pe.sem_inc(score_ready, AHEAD)
            pe.sem_inc(pv_done, 4)
            pe.wait_ge(set_up, 2)
            with pe.Fori(0, 1) as z:
                for t in range(PREP):
                    project(z, 0, t, z + t)
                pe.wait_ge(proj_done, PJ)
                pe.wait_ge(staged_pick, 1)
                for i in range(MX):
                    max_scores(z, i)
                turn_rows(z, z + PREP)

            def image(b, last):
                for g in range(NG):
                    G = b * NG + g

                    def step(c, before, maxima, projections):
                        n = G * NC + c
                        m = n + 1
                        for k in range(EX):
                            tiles = iter(range(ahead(k - 1, g, c), ahead(k, g, c)) if maxima else ())

                            def next_max():
                                i = next(tiles, None)
                                if i == 0:
                                    pe.wait_ge(staged_pick, m + 1)
                                if i is not None:
                                    max_scores(m, i)

                            if k % 2 == 0:
                                next_max()
                            if k == 0:
                                next_max()
                                if before is not None:
                                    pe.wait_ge(exp_done, 2 + n * EX)
                                    for i in (EX - 2, EX - 1):
                                        weigh(g if not (isinstance(c, int) and c == 0) else 1 - g, i)
                            pe.wait_ge(exp_done, 2 + n * EX + k - 1)
                            if k == 0:
                                pe.wait_ge(staged_exp, HEAD + (n + 1) * 2)
                            scores(g, k, next_max)
                            next_max()
                            if k > 1 and k % 2:
                                if k == 3 and before is not None:
                                    pe.wait_ge(ctx_copied, n)
                                weigh(g, k - 3)
                                weigh(g, k - 2)
                            next_max()
                            if k == K_SUM and before is not None:
                                spread_sums(n - 1, side(b, last, g, c, "sum"))
                            if k == K_MIX and before is not None and g and not (isinstance(c, int) and c == 0):
                                mix(n - 1, side(b, last, g, c, "mix"))
                            if maxima:
                                if k == K_ROWS:
                                    turn_rows(m, side(b, last, g, c, "rows"))
                            if projections and K_PREP <= k < K_PREP + PREP:
                                project(G + 1, 1 - g, k - K_PREP, side(b, last, g, c, k - K_PREP))

                    pe.wait_ge(v_done, (G + 1) * NC)
                    chunks(pe, g, last, step)
                n = b * NG * NC + NG * NC - 1
                for k in range(2):
                    pe.wait_ge(exp_done, 2 + n * EX + EX - 1 + k)
                    weigh(1, EX - 2 + k)
                spread_sums(n, side(b, last, "end", 0, "sum"))
                mix(n, side(b, last, "end", 0, "mix"))
            images(pe, image)

        @block.scalar
        def _(act):
            def project(G, g, t, n):
                ch, i = t // 6, t % 6
                if i == 0:
                    act.wait_ge(side_ready, n + 1)
                    nc.scalar.copy(rows(xT[:])[:, :, 0:W], rows(ps[:, MB, 0:CH], W)).then_inc(side_free, 1)
                    act.wait_ge(side_free, HEAD + n + 1)
                    act.sem_inc(xt_ready, 1)
                elif i < 5:
                    pn = ch * 4 + i - 1
                    is_k, m = i % 2 == 0, g * 2 + (i - 1) // 2
                    act.wait_ge(side_ready, n + 1)
                    if pn >= 3:
                        act.wait_ge(proj_done, G * PJ + pn - 2)
                    nc.scalar.activation(full[pn % 3][:], ps[:, MB, 0:CH], ACT.Identity,
                                         bias=(bk4 if is_k else bq4)[:, m:m + 1],
                                         scale=1.0 if is_k else DK ** -0.5).then_inc(proj_full, 1)
                    act.wait_ge(proj_full, G * PJ + pn + 1)
                    act.sem_inc(side_free, 1)

            def copy_rows(n):
                act.wait_ge(side_ready, n + 1)
                for j in (2, 3):
                    nc.scalar.copy(q_max[STK:STK + 1, j, :], ps[32 * j:32 * j + 1, MB, 0:CH]).then_inc(row_copied, 1)

            def copy_context(n):
                act.wait_ge(pv_done, 4 + (n + 1) * EX)
                act.wait_ge(ctx_ready, HEAD + n)
                nc.scalar.copy(ctx_raw[:], ps[:, CB, 0:CH]).then_inc(ctx_copied, 1)

            act.sem_inc(exp_done, 2)
            act.sem_inc(side_free, HEAD)
            act.wait_ge(set_up, 2)
            with act.Fori(0, 1) as z:
                for t in range(PREP):
                    project(z, 0, t, z + t)
                copy_rows(z + PREP)

            def image(b, last):
                for g in range(NG):
                    G = b * NG + g

                    def step(c, before, maxima, projections):
                        n = G * NC + c
                        for k in range(EX):
                            if k == K_CTX and before is not None:
                                copy_context(n - 1)
                            act.wait_ge(pv_done, 4 + n * EX + k - 3)
                            act.wait_ge(exp_ready, HEAD + n * EX + k + 1)
                            bank = SB + 2 * (k % 2)
                            nc.scalar.activation(p[k % 4][:], ps[0:GP + W, bank:bank + 2, 0:CH], ACT.Exp).then_inc(exp_done, 1)
                            if maxima and k == K_ROWS:
                                copy_rows(side(b, last, g, c, "rows"))
                            if projections and K_PREP <= k < K_PREP + PREP:
                                project(G + 1, 1 - g, k - K_PREP, side(b, last, g, c, k - K_PREP))
                    chunks(act, g, last, step)
                copy_context(b * NG * NC + NG * NC - 1)
            images(act, image)

        @block.vector
        def _(dve):
            for head in (ctx_ready, mixed_in, staged_exp, out_ready):
                dve.sem_inc(head, HEAD)
            nc.vector.memset(wo[:], 0.0)
            nc.vector.memset(bv[:], 0.0).then_inc(set_up, 1)
            for t in v:
                nc.vector.memset(t[:], 0.0).then_inc(clear, 1)
            nc.vector.memset(xT[:], 0.0)
            for g in range(NG):
                nc.vector.memset(key_rows(g)[:, :, W:RP], 0.0).then_inc(clear, 1)
            nc.vector.memset(key_rows(0)[STK:STK + 1, :, 0:W], 1.0).then_inc(clear, 1)
            dve.wait_ge(clear, CLEARED)
            for g in range(NG):
                for r in range(2):
                    nc.vector.memset(v[g][r * GP:r * GP + W, 0:NT * HG * VW].rearrange("p (t d) -> p t d", d=VW)[:, :, DK:VW], 1.0)
            dve.wait_ge(loaded, 16 * LOADS)
            nc.vector.tensor_copy(fold16[:], ctx0c[0:KT, 0:W])
            nc.vector.tensor_copy(id16[:], w["ident"][0:KT, 0:KT])
            nc.vector.tensor_copy(q_pick[:].rearrange("p h (u q) -> p (h u) q", q=KT),
                                  w["ident"][:, DK:DK + KT].unsqueeze(1).broadcast_to([128, HG * UT, KT]))
            nc.vector.tensor_scalar(bq4[:], bq4[:], DK ** -0.5, None, ALU.mult).then_inc(set_up, 1)
            dve.wait_ge(set_up, 2)

            def split(G, g, t):
                ch, i = t // 6, t % 6
                if 1 <= i < 5:
                    pn = ch * 4 + i - 1
                    is_k, m = i % 2 == 0, (i - 1) // 2
                    dve.wait_ge(proj_half, G * PJ + pn + 1)
                    for e in range(2):
                        part = slice(STK * e, STK * e + STK)
                        dst = (rows(ks[g][0:STK, 2 * m + e, :])[:, ch * QC:(ch + 1) * QC, 0:W] if is_k
                               else rows(qs[0:STK, 2 * m + e, :], W)[:, ch * QC:(ch + 1) * QC, :])
                        last = nc.vector.scalar_tensor_tensor(dst, rows(half[pn % 3][part, :], W),
                                                              w["flags"][part, 0:1] if is_k else w["flags"][part, 1:2],
                                                              rows(full[pn % 3][part, :], W), ALU.mult, ALU.add)
                    last.then_inc(proj_done, 1)

            def add_values(g, t, n):
                ch, i = t // 6, t % 6
                if i == 5:
                    dve.wait_ge(side_ready, n + 1)
                    nc.vector.tensor_tensor(
                        v[g][:, 0:NT * HG * VW].rearrange("p (t h d) -> p t h d", h=HG, d=VW)[:, ch * UT:(ch + 1) * UT, :, 0:DK],
                        ps[0:GP + W, MB, 0:UT * HG * DK].rearrange("p (t h d) -> p t h d", h=HG, d=DK),
                        bv[:, g * HG * DK:(g + 1) * HG * DK].rearrange("p (h d) -> p h d", d=DK).unsqueeze(1).broadcast_to([GP + W, UT, HG, DK]),
                        ALU.add).then_inc(v_done, 1)

            def stage_max(m, c):
                dve.wait_ge(staged_exp, HEAD + m * 2)
                nc.vector.tensor_copy(q_max[0:STK], qs[:, :, bass.ds(c * CH, CH)]).then_inc(staged_max, 1)

            def stage_pick(m, c):
                dve.wait_ge(neg_ready, m)
                dve.sem_inc(passed, 1)
                nc.vector.tensor_copy(q_pick[0:DK], qs[0:DK, :, bass.ds(c * CH, CH)]).then_inc(staged_pick, 1)

            def stage_exp(n, c):
                dve.wait_ge(exp_ready, HEAD + n * EX)
                dve.wait_ge(row_copied, (n + 1) * HG)
                nc.vector.tensor_copy(q_exp[:], q_max[:]).then_inc(staged_exp, 1)
                nc.vector.tensor_copy(win_exp[:], w["by_key"][:, bass.ds(c * QC * W, STG_K)]).then_inc(staged_exp, 1)

            def find_max(i, base):
                tile, kc = i // NC, i % NC
                dve.wait_ge(score_ready, AHEAD + base + i + 1)
                nc.vector.tensor_reduce(partial[:, tile, kc:kc + 1], ps[0:KT, AB + i % 2, 0:CH], AX.X,
                                        ALU.max).then_inc(max_done, 1)

            def join_max(m):
                dve.wait_ge(max_done, (m + 1) * MX)
                nc.vector.tensor_reduce(neg_max[:], partial[:], AX.X, ALU.max, negate=True).then_inc(neg_ready, 1)

            def copy_rows(m, n):
                dve.wait_ge(side_ready, n + 1)
                dve.wait_ge(staged_max, m + 1)
                for j in (0, 1):
                    nc.vector.tensor_copy(q_max[STK:STK + 1, j, :], ps[32 * j:32 * j + 1, MB, 0:CH]).then_inc(row_copied, 1)
                dve.wait_ge(row_copied, (m + 1) * HG)
                dve.sem_inc(side_free, 1)

            def invert(piece, n_chunk, n):
                cut = slice(piece * KT, (piece + 1) * KT)
                if piece == 0:
                    dve.wait_ge(ctx_ready, HEAD + n_chunk)
                dve.wait_ge(side_ready, n + 1)
                nc.vector.reciprocal(recip[:, cut], ps[:, MB, cut]).then_inc(recip_done, 1)

            def normalise_context(g, c, n_chunk):
                dve.wait_ge(recip_done, (n_chunk + 1) * UT)
                dve.sem_inc(side_free, 1)
                if g == 0:
                    nc.vector.tensor_tensor(ctx0[:, bass.ds(c * CH, CH)], ctx_raw[:], recip[:], ALU.mult).then_inc(ctx_ready, 1)
                else:
                    nc.vector.tensor_copy(ctx0c[:], ctx0[:, bass.ds(c * CH, CH)])
                    nc.vector.tensor_tensor(ctx1[:], ctx_raw[:], recip[:], ALU.mult).then_inc(ctx_ready, 1)

            def norm(n, n_side):
                done = 0

                def link(ins):
                    nonlocal done
                    done += 1
                    ins.then_inc(norm_step, 1)
                    return done

                spread = lambda t: t.unsqueeze(2).broadcast_to([KT, UT, C])
                each = lambda t: t[:].unsqueeze(1).broadcast_to([KT, UT, C])
                after = lambda: dve.wait_ge(norm_step, n * LINKS + done)
                dve.wait_ge(side_ready, n_side + 1)
                dve.wait_ge(res_loaded, (n + 1) * 32)
                dve.wait_ge(res_free, HEAD + n)
                nc.vector.tensor_tensor(res[:], ps[0:KT, MB, :].rearrange("p (u c) -> p u c", c=C),
                                        res_in[:], ALU.add).then_inc(mixed_in, 1)
                yield
                dve.wait_ge(mixed_in, HEAD + n + 1)
                dve.sem_inc(side_free, 1)
                link(nc.vector.tensor_tensor(res[:], res[:], each(bo), ALU.add))
                yield
                after()
                link(nc.vector.tensor_reduce(stat[:, 0, :], res[:], AX.X, ALU.add))
                yield
                after()
                link(nc.vector.tensor_scalar(stat[:, 0, :], stat[:, 0, :], 1.0 / C, None, ALU.mult))
                yield
                after()
                link(nc.vector.tensor_tensor(res[:], res[:], spread(stat[:, 0, :]), ALU.subtract))
                yield
                after()
                link(nc.vector.tensor_tensor(res_in[:], res[:], res[:], ALU.mult))
                yield
                after()
                link(nc.vector.tensor_reduce(stat[:, 1, :], res_in[:], AX.X, ALU.add))
                yield
                after()
                var, y, t = stat[:, 2, :], stat[:, 0, :], stat[:, 1, :]
                link(nc.vector.tensor_scalar(var, stat[:, 1, :], 1.0 / C, LN_EPS, ALU.mult, ALU.add))
                yield
                after()
                link(nc.vector.tensor_scalar(y.bitcast(I32), var.bitcast(I32), 1, None, ALU.logical_shift_right))
                yield
                after()
                link(nc.vector.tensor_scalar(y.bitcast(I32), y.bitcast(I32), -1, RSQRT_GUESS, ALU.mult, ALU.add))
                yield
                for _ in range(NEWTON):
                    after()
                    link(nc.vector.tensor_tensor(t, y, y, ALU.mult))
                    yield
                    after()
                    link(nc.vector.tensor_tensor(t, t, var, ALU.mult))
                    yield
                    after()
                    link(nc.vector.tensor_scalar(t, t, -0.5, 1.5, ALU.mult, ALU.add))
                    yield
                    after()
                    link(nc.vector.tensor_tensor(y, y, t, ALU.mult))
                    yield
                after()
                link(nc.vector.tensor_tensor(res[:], res[:], spread(y), ALU.mult))
                yield
                after()
                link(nc.vector.tensor_tensor(res_in[:], res[:], each(gamma), ALU.mult))
                yield
                after()
                assert done == LINKS
                nc.vector.tensor_tensor(res[:], res_in[:], each(beta), ALU.add).then_inc(out_ready, 1)
                yield

            with dve.Fori(0, 1) as z:
                for t in range(PREP):
                    add_values(0, t, z + t)
                    if t % 6 == 5:
                        dve.wait_ge(v_done, z + t // 6 + 1)
                        dve.sem_inc(side_free, 1)
                    if t >= LAG:
                        split(z, 0, t - LAG)
                for t in range(PREP - LAG, PREP):
                    split(z, 0, t)
                dve.wait_ge(proj_done, PJ)
                stage_max(z, z)
                nc.vector.tensor_copy(q_pick[0:DK], qs[0:DK, :, 0:CH]).then_inc(staged_pick, 1)
                for i in range(MX):
                    find_max(i, z)
                join_max(z)
                copy_rows(z, z + PREP)
                stage_pick(z + 1, z + 1)
                stage_exp(z, z)

            def image(b, last):
                for g in range(NG):
                    G = b * NG + g

                    def step(c, before, maxima, projections):
                        n = G * NC + c
                        m = n + 1
                        cross = isinstance(c, int) and c == 0
                        g_before = 1 - g if cross else g
                        if g or not (isinstance(c, int) and c == 0):
                            stage_exp(n, c)
                        if maxima:
                            if isinstance(c, int) and c == NC - 1:
                                dve.wait_ge(proj_done, (G + 2) * PJ)
                                stage_max(m, b * 0)
                            else:
                                stage_max(m, c + 1)
                        finish = norm(b * NC + before, side(b, last, g, c, "mix")) if before is not None and g_before else None
                        for k in range(EX):
                            if maxima:
                                for i in range(ahead(k - 1, g, c), ahead(k, g, c)):
                                    find_max(i, m * MX)
                                if k == K_ROWS - 3:
                                    join_max(m)
                                if k == K_ROWS:
                                    copy_rows(m, side(b, last, g, c, "rows"))
                            if before is not None:
                                if K_RECIP <= k < K_RECIP + UT:
                                    invert(k - K_RECIP, n - 1, side(b, last, g, c, "sum"))
                                if k == K_RECIP + UT:
                                    normalise_context(g_before, before, n - 1)
                                if finish and k >= K_NORM:
                                    next(finish, None)
                            if projections and k >= K_PREP:
                                t = k - K_PREP
                                if t < PREP:
                                    add_values(1 - g, t, side(b, last, g, c, t))
                                if t < PREP and t % 6 == 5:
                                    dve.wait_ge(v_done, (G + 1) * NC + t // 6 + 1)
                                    dve.sem_inc(side_free, 1)
                                if t >= LAG:
                                    split(G + 1, 1 - g, t - LAG)
                        if projections:
                            for t in range(EX - K_PREP - LAG, PREP):
                                split(G + 1, 1 - g, t)
                            dve.wait_ge(proj_done, (G + 2) * PJ)
                            stage_pick(m + 1, b * 0)
                        elif isinstance(c, int) and c == NC - 1 and maxima:
                            stage_pick(m + 1, b * 0 + 1)
                        elif not isinstance(c, int) or c == 0:
                            stage_pick(m + 1, c + 2)
                    chunks(dve, g, last, step)
                n = b * NG * NC + NG * NC - 1
                if not last:
                    stage_exp(n + 1, b * 0)
                for piece in range(UT):
                    invert(piece, n, side(b, last, "end", 0, "sum"))
                normalise_context(1, b * 0 + NC - 1, n)
                for _ in norm(b * NC + NC - 1, side(b, last, "end", 0, "mix")):
                    pass
            images(dve, image)


def two_layers(nc, a, out):
    h1 = nc.dram_tensor("h1_scratch", [B, H, W, C], F32, kind="Internal").ap()
    w1 = nc.dram_tensor("w1_scratch", [B, H, W, C], F32, kind="Internal").ap()
    y = nc.dram_tensor("y_scratch", [B, H, W, C], F32, kind="Internal").ap()
    rew = nc.dram_tensor("rew_scratch", [2 * B, H, C], F32, kind="Internal").ap()
    dist = nc.dram_tensor("dist_scratch", [DIAG, DIAG], F32, kind="Internal").ap()
    by_query = nc.dram_tensor("by_query_scratch", [KT, (DIAG - 1) * RP], F16, kind="Internal").ap()
    scr = {"h1": h1, "w1": w1, "y": y, "rew": rew, "dist": dist, "by_query": by_query}
    with ExitStack() as whole:
        keep = lambda c, n, s, d=F32: c.enter_context(nc.sbuf_tensor(n, s, d))
        w = {"ident": keep(whole, "ident_sb", [128, 128]), "flags": keep(whole, "flags_sb", [128, 4])}
        with ExitStack() as first:
            w["G"] = [keep(first, f"G{r}", [KT, NK, DIM]) for r in range(2)]
            w["dft_e"], w["dft_o"] = keep(first, "dft_e", [KR, NK, HALF]), keep(first, "dft_o", [KR, NK, HALF])
            w["chan_t"] = keep(first, "chan_t", [C, 3, C])
            w["par"], w["thr"] = keep(first, "par", [KT, 2, HALF]), keep(first, "thr", [KT, 2, HALF])
            w["Y"] = keep(first, "Y", [KT, NK, GROUPS * GP])
            prepare_layer0(nc, a, w)
            layer0(nc, a, w, scr)
        w["by_key"] = keep(whole, "by_key", [KT, WIN], F16)
        prepare_windows(nc, a, w, scr)
        layer1(nc, a, w, scr, out)


_INS = ["x", "L0_conv_mlp_h1_w", "L0_conv_mlp_w1_w", "L0_conv_mlp_c_w", "L0_conv_reweight_h_w", "L0_conv_reweight_w_w",
        "L0_conv_param_h", "L0_conv_param_w", "L1_conv_wq", "L1_conv_bq", "L1_conv_wk", "L1_conv_bk", "L1_conv_wv",
        "L1_conv_bv", "L1_conv_wo", "L1_conv_bo", "L1_conv_ln_gamma", "L1_conv_ln_beta", "L1_conv_spatial_bias"]


def kernel(**inputs):
    import numpy as _np
    import concourse.bacc as _bacc
    from concourse import mybir as _mybir
    from concourse.bass_utils import run_bass_kernel_spmd as _run

    nc = _bacc.Bacc("TRN2", target_bir_lowering=False, num_devices=1)
    arrays, args = {}, {}
    given = {n: _np.ascontiguousarray(inputs[n]) for n in _INS}
    given.update(constants())
    for name, a in given.items():
        arrays[f"in_{name}"] = a
        args[name] = nc.dram_tensor(f"in_{name}", a.shape, _mybir.dt.from_np(a.dtype), kind="ExternalInput").ap()
    out = nc.dram_tensor("out_0", (B, H, W, C), _mybir.dt.from_np(_np.dtype("float32")), kind="ExternalOutput").ap()
    two_layers(nc, args, out)
    r = _run(nc, [arrays], core_ids=[0])
    return r.results[0]["out_0"]
```
